# Optimizing a Trainium2 kernel written in Bass

```python
import numpy as np
import jax
import jax.numpy as jnp

def _softmax(x, axis=-1):
    return jax.nn.softmax(x, axis=axis)

def _gelu(x):
    return jax.nn.gelu(x, approximate=True)

def _silu(x):
    return jax.nn.silu(x)

def _sigmoid(x):
    return jax.nn.sigmoid(x)

def _layernorm(x, axis=-1, eps=1e-05):
    m = jnp.mean(x, axis=axis, keepdims=True)
    v = jnp.var(x, axis=axis, keepdims=True)
    return (x - m) / jnp.sqrt(v + eps)

def _scatter_add(tgt, idx, src, axis=0):
    return tgt.at[idx].add(src)

def _segment_sum(src, seg, n):
    return jax.ops.segment_sum(src, seg, n)
kernel_name = 'mk_macaron_d2_jaxref_r8_9049d6'

def setup_inputs(seed: int=0):
    np.random.seed(seed)
    _w = jnp.asarray

    def _L0_attn_setup():
        import jax, jax.numpy as jnp
        import numpy as np
        DIM = 256
        NUM_HEADS = 128
        TOP_K = 32
        D_HEAD_V = DIM // NUM_HEADS
        key = jax.random.key(seed)
        ks = jax.random.split(key, 5)
        s = 1.0 / np.sqrt(DIM)
        x = jax.random.normal(ks[0], (4, 512, DIM), dtype=jnp.float32)
        Wq = jax.random.uniform(ks[1], (NUM_HEADS, DIM), minval=-s, maxval=s, dtype=jnp.float32)
        Wk = jax.random.uniform(ks[2], (NUM_HEADS, DIM), minval=-s, maxval=s, dtype=jnp.float32)
        Wv = jax.random.uniform(ks[3], (DIM, DIM), minval=-s, maxval=s, dtype=jnp.float32)
        Wo = jax.random.uniform(ks[4], (DIM, DIM), minval=-s, maxval=s, dtype=jnp.float32)
        return {'x': x, 'Wq': Wq, 'Wk': Wk, 'Wv': Wv, 'Wo': Wo}
    _L0_attn_in = _L0_attn_setup()

    def _L0_ffn_setup():
        import jax, jax.numpy as jnp
        import numpy as np
        HIDDEN = 256
        INTER = 688
        LUT_SIZE = 16

        def _ghost_linear(x, idx, lut):
            w = lut[idx]
            return jnp.einsum('bsh,oh->bso', x, w)
        key = jax.random.key(seed)
        k_x, k_lut, k_g, k_u, k_d = jax.random.split(key, 5)
        x = jax.random.normal(k_x, (2, 512, HIDDEN), dtype=jnp.float32)
        lut = jax.random.normal(k_lut, (LUT_SIZE,), dtype=jnp.float32) * 0.02
        gate_idx = jax.random.randint(k_g, (INTER, HIDDEN), 0, LUT_SIZE, dtype=jnp.int32)
        up_idx = jax.random.randint(k_u, (INTER, HIDDEN), 0, LUT_SIZE, dtype=jnp.int32)
        down_idx = jax.random.randint(k_d, (HIDDEN, INTER), 0, LUT_SIZE, dtype=jnp.int32)
        return {'x': x, 'lut': lut, 'gate_idx': gate_idx, 'up_idx': up_idx, 'down_idx': down_idx}
    _L0_ffn_in = _L0_ffn_setup()

    def _L1_attn_setup():
        import jax, jax.numpy as jnp
        import numpy as np
        D_MODEL = 256
        EXPAND = 2
        D_STATE = 128
        D_CONV = 4
        HEADDIM = D_MODEL // 32
        D_INNER = EXPAND * D_MODEL
        NHEADS = D_INNER // HEADDIM
        CONV_DIM = D_INNER + 2 * D_STATE
        D_IN_PROJ = 2 * D_INNER + 2 * D_STATE + NHEADS
        CHUNK = 32
        BATCH, SEQLEN = (1, 512)
        EPS = 1e-05

        def silu(x):
            return x * jax.nn.sigmoid(x)

        def _causal_decay(dA):
            cs = jnp.cumsum(dA, axis=-1)
            d = cs[..., :, None] - cs[..., None, :]
            c = dA.shape[-1]
            mask = jnp.tril(jnp.ones((c, c), bool))
            return jnp.where(mask, jnp.exp(jnp.where(mask, d, 0.0)), 0.0)

        def _chunked_scan(x, dt, A, B, C):
            b, l, h, p = x.shape
            n = B.shape[-1]
            nc = l // CHUNK
            xc = x.reshape(b, nc, CHUNK, h, p)
            dtc = dt.reshape(b, nc, CHUNK, h)
            Bc = B.reshape(b, nc, CHUNK, n)
            Cc = C.reshape(b, nc, CHUNK, n)
            dA = dtc * A
            dA_cum = jnp.cumsum(dA, axis=2)
            L = _causal_decay(jnp.moveaxis(dA, 2, 3))
            Xdt = xc * dtc[..., None]
            Y_diag = jnp.einsum('bzcn,bzsn,bzhcs,bzshp->bzchp', Cc, Bc, L, Xdt)
            decay_states = jnp.exp(dA_cum[:, :, -1:, :] - dA_cum)
            states = jnp.einsum('bzcn,bzch,bzchp->bzhpn', Bc, decay_states, Xdt)
            chunk_decay = jnp.exp(dA_cum[:, :, -1, :])

            def step(hprev, inp):
                st, dec = inp
                return (hprev * dec[:, :, None, None] + st, hprev)
            init = jnp.zeros((b, h, p, n), x.dtype)
            _, prev = jax.lax.scan(step, init, (jnp.moveaxis(states, 1, 0), jnp.moveaxis(chunk_decay, 1, 0)))
            prev = jnp.moveaxis(prev, 0, 1)
            Y_off = jnp.einsum('bzcn,bzhpn,bzch->bzchp', Cc, prev, jnp.exp(dA_cum))
            return (Y_diag + Y_off).reshape(b, l, h, p)
        key = jax.random.key(seed)
        ks = jax.random.split(key, 8)
        s = 0.02
        u = jax.random.normal(ks[0], (BATCH, SEQLEN, D_MODEL), jnp.float32)
        in_proj_w = jax.random.normal(ks[1], (D_IN_PROJ, D_MODEL), jnp.float32) * s
        conv_w = jax.random.normal(ks[2], (CONV_DIM, D_CONV), jnp.float32) * 0.2
        conv_b = jax.random.normal(ks[3], (CONV_DIM,), jnp.float32) * 0.02
        dt = jnp.exp(jax.random.uniform(ks[4], (NHEADS,)) * (np.log(0.1) - np.log(0.001)) + np.log(0.001))
        dt_bias = dt + jnp.log(-jnp.expm1(-dt))
        A_log = jnp.log(jax.random.uniform(ks[5], (NHEADS,), minval=1.0, maxval=16.0))
        D = jnp.ones((NHEADS,), jnp.float32)
        norm_weight = jnp.ones((D_INNER,), jnp.float32)
        out_proj_w = jax.random.normal(ks[6], (D_MODEL, D_INNER), jnp.float32) * s
        return dict(u=u, in_proj_w=in_proj_w, conv_w=conv_w, conv_b=conv_b, dt_bias=dt_bias, A_log=A_log, D=D, norm_weight=norm_weight, out_proj_w=out_proj_w)
    _L1_attn_in = _L1_attn_setup()

    def _L1_ffn_setup():
        import jax, jax.numpy as jnp
        import numpy as np
        HIDDEN = 256
        INTER = 1024
        SCALE = 64.0

        def fwht(x):
            orig_shape = x.shape
            n = orig_shape[-1]
            x = x.reshape(-1, n)
            h = 1
            while h < n:
                x = x.reshape(-1, n // (2 * h), 2, h)
                a, b = (x[:, :, 0, :], x[:, :, 1, :])
                x = jnp.stack([a + b, a - b], axis=2).reshape(-1, n)
                h *= 2
            return (x / jnp.sqrt(jnp.asarray(n, x.dtype))).reshape(orig_shape)
        key = jax.random.key(seed)
        ks = jax.random.split(key, 8)
        inp = jax.random.normal(ks[0], (4, 256, HIDDEN), dtype=jnp.float32)
        SU_ug = jnp.where(jax.random.bernoulli(ks[1], 0.5, (HIDDEN,)), 1.0, -1.0).astype(jnp.float32)
        SU_dp = jnp.where(jax.random.bernoulli(ks[2], 0.5, (INTER,)), 1.0, -1.0).astype(jnp.float32)
        Wscale_ug = jax.random.uniform(ks[3], (2 * INTER,), jnp.float32, 0.5, 1.5)
        Wscale_dp = jax.random.uniform(ks[4], (HIDDEN,), jnp.float32, 0.5, 1.5)
        W_up = jax.random.normal(ks[5], (INTER, HIDDEN), dtype=jnp.float32) * 0.02
        W_gate = jax.random.normal(ks[6], (INTER, HIDDEN), dtype=jnp.float32) * 0.02
        W_down = jax.random.normal(ks[7], (HIDDEN, INTER), dtype=jnp.float32) * 0.02
        return {'input': inp, 'SU_ug': SU_ug, 'SU_dp': SU_dp, 'Wscale_ug': Wscale_ug, 'Wscale_dp': Wscale_dp, 'W_up': W_up, 'W_gate': W_gate, 'W_down': W_down}
    _L1_ffn_in = _L1_ffn_setup()
    _d = {'L0_attn_x': _L0_attn_in['x'], 'L0_attn_Wq': _L0_attn_in['Wq'], 'L0_attn_Wk': _L0_attn_in['Wk'], 'L0_attn_Wv': _L0_attn_in['Wv'], 'L0_attn_Wo': _L0_attn_in['Wo'], 'L0_ffn_lut': _L0_ffn_in['lut'], 'L0_ffn_gate_idx': _L0_ffn_in['gate_idx'], 'L0_ffn_up_idx': _L0_ffn_in['up_idx'], 'L0_ffn_down_idx': _L0_ffn_in['down_idx'], 'L1_attn_in_proj_w': _L1_attn_in['in_proj_w'], 'L1_attn_conv_w': _L1_attn_in['conv_w'], 'L1_attn_conv_b': _L1_attn_in['conv_b'], 'L1_attn_dt_bias': _L1_attn_in['dt_bias'], 'L1_attn_A_log': _L1_attn_in['A_log'], 'L1_attn_D': _L1_attn_in['D'], 'L1_attn_norm_weight': _L1_attn_in['norm_weight'], 'L1_attn_out_proj_w': _L1_attn_in['out_proj_w'], 'L1_ffn_SU_ug': _L1_ffn_in['SU_ug'], 'L1_ffn_SU_dp': _L1_ffn_in['SU_dp'], 'L1_ffn_Wscale_ug': _L1_ffn_in['Wscale_ug'], 'L1_ffn_Wscale_dp': _L1_ffn_in['Wscale_dp'], 'L1_ffn_W_up': _L1_ffn_in['W_up'], 'L1_ffn_W_gate': _L1_ffn_in['W_gate'], 'L1_ffn_W_down': _L1_ffn_in['W_down']}
    _x0 = _d['L0_attn_x']
    _d['L0_attn_x'] = jax.random.normal(jax.random.fold_in(jax.random.key(seed), 1), (2, 512, 256), dtype=_x0.dtype)
    del _x0
    return _d

def reference(L0_attn_x, L0_attn_Wq, L0_attn_Wk, L0_attn_Wv, L0_attn_Wo, L0_ffn_lut, L0_ffn_gate_idx, L0_ffn_up_idx, L0_ffn_down_idx, L1_attn_in_proj_w, L1_attn_conv_w, L1_attn_conv_b, L1_attn_dt_bias, L1_attn_A_log, L1_attn_D, L1_attn_norm_weight, L1_attn_out_proj_w, L1_ffn_SU_ug, L1_ffn_SU_dp, L1_ffn_Wscale_ug, L1_ffn_Wscale_dp, L1_ffn_W_up, L1_ffn_W_gate, L1_ffn_W_down):

    def _L0_attn_ref(x, Wq, Wk, Wv, Wo):
        import jax, jax.numpy as jnp
        import numpy as np
        DIM = 256
        NUM_HEADS = 128
        TOP_K = 32
        D_HEAD_V = DIM // NUM_HEADS
        B, S, _ = x.shape
        H, dv, k = (NUM_HEADS, D_HEAD_V, TOP_K)
        q = jnp.einsum('bsd,hd->bhs', x, Wq)
        keys = jnp.einsum('bsd,hd->bhs', x, Wk)
        v = jnp.einsum('bsd,ed->bse', x, Wv).reshape(B, S, H, dv).transpose(0, 2, 1, 3)
        k_idx = jnp.argsort(keys, axis=-1)
        k_sorted = jnp.take_along_axis(keys, k_idx, axis=-1)
        v_sorted = jnp.take_along_axis(v, k_idx[..., None], axis=2)
        top_keys = k_sorted[:, :, -k:]
        bot_keys = k_sorted[:, :, :k]
        top_vals = v_sorted[:, :, -k:, :]
        bot_vals = v_sorted[:, :, :k, :]
        attn_top = jax.nn.softmax(q[..., None] * top_keys[:, :, None, :], axis=-1)
        attn_bot = jax.nn.softmax(q[..., None] * bot_keys[:, :, None, :], axis=-1)
        out_top = jnp.einsum('bhsk,bhkd->bhsd', attn_top, top_vals)
        out_bot = jnp.einsum('bhsk,bhkd->bhsd', attn_bot, bot_vals)
        q_pos = (q > 0).astype(x.dtype)[..., None]
        out = q_pos * out_top + (1.0 - q_pos) * out_bot
        out = out.transpose(0, 2, 1, 3).reshape(B, S, H * dv)
        return jnp.einsum('bsd,ed->bse', out, Wo)

    def _L0_ffn_ref(x, lut, gate_idx, up_idx, down_idx):
        import jax, jax.numpy as jnp
        import numpy as np
        HIDDEN = 256
        INTER = 688
        LUT_SIZE = 16

        def _ghost_linear(x, idx, lut):
            w = lut[idx]
            return jnp.einsum('bsh,oh->bso', x, w)
        gate = _ghost_linear(x, gate_idx, lut)
        up = _ghost_linear(x, up_idx, lut)
        h = jax.nn.silu(gate) * up
        return _ghost_linear(h, down_idx, lut)

    def _L1_attn_ref(u, in_proj_w, conv_w, conv_b, dt_bias, A_log, D, norm_weight, out_proj_w):
        import jax, jax.numpy as jnp
        import numpy as np
        D_MODEL = 256
        EXPAND = 2
        D_STATE = 128
        D_CONV = 4
        HEADDIM = D_MODEL // 32
        D_INNER = EXPAND * D_MODEL
        NHEADS = D_INNER // HEADDIM
        CONV_DIM = D_INNER + 2 * D_STATE
        D_IN_PROJ = 2 * D_INNER + 2 * D_STATE + NHEADS
        CHUNK = 32
        BATCH, SEQLEN = (1, 512)
        EPS = 1e-05

        def silu(x):
            return x * jax.nn.sigmoid(x)

        def _causal_decay(dA):
            cs = jnp.cumsum(dA, axis=-1)
            d = cs[..., :, None] - cs[..., None, :]
            c = dA.shape[-1]
            mask = jnp.tril(jnp.ones((c, c), bool))
            return jnp.where(mask, jnp.exp(jnp.where(mask, d, 0.0)), 0.0)

        def _chunked_scan(x, dt, A, B, C):
            b, l, h, p = x.shape
            n = B.shape[-1]
            nc = l // CHUNK
            xc = x.reshape(b, nc, CHUNK, h, p)
            dtc = dt.reshape(b, nc, CHUNK, h)
            Bc = B.reshape(b, nc, CHUNK, n)
            Cc = C.reshape(b, nc, CHUNK, n)
            dA = dtc * A
            dA_cum = jnp.cumsum(dA, axis=2)
            L = _causal_decay(jnp.moveaxis(dA, 2, 3))
            Xdt = xc * dtc[..., None]
            Y_diag = jnp.einsum('bzcn,bzsn,bzhcs,bzshp->bzchp', Cc, Bc, L, Xdt)
            decay_states = jnp.exp(dA_cum[:, :, -1:, :] - dA_cum)
            states = jnp.einsum('bzcn,bzch,bzchp->bzhpn', Bc, decay_states, Xdt)
            chunk_decay = jnp.exp(dA_cum[:, :, -1, :])

            def step(hprev, inp):
                st, dec = inp
                return (hprev * dec[:, :, None, None] + st, hprev)
            init = jnp.zeros((b, h, p, n), x.dtype)
            _, prev = jax.lax.scan(step, init, (jnp.moveaxis(states, 1, 0), jnp.moveaxis(chunk_decay, 1, 0)))
            prev = jnp.moveaxis(prev, 0, 1)
            Y_off = jnp.einsum('bzcn,bzhpn,bzch->bzchp', Cc, prev, jnp.exp(dA_cum))
            return (Y_diag + Y_off).reshape(b, l, h, p)
        b, l, _ = u.shape
        zxbcdt = u @ in_proj_w.T
        z, xBC, dt_raw = jnp.split(zxbcdt, [D_INNER, D_INNER + CONV_DIM], axis=-1)
        xt = jnp.transpose(xBC, (0, 2, 1))
        conv = jax.lax.conv_general_dilated(xt, conv_w[:, None, :], (1,), [(D_CONV - 1, 0)], dimension_numbers=('NCH', 'OIH', 'NCH'), feature_group_count=CONV_DIM)
        xBC = silu(jnp.transpose(conv + conv_b[None, :, None], (0, 2, 1)))
        x, B, C = jnp.split(xBC, [D_INNER, D_INNER + D_STATE], axis=-1)
        dt = jax.nn.softplus(dt_raw + dt_bias)
        A = -jnp.exp(A_log)
        xh = x.reshape(b, l, NHEADS, HEADDIM)
        y = _chunked_scan(xh, dt, A, B, C)
        y = y + xh * D[:, None]
        y = y.reshape(b, l, D_INNER)
        yg = y * silu(z)
        yn = yg * jax.lax.rsqrt(jnp.mean(yg * yg, axis=-1, keepdims=True) + EPS) * norm_weight
        return yn @ out_proj_w.T

    def _L1_ffn_ref(input, SU_ug, SU_dp, Wscale_ug, Wscale_dp, W_up, W_gate, W_down):
        import jax, jax.numpy as jnp
        import numpy as np
        HIDDEN = 256
        INTER = 1024
        SCALE = 64.0

        def fwht(x):
            orig_shape = x.shape
            n = orig_shape[-1]
            x = x.reshape(-1, n)
            h = 1
            while h < n:
                x = x.reshape(-1, n // (2 * h), 2, h)
                a, b = (x[:, :, 0, :], x[:, :, 1, :])
                x = jnp.stack([a + b, a - b], axis=2).reshape(-1, n)
                h *= 2
            return (x / jnp.sqrt(jnp.asarray(n, x.dtype))).reshape(orig_shape)
        n = SU_ug.shape[0]
        x = input.reshape(-1, n)
        x = fwht(x * SU_ug) / SCALE
        x_up = x @ W_up.T * (Wscale_ug[:INTER] * SCALE)
        x_gate = x @ W_gate.T * (Wscale_ug[INTER:] * SCALE)
        x = jax.nn.silu(x_gate) * x_up
        x = fwht(x * SU_dp) / SCALE
        x = x @ W_down.T * (Wscale_dp * SCALE)
        return x.reshape(input.shape)
    x = L0_attn_x
    x = x + 0.5 * _L0_ffn_ref(_layernorm(x, axis=-1), L0_ffn_lut, L0_ffn_gate_idx, L0_ffn_up_idx, L0_ffn_down_idx)
    x = x + _L0_attn_ref(_layernorm(x, axis=-1), L0_attn_Wq, L0_attn_Wk, L0_attn_Wv, L0_attn_Wo)
    x = x + 0.5 * _L0_ffn_ref(_layernorm(x, axis=-1), L0_ffn_lut, L0_ffn_gate_idx, L0_ffn_up_idx, L0_ffn_down_idx)
    x = x + 0.5 * _L1_ffn_ref(_layernorm(x, axis=-1), L1_ffn_SU_ug, L1_ffn_SU_dp, L1_ffn_Wscale_ug, L1_ffn_Wscale_dp, L1_ffn_W_up, L1_ffn_W_gate, L1_ffn_W_down)
    x = x + _L1_attn_ref(_layernorm(x, axis=-1), L1_attn_in_proj_w, L1_attn_conv_w, L1_attn_conv_b, L1_attn_dt_bias, L1_attn_A_log, L1_attn_D, L1_attn_norm_weight, L1_attn_out_proj_w)
    x = x + 0.5 * _L1_ffn_ref(_layernorm(x, axis=-1), L1_ffn_SU_ug, L1_ffn_SU_dp, L1_ffn_Wscale_ug, L1_ffn_Wscale_dp, L1_ffn_W_up, L1_ffn_W_gate, L1_ffn_W_down)
    return x

_drawn_inputs = setup_inputs


def setup_inputs(seed=0):
    import zlib

    import numpy as np

    out = dict(_drawn_inputs(seed))
    spreads = {'L1_attn_D': (1.0, 0.2), 'L1_attn_norm_weight': (1.0, 0.2)}
    factors = {'L1_attn_dt_bias': 8.0,
     'L1_attn_A_log': 8.0,
     'L1_ffn_Wscale_ug': 4.351,
     'L1_ffn_Wscale_dp': 6.028}
    for name, (base, spread) in spreads.items():
        noise = np.random.default_rng([zlib.crc32(name.encode()), seed]).standard_normal(out[name].shape)
        drawn = base * np.exp(spread * noise) if base else spread * noise
        out[name] = jnp.asarray(drawn.astype(out[name].dtype))
    for name, factor in factors.items():
        out[name] = (out[name] * factor).astype(out[name].dtype)
    return out
```

```python
import concourse.bass as bass
from concourse import mybir
from contextlib import ExitStack
import numpy as np

B = 2
S = 512
D = 256
P = 128
T = S // P
KD = D // P
INTER0 = 688
M0 = -(-INTER0 // P)
LAST0 = INTER0 - (M0 - 1) * P
LUT = 16
INTER1 = 1024
M1 = INTER1 // P
HEADS = 128
TOPK = 32
SETS = 2
GR = 16
G32 = 32
DI = 512
NH = 64
HP = DI // NH
CONVC = 768
CT = CONVC // P
DCONV = 4
LEVELS = 7
NCUM = LEVELS + 3
EPS = 1e-5
LOWEST = -3.0e38
NPHASE = 12

PHASES = [(kind, b) for kind in ("F0", "A", "F0", "F1", "M", "F1") for b in range(B)]
TILES_OF = {"F0": M0, "F1": M1, "A": 0, "M": 0}
UNITS = [(p, m) for p, (kind, _) in enumerate(PHASES) for m in range(TILES_OF[kind])]
UNIT0 = [sum(TILES_OF[k] for k, _ in PHASES[:p]) for p in range(NPHASE)]


def constants():
    ident = np.eye(P, dtype=np.float32)
    had = np.array([[1.0]], np.float32)
    while had.shape[0] < P:
        had = np.block([[had, had], [had, -had]]).astype(np.float32)
    t = np.arange(P)
    cum = np.zeros((NCUM, P, P), np.float32)
    pair = np.zeros((LEVELS, P, P), np.float32)
    r, c = np.meshgrid(t, t, indexing="ij")
    for lv in range(LEVELS):
        half = 1 << lv
        mid = (c // (2 * half)) * 2 * half + half
        right = c >= mid
        cum[lv] = np.where(right, (r >= mid) & (r <= c), (r > c) & (r < mid))
        pair[lv] = (r // (2 * half) == c // (2 * half)) & right & (r < mid)
    cum[LEVELS] = r <= c
    cum[LEVELS + 1] = r > c
    cum[LEVELS + 2] = 1.0
    rows = t
    q, g = (rows // 32) % 2, rows % 32
    slot = np.zeros((P, GR, 4), np.float32)
    slot[rows, g // 2, 2 * q + g % 2] = 1.0
    iota32 = np.broadcast_to(np.arange(32, dtype=np.float32), (P, 32))
    return np.concatenate([
        ident, had, -had,
        cum.transpose(1, 0, 2).reshape(P, -1),
        pair.transpose(1, 0, 2).reshape(P, -1),
        slot.reshape(P, -1), iota32,
    ], axis=1).astype(np.float32)


C_ID, C_H, C_NH = 0, P, 2 * P
C_CUM = 3 * P
C_PAIR = C_CUM + NCUM * P
C_SLOT = C_PAIR + LEVELS * P
C_IOTA = C_SLOT + GR * 4
C_ALL = C_IOTA + 32


def psum_uses():
    uses, count = {}, [0] * 8

    def use(bank, *name):
        count[bank] += 1
        uses[name] = (bank, count[bank])

    def front(p):
        for k in range(KD):
            use(6 + k, "xT", p, k)

    for i in range(8):
        use(i % 4, "foldug", i)
    for i in range(4):
        use(4 + i % 2, "folddn", i)
    front(0)
    for p, (kind, b) in enumerate(PHASES):
        if kind in ("F0", "F1"):
            for m in range(TILES_OF[kind]):
                ring = 2 * ((UNIT0[p] + m) % 2)
                use(ring, "gate", p, m)
                use(ring + 1, "up", p, m)
        if kind == "A" and b == 0:
            for bb in range(B):
                if bb == 1:
                    front(p + 1)
                for i, n in enumerate(("q0", "q1", "k0", "k1", "v00", "v01", "v10", "v11")):
                    use(i % 4, n, bb)
                use(bb, "qt", bb)
        if kind == "A":
            for s in range(SETS):
                for i in range(2):
                    use(4 + i, "gat", b, s, i)
                for t in range(T):
                    use(t, "O", b, s, t)
                for g in range(GR):
                    use(4 + g % 2, "arg", b, s, g)
            for k in range(2):
                use(k, "oT", b, k)
        if kind == "M":
            n = 0
            for c in range(CT):
                use(n % 4, "conv", b, c)
                n += 1
            use(n % 4, "dt", b)
            n += 1
            for t in range(T):
                use(n % 4, "z", b, t)
                n += 1
            use(4, "G", b)
            use(5, "BT", b)
            for t in range(T):
                use(n % 4, "XT", b, t)
                n += 1
            for i in range(NCUM // 2):
                use(n % 4, "cum", b, i)
                n += 1
            for t in range(T):
                for lv in range(LEVELS):
                    use(n % 4, "lev", b, t, lv)
                    n += 1
                if t:
                    use(n % 4, "off", b, t)
                    n += 1
                if t < T - 1:
                    use(n % 4, "st", b, t)
                    n += 1
            for t in range(T):
                use(n % 4, "yT", b, t)
                n += 1
        if p + 1 < NPHASE and not (kind == "A" and b == 0):
            front(p + 1)
        for j in range(2):
            use(4 + j, "tail", p, j)
    return uses


def program(nc, x, cst, gate_idx, up_idx, down_idx, lut, w_ug, w_dn, su_ug, su_dp, ws_ug, ws_dp,
            w_qkv, w_qt, w_o, w_in, conv_w, conv_b, dt_bias, a_log, skip_d, norm_w, w_out, out,
            phases_run=NPHASE):
    f32, i32, u32 = mybir.dt.float32, mybir.dt.int32, mybir.dt.uint32
    ALU, ACT = mybir.AluOpType, mybir.ActivationFunctionType
    AX = mybir.AxisListType
    USES = psum_uses()
    ctx = ExitStack()
    with ctx:
        def sb(name, shape, dt=f32):
            return ctx.enter_context(nc.sbuf_tensor(name, shape, dt))

        def sem(name):
            return ctx.enter_context(nc.semaphore(name))

        bank = [ctx.enter_context(nc.psum_tensor(f"bank{i}", [P, 512], f32)) for i in range(8)]

        CST = sb("CST", [P, C_ALL])
        IDENT = CST[:, C_ID:C_ID + P]
        HAD, NHAD = CST[:, C_H:C_H + P], CST[:, C_NH:C_NH + P]
        SLOT = CST[:, C_SLOT:C_SLOT + GR * 4]
        IOTA = CST[:, C_IOTA:C_IOTA + 32]
        X = sb("X", [P, B * T, D])
        XH = sb("XH", [P, T, D])
        XT = [sb(f"XT{b}", [P, KD, S]) for b in range(B)]
        STAT = sb("STAT", [P, T, 6])
        MV = sb("MV", [P, T, 2])
        VEPS = sb("VEPS", [P, T])
        RSTD = sb("RSTD", [P, T])
        NHALF = sb("NHALF", [P, T])
        WGATE = sb("WGATE", [P, KD, INTER0])
        WUP = sb("WUP", [P, KD, INTER0])
        WDOWN = sb("WDOWN", [P, M0, D])
        WUG = sb("WUG", [P, KD, 2 * INTER1])
        WDN = sb("WDN", [P, M1, D])
        HT = [sb(f"HT{b}", [P, M1, S]) for b in range(B)]
        SG = [sb(f"SG{i}", [P, S]) for i in range(2)]
        WSUG = sb("WSUG", [P, 2 * M1])
        WSUG16 = sb("WSUG16", [P, 2 * M1])
        SUUG = sb("SUUG", [P, KD])
        SUDP = sb("SUDP", [P, M1])
        WO = sb("WO", [P, 2, D])
        WOUT = sb("WOUT", [P, 4, D])
        NW = sb("NW", [P, 4])
        CW = sb("CW", [P, CT, DCONV])
        CB = sb("CB", [P, CT])
        DTB = sb("DTB", [P, NH])
        NEGA = sb("NEGA", [P, NH])
        SKIP = sb("SKIP", [P, NH])

        USIZE = 23600
        U = sb("U", [P, USIZE])
        cur = [0]

        def part(n):
            cur[0] += n
            assert cur[0] <= USIZE, cur[0]
            return U[:, cur[0] - n:cur[0]]

        def ht(b, at, n):
            return HT[b][:, :, :].rearrange("p a b -> p (a b)")[:, at:at + n]

        NIDX = 2 * KD * INTER0 + M0 * D
        CH = M0 * D
        LUTB = sb("LUTB", [P, LUT])
        LUTX = sb("LUTX", [P, LUT // 2])
        cur[0] = 0
        IDX = part(NIDX)
        MASK = [part(CH) for _ in range(4)]
        SEL = [part(CH) for _ in range(8)]
        WUGRAW = [HT[k][:, :, :].rearrange("p a b -> p (a b)")[:, 0:2 * INTER1] for k in range(KD)]
        WDNRAW = [HT[k][:, :, :].rearrange("p a b -> p (a b)")[:, 2 * INTER1:2 * INTER1 + 4 * D] for k in range(2)]
        WSDP = sb("WSDP", [P, D])

        cur[0] = 0
        WQKV = part(KD * 8 * P).rearrange("p (k n) -> p k n", k=KD)
        WQT = part(KD * P).rearrange("p (k n) -> p k n", k=KD)
        QS = [[part(S) for _ in range(SETS)] for _ in range(B)]
        KEYS = [[part(S) for _ in range(SETS)] for _ in range(B)]
        V = [[[part(S) for _ in range(2)] for _ in range(SETS)] for _ in range(B)]
        QM = [part(S) for _ in range(B)]
        TOP = part(TOPK)
        IDX8 = part(TOPK)
        IA, IB = part(TOPK), part(TOPK)
        IAF, IBF = part(TOPK), part(TOPK)
        IAT, IBT = part(TOPK), part(TOPK)
        VB = ht(1, 0, 2 * S)
        OHC = part(G32 * 32)
        OHA = ht(1, 7 * S, G32 * 16)
        OHB = part(G32 * 4 * 32)
        PR = part(G32 * 2 * 16)
        VS = part(G32 * 2)
        AW = [part(GR * P) for _ in range(2)]
        VM = [part(GR * 4 * 5) for _ in range(2)]
        E = [ht(1, (4 + i) * S, S) for i in range(3)]
        OS = ht(0, 0, T * 2 * GR * 20)
        OH = ht(0, T * 2 * GR * 20, T * D)
        RD, R1 = ht(0, 7 * S, P), ht(0, 7 * S + P, P)
        OT = ht(1, 2 * S, 2 * S)
        OTMP = ht(0, 7 * S + 2 * P, D)

        cur[0] = 0
        WIN = part(KD * 1344).rearrange("p (k n) -> p k n", k=KD)
        XC = part(CT * S).rearrange("p (c s) -> p c s", c=CT)
        ZS = ht(1, 4 * S, T * DI).rearrange("p (t n) -> p t n", t=T)
        XTOK = part(T * DI).rearrange("p (t n) -> p t n", t=T)
        XDT = ht(0, 4 * S, T * DI).rearrange("p (t n) -> p t n", t=T)
        BT = part(T * P)
        GM = part(T * LEVELS * P)
        F = part(NCUM * T * NH)
        DTV, DTA, DTU, DTP, DTQ = (part(T * NH) for _ in range(5))
        GCC = part(T)
        GPR = part(T * P)
        W = [part(DI) for _ in range(3)]
        Y = part(DI)
        RF = [part(DI) for _ in range(2)]
        ST = [part(DI) for _ in range(2)]
        YT = SG
        SS = part(T)
        SSM = part(T)
        RR = part(T)
        SQ = part(DI)
        COEF = part(NH)

        bank_full = [sem(f"bank_full{i}") for i in range(8)]
        bank_free = [sem(f"bank_free{i}") for i in range(8)]
        x_in = sem("x_in")
        cst_in = sem("cst_in")
        idx_in = sem("idx_in")
        idx_zero = sem("idx_zero")
        wug_in = sem("wug_in")
        wdn_in = sem("wdn_in")
        small_in = sem("small_in")
        attn_w_in = sem("attn_w_in")
        win_in = sem("win_in")
        out_done = sem("out_done")
        dve_step = sem("dve_step")
        pool_step = sem("pool_step")
        act_step = sem("act_step")
        ghost_w = sem("ghost_w")
        butter = sem("butter")
        fold_scaled = sem("fold_scaled")
        var_ready = sem("var_ready")
        rstd_ready = sem("rstd_ready")
        xhat_ready = sem("xhat_ready")
        xT_ready = sem("xT_ready")
        small_ready = sem("small_ready")
        nega_ready = sem("nega_ready")
        proj_ready = sem("proj_ready")
        oh_zero = sem("oh_zero")
        onehot_ready = sem("onehot_ready")
        aw_ready = sem("aw_ready")
        e_ready = sem("e_ready")
        e_used = sem("e_used")
        set_used = sem("set_used")
        os_ready = sem("os_ready")
        oh_ready = sem("oh_ready")
        oT_ready = sem("oT_ready")
        conv_ready = sem("conv_ready")
        xc_ready = sem("xc_ready")
        zs_ready = sem("zs_ready")
        dtabs_ready = sem("dtabs_ready")
        dtexp_ready = sem("dtexp_ready")
        da_ready = sem("da_ready")
        bt_ready = sem("bt_ready")
        xtok_ready = sem("xtok_ready")
        xdt_ready = sem("xdt_ready")
        gm_ready = sem("gm_ready")
        w_ready = sem("w_ready")
        rf_ready = sem("rf_ready")
        y_step = sem("y_step")
        state_ready = sem("state_ready")
        yg_ready = sem("yg_ready")
        ss_ready = sem("ss_ready")
        rr_ready = sem("rr_ready")
        yT_ready = sem("yT_ready")
        block = ctx.enter_context(nc.Block())

        def full(eng, *name):
            i, n = USES[name]
            eng.wait_ge(bank_full[i], n)
            return bank[i]

        def emptied(*name):
            return bank_free[USES[name][0]]

        def copied(eng, *name):
            i, n = USES[name]
            eng.wait_ge(bank_free[i], n)

        LAST = phases_run

        @block.sync
        def _(sp):
            sp.dma_start(CST[:, :], cst).then_inc(cst_in, 16)
            sp.dma_start(LUTB[:, :], lut).then_inc(idx_in, 16)
            sp.wait_ge(idx_zero, 1)
            sp.dma_start(IDX[:, 0:KD * INTER0].bitcast(i32), gate_idx).then_inc(idx_in, 16)
            sp.dma_start(IDX[:, KD * INTER0:2 * KD * INTER0].bitcast(i32), up_idx).then_inc(idx_in, 16)
            dn = IDX[:, 2 * KD * INTER0:NIDX].bitcast(i32)
            sp.dma_start(dn[:, 0:(M0 - 1) * D].rearrange("p (m n) -> p m n", n=D),
                         down_idx[0:(M0 - 1) * P, :].rearrange("(m p) n -> p m n", p=P)).then_inc(idx_in, 16)
            sp.dma_start(dn[0:LAST0, (M0 - 1) * D:M0 * D], down_idx[(M0 - 1) * P:INTER0, :]).then_inc(idx_in, 16)
            sp.dma_start(X[:, :, :], x.rearrange("(t p) d -> p t d", p=P)).then_inc(x_in, 16)
            sp.wait_ge(ghost_w, 3)
            sp.dma_start(WQKV, w_qkv).then_inc(attn_w_in, 16)
            sp.dma_start(WQT, w_qt).then_inc(attn_w_in, 16)
            if LAST > 8:
                copied(sp, "tail", 3, 1)
                sp.dma_start(WIN, w_in).then_inc(win_in, 16)
            for p in range(LAST - B, LAST):
                for j in range(2):
                    copied(sp, "tail", p, j)
            sp.dma_start(out.rearrange("(t p) d -> p t d", p=P), X[:, :, :]).then_inc(out_done, 16)
            sp.wait_ge(out_done, 16)

        WLIST = [(b, t, lv) for b in range(B) for t in range(T) for lv in range(LEVELS + (t < T - 1))]

        def wcount(b, t, lv):
            return WLIST.index((b, t, lv))

        def wname(n):
            b, t, lv = WLIST[n]
            return ("lev", b, t, lv) if lv < LEVELS else ("st", b, t)

        @block.gpsimd
        def _(pool):
            pool.memset(IDX[:, 2 * KD * INTER0 + (M0 - 1) * D:NIDX], 0.0).then_inc(idx_zero, 1)
            pool.memset(NHALF[:, :], -0.5).then_inc(pool_step, 1)
            steps = [1]

            def link(ins):
                steps[0] += 1
                ins.then_inc(pool_step, 1)
                pool.wait_ge(pool_step, steps[0])

            pool.wait_ge(small_in, 16 * 11)
            nc.gpsimd.tensor_scalar(WSUG16[:, :], WSUG[:, :], 1.0 / 16.0, None, ALU.mult).then_inc(small_ready, 1)
            for k in range(4):
                last = nc.gpsimd.tensor_scalar(WOUT[:, k, :], WOUT[:, k, :], NW[:, k:k + 1], None, ALU.mult)
            last.then_inc(small_ready, 1)
            for i in range(4):
                copied(pool, "folddn", i)
                nc.gpsimd.tensor_tensor(WDN[:, 2 * i:2 * i + 2, :], WDN[:, 2 * i:2 * i + 2, :],
                                        WSDP[:, :].unsqueeze(1).to_broadcast([P, 2, D]),
                                        ALU.mult).then_inc(fold_scaled, 1)

            def rstd(p):
                pool.wait_ge(var_ready, p + 1)
                if p == 0:
                    pool.wait_ge(pool_step, 1)
                nc.gpsimd.tensor_tensor(RSTD[:, :], VEPS[:, :], NHALF[:, :], ALU.pow).then_inc(rstd_ready, 1)

            rstd(0)
            for p, (kind, b) in enumerate(PHASES[:LAST]):
                if kind == "A" and b == 0:
                    nc.gpsimd.memset(OHB, 0.0).then_inc(oh_zero, 1)
                    for i in range(2):
                        nc.gpsimd.memset(VM[i], 0.0).then_inc(oh_zero, 1)
                    pool.wait_ge(oh_zero, 3)
                    for i in range(2):
                        vm = VM[i].rearrange("p (g s c) -> p g s c", g=GR, s=4)
                        for sl in range(4):
                            nc.gpsimd.memset(vm[32 * sl:32 * sl + 32, :, sl, 0:1], 1.0).then_inc(oh_zero, 1)
                    pool.wait_ge(oh_zero, 11)
                if p + 1 < LAST:
                    rstd(p + 1)
                if kind == "M":
                    for t in range(T):
                        xd = XDT[:, t, :].rearrange("p (h c) -> p h c", c=HP)
                        if t == 0:
                            for i in range(NCUM // 2):
                                copied(pool, "cum", b, i)
                        pool.wait_ge(xdt_ready, T * b + t + 1)
                        for lv in range(LEVELS + (t < T - 1)):
                            tab = lv if lv < LEVELS else LEVELS + 1
                            n = wcount(b, t, lv)
                            if n >= 3:
                                full(pool, *wname(n - 3))
                            ft = F.rearrange("p (i t h) -> p i t h", i=NCUM, t=T)[:, tab, t, :]
                            nc.gpsimd.tensor_tensor(W[n % 3].rearrange("p (h c) -> p h c", c=HP), xd,
                                                    ft.unsqueeze(2).to_broadcast([P, NH, HP]),
                                                    ALU.mult).then_inc(w_ready, 1)
                    pool.wait_ge(ss_ready, T * (b + 1))
                    link(nc.gpsimd.tensor_scalar(SSM, SS, 1.0 / DI, EPS, ALU.mult, ALU.add))
                    nc.gpsimd.tensor_tensor(RR, SSM, NHALF[:, :], ALU.pow).then_inc(rr_ready, 1)

        @block.scalar
        def _(act):
            steps = [0]

            def link(ins):
                steps[0] += 1
                ins.then_inc(act_step, 1)
                act.wait_ge(act_step, steps[0])

            for k in range(KD):
                act.dma_start(WUGRAW[k], w_ug[k]).then_inc(wug_in, 16)
            for k in range(2):
                act.dma_start(WDNRAW[k].rearrange("p (m n) -> p m n", n=D), w_dn[k]).then_inc(wdn_in, 16)
            act.dma_start(SUUG[:, :], su_ug).then_inc(small_in, 16)
            act.dma_start(SUDP[:, :], su_dp).then_inc(small_in, 16)
            act.dma_start(WSUG[:, :], ws_ug).then_inc(small_in, 16)
            act.dma_start(WSDP[:, :], ws_dp).then_inc(small_in, 16)
            act.dma_start(WO[:, :, :], w_o).then_inc(small_in, 16)
            act.dma_start(WOUT[:, :, :], w_out).then_inc(small_in, 16)
            act.dma_start(NW[:, :], norm_w).then_inc(small_in, 16)
            act.dma_start(CW[:, :, :], conv_w).then_inc(small_in, 16)
            act.dma_start(CB[:, :], conv_b).then_inc(small_in, 16)
            act.dma_start(DTB[:, :], dt_bias).then_inc(small_in, 16)
            act.dma_start(SKIP[:, :], skip_d).then_inc(small_in, 16)
            act.dma_start(NEGA[:, :], a_log).then_inc(nega_ready, 16)
            act.wait_ge(small_in, 16 * 11)
            for i in range(8):
                c, n = i // 4, i % 4
                src = full(act, "foldug", i)
                nc.scalar.activation(WUG[:, c, n * 512:(n + 1) * 512], src[:, :], ACT.Copy,
                                     scale=SUUG[:, c:c + 1]).then_inc(emptied("foldug", i), 1)
            for i in range(4):
                src = full(act, "folddn", i)
                link(nc.scalar.activation(WDN[:, 2 * i, :], src[:, 0:D], ACT.Copy, scale=SUDP[:, 2 * i:2 * i + 1]))
                nc.scalar.activation(WDN[:, 2 * i + 1, :], src[:, D:2 * D], ACT.Copy,
                                     scale=SUDP[:, 2 * i + 1:2 * i + 2]).then_inc(emptied("folddn", i), 1)
            act.wait_ge(nega_ready, 16)
            link(nc.scalar.activation(NEGA[:, :], NEGA[:, :], ACT.Exp))

            def take_xT(p):
                for k in range(KD):
                    src = full(act, "xT", p, k)
                    nc.scalar.activation(XT[PHASES[p][1]][:, k, :], src[:, :], ACT.Copy).then_inc(emptied("xT", p, k), 1)

            def take_projections(b):
                lo, hi = slice(0, 64), slice(64, P)
                for s in range(SETS):
                    src = full(act, f"q{s}", b)
                    link(nc.scalar.activation(QS[b][s][lo, :], src[lo, :], ACT.Relu))
                    nc.scalar.activation(QS[b][s][hi, :], src[hi, :], ACT.Relu, scale=-1.0).then_inc(emptied(f"q{s}", b), 1)
                for s in range(SETS):
                    src = full(act, f"k{s}", b)
                    link(nc.scalar.activation(KEYS[b][s][lo, ::-1], src[lo, :], ACT.Copy))
                    nc.scalar.activation(KEYS[b][s][hi, :], src[hi, :], ACT.Copy, scale=-1.0).then_inc(emptied(f"k{s}", b), 1)
                for s in range(SETS):
                    for c in range(2):
                        src = full(act, f"v{s}{c}", b)
                        link(nc.scalar.activation(V[b][s][c][lo, ::-1], src[lo, :], ACT.Copy))
                        nc.scalar.activation(V[b][s][c][hi, :], src[hi, :], ACT.Copy).then_inc(emptied(f"v{s}{c}", b), 1)

            take_xT(0)
            for p, (kind, b) in enumerate(PHASES[:LAST]):
                if kind in ("F0", "F1"):
                    for m in range(TILES_OF[kind]):
                        u = UNIT0[p] + m
                        rows = LAST0 if (kind == "F0" and m == M0 - 1) else P
                        if u >= 2:
                            copied(act, "up", *UNITS[u - 2])
                        src = full(act, "gate", p, m)
                        if kind == "F0":
                            ins = nc.scalar.activation(SG[u % 2][0:rows, :], src[0:rows, :], ACT.Silu)
                        else:
                            if m == 0:
                                act.wait_ge(small_ready, 1)
                            ins = nc.scalar.activation(SG[u % 2][:, :], src[:, :], ACT.Silu,
                                                       scale=WSUG16[:, M1 + m:M1 + m + 1])
                        ins.then_inc(emptied("gate", p, m), 1)
                if kind == "A":
                    if b == 0:
                        take_projections(0)
                        take_xT(p + 1)
                        take_projections(1)
                    for s in range(SETS):
                        for g in range(GR):
                            n = (b * SETS + s) * GR + g
                            if n >= 3:
                                act.wait_ge(e_used, n - 2)
                            src = full(act, "arg", b, s, g)
                            nc.scalar.activation(E[n % 3], src[:, :], ACT.Exp).then_inc(emptied("arg", b, s, g), 1)
                        for t in range(T):
                            src = full(act, "O", b, s, t)
                            if t == 0 and s == 0 and b == 1:
                                act.wait_ge(oh_ready, T)
                            os = OS.rearrange("p (t s c) -> p t s c", t=T, s=2)
                            nc.scalar.activation(os[:, t, s, :], src[:, 0:GR * 20], ACT.Copy).then_inc(emptied("O", b, s, t), 1)
                    for k in range(2):
                        src = full(act, "oT", b, k)
                        ot = OT.rearrange("p (k n) -> p k n", k=2)
                        nc.scalar.activation(ot[:, k, :], src[:, :], ACT.Copy).then_inc(emptied("oT", b, k), 1)
                if kind == "M":
                    for c in range(CT):
                        src = full(act, "conv", b, c)
                        nc.scalar.activation(XC[:, c, :], src[:, :], ACT.Identity, bias=CB[:, c:c + 1],
                                             scale=CW[:, c, DCONV - 1:DCONV]).then_inc(conv_ready, 1)
                        if c >= 1:
                            copied(act, "conv", b, c - 1)
                            nc.scalar.activation(XC[:, c - 1, :], XC[:, c - 1, :], ACT.Silu).then_inc(xc_ready, 1)
                    copied(act, "conv", b, CT - 1)
                    nc.scalar.activation(XC[:, CT - 1, :], XC[:, CT - 1, :], ACT.Silu).then_inc(xc_ready, 1)
                    for t in range(T):
                        src = full(act, "z", b, t)
                        nc.scalar.activation(ZS[:, t, :], src[:, :], ACT.Silu).then_inc(emptied("z", b, t), 1)
                    src = full(act, "BT", b)
                    nc.scalar.activation(BT, src[:, :], ACT.Copy).then_inc(emptied("BT", b), 1)
                    for t in range(T):
                        src = full(act, "XT", b, t)
                        nc.scalar.activation(XTOK[:, t, :], src[:, :], ACT.Copy).then_inc(emptied("XT", b, t), 1)
                    act.wait_ge(dtabs_ready, b + 1)
                    nc.scalar.activation(DTU, DTA, ACT.Exp, scale=-1.0).then_inc(dtexp_ready, 1)
                    for i in range(NCUM // 2):
                        src = full(act, "cum", b, i)
                        nc.scalar.activation(F[:, i * 2 * T * NH:(i + 1) * 2 * T * NH], src[:, :], ACT.Exp)\
                          .then_inc(emptied("cum", b, i), 1)
                    for t in range(T):
                        act.wait_ge(yg_ready, T * b + t + 1)
                        if t:
                            act.wait_ge(ss_ready, T * b + t)
                        nc.scalar.activation(SQ, XTOK[:, t, :], ACT.Square, accum_out=SS[:, t:t + 1]).then_inc(ss_ready, 1)
                    for t in range(T):
                        src = full(act, "yT", b, t)
                        nc.scalar.activation(HT[b][:, t, :], src[:, :], ACT.Copy).then_inc(emptied("yT", b, t), 1)
                if p + 1 < LAST and not (kind == "A" and b == 0):
                    take_xT(p + 1)

        @block.vector
        def _(dve):
            steps = [0]

            def link(ins):
                steps[0] += 1
                ins.then_inc(dve_step, 1)
                dve.wait_ge(dve_step, steps[0])

            def lookup(dst, at, n):
                idx = IDX[:, at:at + n].bitcast(i32)
                mask = [m[:, 0:n].bitcast(i32) for m in MASK]
                sel = [s[:, 0:n] for s in SEL]
                for i in range(4):
                    link(nc.vector.tensor_scalar(mask[i], idx, 31 - i, 31, ALU.logical_shift_left, ALU.arith_shift_right))
                for k in range(8):
                    link(nc.vector.tensor_scalar(sel[k].bitcast(i32), mask[0], LUTX[:, k:k + 1].bitcast(i32),
                                            LUTB[:, 2 * k:2 * k + 1].bitcast(i32), ALU.bitwise_and, ALU.bitwise_xor))
                for bit, n_left in ((1, 4), (2, 2)):
                    for k in range(n_left):
                        step = 1 << (bit - 1)
                        a, b_ = sel[2 * k * step], sel[(2 * k + 1) * step]
                        link(nc.vector.copy_predicated(a, mask[bit], b_))
                link(nc.vector.copy_predicated(sel[0], mask[3], sel[4]))
                nc.vector.tensor_copy(dst, sel[0]).then_inc(ghost_w, 1)

            dve.wait_ge(idx_in, 16 * 5)
            link(nc.vector.tensor_tensor(LUTX[:, :].bitcast(i32), LUTB[:, 0:LUT:2].bitcast(i32),
                                         LUTB[:, 1:LUT:2].bitcast(i32), ALU.bitwise_xor))

            def layer_norm(p):
                b = PHASES[p][1]
                for t in range(T):
                    link(nc.vector.bn_stats(STAT[:, t, :], X[:, b * T + t, :]))
                    link(nc.vector.bn_aggr(MV[:, t, :], STAT[:, t, :]))
                nc.vector.tensor_scalar(VEPS[:, :], MV[:, :, 1], EPS, None, ALU.add).then_inc(var_ready, 1)
                dve.wait_ge(rstd_ready, p + 1)
                if p:
                    full(dve, "xT", p - 1, 0)
                    full(dve, "xT", p - 1, 1)
                for t in range(T):
                    nc.vector.tensor_scalar(XH[:, t, :], X[:, b * T + t, :], MV[:, t, 0:1], RSTD[:, t:t + 1],
                                            ALU.subtract, ALU.mult).then_inc(xhat_ready, 1)

            def residual(p):
                kind, b = PHASES[p]
                if kind == "M":
                    dve.wait_ge(rr_ready, b + 1)
                for j in range(2):
                    src = full(dve, "tail", p, j)
                    if kind == "M":
                        for i in range(2):
                            t = 2 * j + i
                            ins = nc.vector.scalar_tensor_tensor(X[:, b * T + t, :], src[:, i * D:(i + 1) * D], RR[:, t:t + 1],
                                                                 X[:, b * T + t, :], ALU.mult, ALU.add)
                            if i == 0:
                                link(ins)
                    else:
                        scale = {"F0": 0.5, "A": 1.0, "F1": 0.5 / 32.0}[kind]
                        xs = X[:, b * T + 2 * j:b * T + 2 * j + 2, :].rearrange("p t d -> p (t d)")
                        ins = nc.vector.scalar_tensor_tensor(xs, src[:, :], scale, xs, ALU.mult, ALU.add)
                    if j == 0:
                        ins.then_inc(emptied("tail", p, 0), 1)
                        dve.wait_ge(emptied("tail", p, 0), USES[("tail", p, 0)][1])
                    else:
                        ins.then_inc(emptied("tail", p, 1), 1)
                        dve.wait_ge(emptied("tail", p, 1), USES[("tail", p, 1)][1])

            dve.wait_ge(wdn_in, 32)
            hd = [WDNRAW[i].rearrange("p (m n) -> p m n", n=D) for i in range(2)]
            tmp = [SEL[i][:, 0:D * 4].rearrange("p (m n) -> p m n", n=D) for i in range(2)]
            link(nc.vector.tensor_tensor(tmp[0], hd[0], hd[1], ALU.add))
            link(nc.vector.tensor_tensor(tmp[1], hd[0], hd[1], ALU.subtract))
            for h in range(2):
                link(nc.vector.tensor_tensor(hd[h][:, 0:2, :], tmp[h][:, 0:2, :], tmp[h][:, 2:4, :], ALU.add))
                link(nc.vector.tensor_tensor(hd[h][:, 2:4, :], tmp[h][:, 0:2, :], tmp[h][:, 2:4, :], ALU.subtract))
            for h in range(2):
                link(nc.vector.tensor_tensor(tmp[h][:, 0:4:2, :], hd[h][:, 0:4:2, :], hd[h][:, 1:4:2, :], ALU.add))
                nc.vector.tensor_tensor(tmp[h][:, 1:4:2, :], hd[h][:, 0:4:2, :], hd[h][:, 1:4:2, :],
                                        ALU.subtract).then_inc(butter, 1)
            for i in range(4):
                full(dve, "folddn", i)
            lookup(WGATE[:, :, :].rearrange("p k n -> p (k n)"), 0, KD * INTER0)
            dve.wait_ge(ghost_w, 1)
            lookup(WUP[:, :, :].rearrange("p k n -> p (k n)"), KD * INTER0, KD * INTER0)
            dve.wait_ge(ghost_w, 2)
            dve.wait_ge(x_in, 16)
            layer_norm(0)
            lookup(WDOWN[:, :, :].rearrange("p k n -> p (k n)"), 2 * KD * INTER0, M0 * D)

            iota_b = IOTA.unsqueeze(1).to_broadcast([P, G32, 32])
            iota_a = CST[:, C_IOTA:C_IOTA + 16].unsqueeze(1).to_broadcast([P, G32, 16])

            def pick_keys(b, s):
                n = b * SETS + s
                copied(dve, f"k{s}", b)
                keys = KEYS[b][s]
                idx = IDX8.bitcast(u32)
                for r in range(TOPK // 8):
                    link(nc.vector.max(TOP[:, 8 * r:8 * r + 8], keys))
                    link(nc.vector.max_index(idx[:, 8 * r:8 * r + 8], TOP[:, 8 * r:8 * r + 8], keys))
                    if r < TOPK // 8 - 1:
                        link(nc.vector.match_replace(keys, TOP[:, 8 * r:8 * r + 8], keys, LOWEST))
                link(nc.vector.tensor_scalar(IAF, TOP, TOP[:, 0:1], None, ALU.subtract))
                if n >= 2:
                    dve.wait_ge(set_used, n - 1)
                aw = AW[n % 2].rearrange("p (g j) -> p g j", j=32)
                link(nc.vector.tensor_tensor(aw, IAF.unsqueeze(1).to_broadcast([P, GR * 4, 32]),
                                             SLOT.unsqueeze(2).to_broadcast([P, GR * 4, 32]), ALU.mult))
                link(nc.vector.tensor_scalar(IA.bitcast(u32), idx, 5, None, ALU.logical_shift_right))
                link(nc.vector.tensor_scalar(IB.bitcast(u32), idx, 31, None, ALU.bitwise_and))
                link(nc.vector.tensor_copy(IAF, IA.bitcast(u32)))
                link(nc.vector.tensor_copy(IBF, IB.bitcast(u32)))
                link(nc.vector.transpose(IAT, IAF))
                link(nc.vector.transpose(IBT, IBF))
                ohc = OHC.rearrange("p (g b) -> p g b", b=32)
                oha = OHA.rearrange("p (g a) -> p g a", a=16)
                link(nc.vector.tensor_tensor(ohc, IBT.unsqueeze(2).to_broadcast([P, G32, 32]), iota_b, ALU.is_equal))
                link(nc.vector.tensor_tensor(oha, IAT.unsqueeze(2).to_broadcast([P, G32, 16]), iota_a, ALU.is_equal))
                if n == 0:
                    dve.wait_ge(oh_zero, 11)
                ohb = OHB.rearrange("p (g k j) -> p g k j", g=G32, k=4)
                if n:
                    full(dve, "gat", (n - 1) // 2, (n - 1) % 2, 1)
                for k in range(4):
                    rows = slice(32 * k, 32 * k + 32)
                    link(nc.vector.transpose(ohb[rows, :, k, :], ohc[rows, :, :]))
                vb = VB.rearrange("p (c a g) -> p c a g", c=2, a=16)
                for c in range(2):
                    copied(dve, f"v{s}{c}", b)
                    ins = nc.vector.transpose(vb[:, c, :, :], V[b][s][c].rearrange("p (a b) -> p a b", b=32))
                    if c == 0:
                        link(ins)
                ins.then_inc(onehot_ready, 1)

            def pick_values(b, s):
                n = b * SETS + s
                oha = OHA.rearrange("p (g a) -> p g a", a=16)
                pr = PR.rearrange("p (g c a) -> p g c a", c=2, a=16)
                vs = VS.rearrange("p (g c) -> p g c", c=2)
                for i in range(2):
                    src = full(dve, "gat", b, s, i)[:, :].rearrange("p (g c a) -> p g c a", c=2, a=16)
                    for c in range(2):
                        ins = nc.vector.tensor_tensor(pr[:, 16 * i:16 * i + 16, c, :], src[:, :, c, :],
                                                      oha[:, 16 * i:16 * i + 16, :], ALU.mult)
                        if c == 0:
                            link(ins)
                    ins.then_inc(emptied("gat", b, s, i), 1)
                copied(dve, "gat", b, s, 0)
                copied(dve, "gat", b, s, 1)
                link(nc.vector.tensor_reduce(VS, PR.rearrange("p (g a) -> p g a", a=16), AX.X, ALU.add))
                vm = VM[n % 2].rearrange("p (g k c) -> p g k c", g=GR, k=4)
                for q in range(2):
                    for e in range(2):
                        for sign in range(2):
                            to = 32 * (2 * q + e)
                            fr = 32 * (2 * sign + q)
                            ins = nc.vector.tensor_copy(vm[to:to + 32, :, 2 * q + e, 1 + 2 * sign:3 + 2 * sign],
                                                        vs[fr:fr + 32, e:G32:2, :])
                            if (q, e, sign) != (1, 1, 1):
                                link(ins)
                ins.then_inc(aw_ready, 1)
                dve.wait_ge(aw_ready, n + 1)

            def combine(b):
                os = OS.rearrange("p (t m c) -> p t m c", t=T, c=5)
                for s in range(SETS):
                    for t in range(T):
                        copied(dve, "O", b, s, t)
                oh = OH.rearrange("p (t m c) -> p t m c", t=T, c=2)
                if b == 1:
                    full(dve, "oT", 0, 1)
                for t in range(T):
                    link(nc.vector.reciprocal(RD, os[:, t, :, 0]))
                    link(nc.vector.tensor_tensor(R1, RD, QM[b][:, t * P:(t + 1) * P], ALU.mult))
                    link(nc.vector.tensor_tensor(RD, RD, R1, ALU.subtract))
                    tm = OTMP.rearrange("p (m c) -> p m c", c=2)
                    link(nc.vector.tensor_tensor(oh[:, t], os[:, t, :, 1:3], R1.unsqueeze(2).to_broadcast([P, P, 2]), ALU.mult))
                    link(nc.vector.tensor_tensor(tm, os[:, t, :, 3:5], RD.unsqueeze(2).to_broadcast([P, P, 2]), ALU.mult))
                    nc.vector.tensor_tensor(oh[:, t], oh[:, t], tm, ALU.add).then_inc(oh_ready, 1)
                    dve.wait_ge(oh_ready, T * b + t + 1)

            def ffn_unit(p, m):
                kind, b = PHASES[p]
                u = UNIT0[p] + m
                rows = LAST0 if (kind == "F0" and m == M0 - 1) else P
                copied(dve, "gate", p, m)
                src = full(dve, "up", p, m)
                if kind == "F0":
                    ins = nc.vector.tensor_tensor(HT[b][0:rows, m, :], src[0:rows, :], SG[u % 2][0:rows, :], ALU.mult)
                else:
                    if m == 0:
                        dve.wait_ge(small_ready, 1)
                    ins = nc.vector.scalar_tensor_tensor(HT[b][:, m, :], src[:, :], WSUG16[:, m:m + 1],
                                                         SG[u % 2][:, :], ALU.mult, ALU.mult)
                ins.then_inc(emptied("up", p, m), 1)

            def heads(ap):
                return ap.rearrange("p (h c) -> p h c", c=HP)

            f4 = F.rearrange("p (i t h) -> p i t h", i=NCUM, t=T)

            def spread(tab, t):
                return f4[:, tab, t, :].unsqueeze(2).to_broadcast([P, NH, HP])

            def convolve(b):
                for c in range(CT):
                    dve.wait_ge(conv_ready, CT * b + c + 1)
                    src = full(dve, "conv", b, c)
                    for back in range(1, DCONV):
                        ins = nc.vector.scalar_tensor_tensor(
                            XC[:, c, back:S], src[:, 0:S - back], CW[:, c, DCONV - 1 - back:DCONV - back],
                            XC[:, c, back:S], ALU.mult, ALU.add)
                        if back < DCONV - 1:
                            link(ins)
                    ins.then_inc(emptied("conv", b, c), 1)

            def time_steps(b):
                src = full(dve, "dt", b)
                v3 = DTV.rearrange("p (t h) -> p t h", t=T)
                nc.vector.tensor_tensor(v3, src[:, 0:T * NH].rearrange("p (t h) -> p t h", t=T),
                                        DTB[:, :].unsqueeze(1).to_broadcast([P, T, NH]), ALU.add)\
                    .then_inc(emptied("dt", b), 1)
                copied(dve, "dt", b)
                nc.vector.tensor_scalar(DTA.bitcast(i32), DTV.bitcast(i32), 0x7FFFFFFF, None, ALU.bitwise_and).then_inc(dtabs_ready, 1)
                dve.wait_ge(dtexp_ready, b + 1)
                link(nc.vector.tensor_scalar(DTA, DTU, 2.0, None, ALU.add))
                link(nc.vector.reciprocal(DTP, DTA))
                link(nc.vector.tensor_tensor(DTU, DTU, DTP, ALU.mult))
                link(nc.vector.tensor_tensor(DTQ, DTU, DTU, ALU.mult))
                link(nc.vector.tensor_scalar(DTP, DTQ, 1.0 / 17.0, None, ALU.mult))
                for k in range(7, 0, -1):
                    link(nc.vector.scalar_tensor_tensor(DTP, DTP, 1.0 / (2 * k + 1), DTQ, ALU.add, ALU.mult))
                link(nc.vector.scalar_tensor_tensor(DTP, DTP, 1.0, DTU, ALU.add, ALU.mult))
                link(nc.vector.tensor_scalar(DTV, DTV, 0.0, None, ALU.max))
                link(nc.vector.scalar_tensor_tensor(DTV, DTP, 2.0, DTV, ALU.mult, ALU.add))
                nc.vector.scalar_tensor_tensor(DTA.rearrange("p (t h) -> p t h", t=T), v3, -1.0,
                                               NEGA[:, :].unsqueeze(1).to_broadcast([P, T, NH]),
                                               ALU.mult, ALU.mult).then_inc(da_ready, 1)

            def scan(b):
                v3 = DTV.rearrange("p (t h) -> p t h", t=T)
                src = full(dve, "G", b)
                gm = GM.rearrange("p (t l c) -> p t l c", t=T, l=LEVELS)
                pair = CST[:, C_PAIR:C_PAIR + LEVELS * P].rearrange("p (l c) -> p l c", l=LEVELS)
                link(nc.vector.tensor_tensor(GPR.rearrange("p (t c) -> p t c", t=T), src[:, :].rearrange("p (t c) -> p t c", t=T),
                                             IDENT.unsqueeze(1).to_broadcast([P, T, P]), ALU.mult))
                link(nc.vector.tensor_reduce(GCC, GPR.rearrange("p (t c) -> p t c", t=T), AX.X, ALU.add))
                for t in range(T):
                    ins = nc.vector.tensor_tensor(gm[:, t], src[:, t * P:(t + 1) * P].unsqueeze(1).to_broadcast([P, LEVELS, P]),
                                                  pair, ALU.mult)
                    if t < T - 1:
                        link(ins)
                ins.then_inc(emptied("G", b), 1)
                for t in range(T):
                    copied(dve, "XT", b, t)
                    nc.vector.tensor_tensor(heads(XDT[:, t, :]), heads(XTOK[:, t, :]),
                                            v3[:, t, :].unsqueeze(2).to_broadcast([P, NH, HP]), ALU.mult).then_inc(xdt_ready, 1)
                for i in range(NCUM // 2):
                    copied(dve, "cum", b, i)
                for t in range(T):
                    link(nc.vector.scalar_tensor_tensor(COEF, v3[:, t, :], GCC[:, t:t + 1], SKIP[:, :], ALU.mult, ALU.add))
                    link(nc.vector.tensor_tensor(heads(Y), heads(XTOK[:, t, :]), COEF.unsqueeze(2).to_broadcast([P, NH, HP]), ALU.mult))
                    for lv in range(LEVELS + (t > 0)):
                        name, tab = (("lev", b, t, lv), lv) if lv < LEVELS else (("off", b, t), LEVELS)
                        src = full(dve, *name)
                        rf = RF[lv % 2]
                        nc.vector.tensor_tensor(heads(rf), heads(src[:, :]), spread(tab, t), ALU.mult).then_inc(emptied(*name), 1)
                        copied(dve, *name)
                        link(nc.vector.tensor_tensor(Y, Y, rf, ALU.add))
                    if t < T - 1:
                        src = full(dve, "st", b, t)
                        if t == 0:
                            nc.vector.tensor_copy(ST[0], src[:, :]).then_inc(emptied("st", b, t), 1)
                        else:
                            link(nc.vector.tensor_tensor(heads(RF[0]), heads(ST[(t - 1) % 2]), spread(LEVELS + 2, t), ALU.mult))
                            nc.vector.tensor_tensor(ST[t % 2], RF[0], src[:, :], ALU.add).then_inc(emptied("st", b, t), 1)
                        copied(dve, "st", b, t)
                    copied(dve, "z", b, t)
                    nc.vector.tensor_tensor(XTOK[:, t, :], Y, ZS[:, t, :], ALU.mult).then_inc(yg_ready, 1)
                    dve.wait_ge(yg_ready, T * b + t + 1)

            for p, (kind, b) in enumerate(PHASES[:LAST]):
                if kind in ("F0", "F1"):
                    for m in range(TILES_OF[kind]):
                        ffn_unit(p, m)
                        if m == TILES_OF[kind] // 2 and p + 1 < LAST:
                            layer_norm(p + 1)
                if kind == "A" and b == 0:
                    layer_norm(p + 1)
                    src = full(dve, "qt", 0)
                    nc.vector.tensor_scalar(QM[0], src[:, :], 0.0, None, ALU.is_gt).then_inc(emptied("qt", 0), 1)
                    pick_keys(0, 0)
                    pick_values(0, 0)
                    src = full(dve, "qt", 1)
                    nc.vector.tensor_scalar(QM[1], src[:, :], 0.0, None, ALU.is_gt).then_inc(emptied("qt", 1), 1)
                    pick_keys(0, 1)
                    pick_values(0, 1)
                    pick_keys(1, 0)
                    combine(0)
                if kind == "A" and b == 1:
                    pick_values(1, 0)
                    pick_keys(1, 1)
                    pick_values(1, 1)
                    if p + 1 < LAST:
                        layer_norm(p + 1)
                    combine(1)
                if kind == "M":
                    convolve(b)
                    time_steps(b)
                    if p + 1 < LAST:
                        layer_norm(p + 1)
                    scan(b)
                residual(p)

        @block.tensor
        def _(pe):
            def begin(*name):
                i, n = USES[name]
                if n > 1:
                    pe.wait_ge(bank_free[i], n - 1)
                return bank[i]

            def done(ins, *name):
                ins.then_inc(bank_full[USES[name][0]], 1)

            def front(p):
                pe.wait_ge(xhat_ready, T * (p + 1))
                for k in range(KD):
                    dst = begin("xT", p, k)
                    for t in range(T):
                        ins = nc.tensor.transpose(dst[:, t * P:(t + 1) * P], XH[:, t, k * P:(k + 1) * P], IDENT)
                    done(ins, "xT", p, k)

            pe.wait_ge(cst_in, 16)
            pe.wait_ge(wug_in, 32)
            for i in range(8):
                c, n = i // 4, i % 4
                dst = begin("foldug", i)
                for k in range(KD):
                    ins = nc.tensor.matmul(dst[:, :], NHAD if (c and k) else HAD, WUGRAW[k][:, n * 512:(n + 1) * 512],
                                           start=(k == 0), stop=(k == KD - 1))
                done(ins, "foldug", i)
            pe.wait_ge(butter, 2)
            for i in range(4):
                dst = begin("folddn", i)
                done(nc.tensor.matmul(dst[:, :], HAD, SEL[i // 2][:, (i % 2) * 2 * D:(i % 2 + 1) * 2 * D],
                                      start=True, stop=True), "folddn", i)
            front(0)

            def projections(b):
                for i, n in enumerate(("q0", "q1", "k0", "k1", "v00", "v01", "v10", "v11")):
                    dst = begin(n, b)
                    for k in range(KD):
                        ins = nc.tensor.matmul(dst[:, :], WQKV[:, k, i * P:(i + 1) * P], XT[b][:, k, :],
                                               start=(k == 0), stop=(k == KD - 1))
                    done(ins, n, b)
                dst = begin("qt", b)
                for t in range(T):
                    for k in range(KD):
                        ins = nc.tensor.matmul(dst[:, t * P:(t + 1) * P], XT[b][:, k, t * P:(t + 1) * P], WQT[:, k, :],
                                               start=(k == 0), stop=(k == KD - 1))
                done(ins, "qt", b)

            def ffn_units(p):
                kind, b = PHASES[p]
                for m in range(TILES_OF[kind]):
                    rows = LAST0 if (kind == "F0" and m == M0 - 1) else P
                    for name in ("gate", "up"):
                        dst = begin(name, p, m)
                        if kind == "F0":
                            w, at = (WGATE if name == "gate" else WUP), m * P
                            if p == 0 and m == 0:
                                pe.wait_ge(ghost_w, 1 if name == "gate" else 2)
                        else:
                            w, at = WUG, m * P + (INTER1 if name == "gate" else 0)
                        for k in range(KD):
                            ins = nc.tensor.matmul(dst[0:rows, :], w[:, k, at:at + rows], XT[b][:, k, :],
                                                   start=(k == 0), stop=(k == KD - 1))
                        done(ins, name, p, m)

            def attend(b, s):
                n = b * SETS + s
                pe.wait_ge(onehot_ready, n + 1)
                vb = VB.rearrange("p (c a g) -> p c a g", c=2, a=16)
                for i in range(2):
                    dst = begin("gat", b, s, i)
                    for g in range(16):
                        gg = 16 * i + g
                        ins = nc.tensor.matmul(dst[:, g * 32:(g + 1) * 32], OHB[:, gg * P:(gg + 1) * P],
                                               vb[:, :, :, gg], start=True, stop=True)
                    done(ins, "gat", b, s, i)
                pe.wait_ge(aw_ready, n + 1)
                for t in range(T):
                    begin("O", b, s, t)
                for step in range(GR + 1):
                    if step < GR:
                        dst = begin("arg", b, s, step)
                        done(nc.tensor.matmul(dst[:, :], AW[n % 2][:, step * P:(step + 1) * P], QS[b][s],
                                              start=True, stop=True), "arg", b, s, step)
                    if step:
                        g = step - 1
                        copied(pe, "arg", b, s, g)
                        for t in range(T):
                            dst = bank[USES[("O", b, s, t)][0]]
                            ins = nc.tensor.matmul(dst[:, g * 20:(g + 1) * 20], E[(n * GR + g) % 3][:, t * P:(t + 1) * P],
                                                   VM[n % 2][:, g * 20:(g + 1) * 20], start=True, stop=True)
                            if g == GR - 1:
                                done(ins, "O", b, s, t)
                        if g < GR - 1:
                            ins.then_inc(e_used, 1)
                full(pe, "O", b, s, T - 1)
                pe.sem_inc(e_used, 1)
                pe.sem_inc(set_used, 1)

            def scan(b):
                for c in range(CT):
                    dst = begin("conv", b, c)
                    for k in range(KD):
                        ins = nc.tensor.matmul(dst[:, :], WIN[:, k, DI + c * P:DI + (c + 1) * P], XT[b][:, k, :],
                                               start=(k == 0), stop=(k == KD - 1))
                    done(ins, "conv", b, c)
                dst = begin("dt", b)
                for t in range(T):
                    for k in range(KD):
                        ins = nc.tensor.matmul(dst[:, t * NH:(t + 1) * NH], XT[b][:, k, t * P:(t + 1) * P],
                                               WIN[:, k, DI + CONVC:DI + CONVC + NH], start=(k == 0), stop=(k == KD - 1))
                done(ins, "dt", b)
                for t in range(T):
                    dst = begin("z", b, t)
                    for k in range(KD):
                        ins = nc.tensor.matmul(dst[:, :], XT[b][:, k, t * P:(t + 1) * P], WIN[:, k, 0:DI],
                                               start=(k == 0), stop=(k == KD - 1))
                    done(ins, "z", b, t)
                pe.wait_ge(xc_ready, CT * (b + 1))
                dst = begin("G", b)
                for t in range(T):
                    ts = slice(t * P, (t + 1) * P)
                    ins = nc.tensor.matmul(dst[:, ts], XC[:, 4, ts], XC[:, 5, ts], start=True, stop=True)
                done(ins, "G", b)
                dst = begin("BT", b)
                for t in range(T):
                    ts = slice(t * P, (t + 1) * P)
                    ins = nc.tensor.transpose(dst[:, ts], XC[:, 4, ts], IDENT)
                done(ins, "BT", b)
                for t in range(T):
                    dst = begin("XT", b, t)
                    for c in range(4):
                        ins = nc.tensor.transpose(dst[:, c * P:(c + 1) * P], XC[:, c, t * P:(t + 1) * P], IDENT)
                    done(ins, "XT", b, t)
                pe.wait_ge(da_ready, b + 1)
                for i in range(NCUM // 2):
                    dst = begin("cum", b, i)
                    for j in range(2):
                        at = C_CUM + (2 * i + j) * P
                        ins = nc.tensor.matmul(dst[:, j * T * NH:(j + 1) * T * NH], CST[:, at:at + P], DTA, start=True, stop=True)
                    done(ins, "cum", b, i)
                copied(pe, "G", b)
                copied(pe, "BT", b)
                for t in range(T):
                    for lv in range(LEVELS):
                        n = wcount(b, t, lv)
                        dst = begin("lev", b, t, lv)
                        pe.wait_ge(w_ready, n + 1)
                        at = (t * LEVELS + lv) * P
                        done(nc.tensor.matmul(dst[:, :], GM[:, at:at + P], W[n % 3], start=True, stop=True), "lev", b, t, lv)
                    if t:
                        dst = begin("off", b, t)
                        copied(pe, "st", b, t - 1)
                        done(nc.tensor.matmul(dst[:, :], XC[:, 5, t * P:(t + 1) * P], ST[(t - 1) % 2],
                                              start=True, stop=True), "off", b, t)
                    if t < T - 1:
                        n = wcount(b, t, LEVELS)
                        dst = begin("st", b, t)
                        pe.wait_ge(w_ready, n + 1)
                        done(nc.tensor.matmul(dst[:, :], BT[:, t * P:(t + 1) * P], W[n % 3], start=True, stop=True), "st", b, t)
                for t in range(T):
                    pe.wait_ge(yg_ready, T * b + t + 1)
                    dst = begin("yT", b, t)
                    for c in range(4):
                        ins = nc.tensor.transpose(dst[:, c * P:(c + 1) * P], XTOK[:, t, c * P:(c + 1) * P], IDENT)
                    done(ins, "yT", b, t)

            def tail(p):
                kind, b = PHASES[p]
                if kind == "F0":
                    if p == 0:
                        pe.wait_ge(ghost_w, 3)
                    for m in range(M0):
                        copied(pe, "up", p, m)
                    rows = [LAST0 if m == M0 - 1 else P for m in range(M0)]
                    terms = [(lambda t, m=m: HT[b][0:rows[m], m, t * P:(t + 1) * P], WDOWN[0:rows[m], m, :]) for m in range(M0)]
                if kind == "F1":
                    pe.wait_ge(fold_scaled, 4)
                    for m in range(M1):
                        copied(pe, "up", p, m)
                    terms = [(lambda t, m=m: HT[b][:, m, t * P:(t + 1) * P], WDN[:, m, :]) for m in range(M1)]
                if kind == "A":
                    copied(pe, "oT", b, 0)
                    copied(pe, "oT", b, 1)
                    terms = [(lambda t, k=k: OT[:, k * S + t * P:k * S + (t + 1) * P], WO[:, k, :]) for k in range(2)]
                if kind == "M":
                    pe.wait_ge(small_ready, 2)
                    for t in range(T):
                        copied(pe, "yT", b, t)
                    terms = [(lambda t, c=c: HT[b][:, t, c * P:(c + 1) * P], WOUT[:, c, :]) for c in range(4)]
                for j in range(2):
                    dst = begin("tail", p, j)
                    for i in range(2):
                        for m, (lhs, rhs) in enumerate(terms):
                            ins = nc.tensor.matmul(dst[:, i * D:(i + 1) * D], lhs(2 * j + i), rhs,
                                                   start=(m == 0), stop=(m == len(terms) - 1))
                    done(ins, "tail", p, j)

            for p, (kind, b) in enumerate(PHASES[:LAST]):
                if not (kind == "A" and b == 1):
                    for k in range(KD):
                        copied(pe, "xT", p, k)
                if kind in ("F0", "F1"):
                    ffn_units(p)
                if kind == "A" and b == 0:
                    pe.wait_ge(attn_w_in, 32)
                    projections(0)
                    front(p + 1)
                    for k in range(KD):
                        copied(pe, "xT", p + 1, k)
                    projections(1)
                if kind == "A":
                    for s in range(SETS):
                        attend(b, s)
                    pe.wait_ge(oh_ready, T * (b + 1))
                    for k in range(2):
                        dst = begin("oT", b, k)
                        for t in range(T):
                            ins = nc.tensor.transpose(dst[:, t * P:(t + 1) * P], OH[:, t * D + k * P:t * D + (k + 1) * P], IDENT)
                        done(ins, "oT", b, k)
                if kind == "M":
                    if b == 0:
                        pe.wait_ge(win_in, 16)
                    scan(b)
                if p + 1 < LAST and not (kind == "A" and b == 0):
                    front(p + 1)
                tail(p)


def kernel(phases_run=NPHASE, **inputs):
    import concourse.bacc as _bacc
    from concourse.bass_utils import run_bass_kernel_spmd as _run

    inp = {k: np.asarray(v) for k, v in inputs.items()}

    def rows(w, k):
        return np.ascontiguousarray(w.reshape(k, P, -1).transpose(1, 0, 2))

    def spread(v):
        return np.ascontiguousarray(np.broadcast_to(v, (P, v.shape[0])))

    def dup(w, s):
        return np.concatenate([w[64 * s:64 * s + 64]] * 2, axis=0).T

    wq, wk, wv = inp["L0_attn_Wq"], inp["L0_attn_Wk"], inp["L0_attn_Wv"]
    wvh = wv.reshape(HEADS, 2, D)
    w_qkv = np.concatenate([dup(wq, 0), dup(wq, 1), dup(wk, 0), dup(wk, 1)]
                           + [dup(wvh[:, c], s) for s in range(SETS) for c in range(2)], axis=1)
    order = np.array([64 * s + 32 * q + 2 * g + e for s in range(SETS) for g in range(GR) for q in range(2) for e in range(2)])
    w_o = inp["L0_attn_Wo"].T.reshape(HEADS, 2, D)[order].reshape(D, D)
    w_up, w_gate = inp["L1_ffn_W_up"], inp["L1_ffn_W_gate"]
    arrays = {
        "x": inp["L0_attn_x"].reshape(B * S, D),
        "cst": constants(),
        "gate_idx": rows(inp["L0_ffn_gate_idx"].T, KD).reshape(P, -1),
        "up_idx": rows(inp["L0_ffn_up_idx"].T, KD).reshape(P, -1),
        "down_idx": inp["L0_ffn_down_idx"].T,
        "lut": spread(inp["L0_ffn_lut"]),
        "w_ug": np.concatenate([w_up, w_gate], axis=0).T.reshape(KD, P, 2 * INTER1),
        "w_dn": inp["L1_ffn_W_down"].T.reshape(2, 4, P, D).transpose(0, 2, 1, 3),
        "su_ug": inp["L1_ffn_SU_ug"].reshape(KD, P).T,
        "su_dp": inp["L1_ffn_SU_dp"].reshape(M1, P).T,
        "ws_ug": inp["L1_ffn_Wscale_ug"].reshape(2 * M1, P).T,
        "ws_dp": spread(inp["L1_ffn_Wscale_dp"]),
        "w_qkv": rows(w_qkv, KD),
        "w_qt": rows(wq[order].T, KD),
        "w_o": rows(w_o, 2),
        "w_in": rows(inp["L1_attn_in_proj_w"].T, KD),
        "conv_w": rows(inp["L1_attn_conv_w"], CT),
        "conv_b": inp["L1_attn_conv_b"].reshape(CT, P).T,
        "dt_bias": spread(inp["L1_attn_dt_bias"]),
        "a_log": spread(inp["L1_attn_A_log"]),
        "skip_d": spread(inp["L1_attn_D"]),
        "norm_w": inp["L1_attn_norm_weight"].reshape(4, P).T,
        "w_out": rows(inp["L1_attn_out_proj_w"].T, 4),
    }
    nc = _bacc.Bacc("TRN2", target_bir_lowering=False, num_devices=1)
    maps, args = {}, []
    for name, a in arrays.items():
        a = np.ascontiguousarray(a)
        maps[f"in_{name}"] = a
        args.append(nc.dram_tensor(f"in_{name}", a.shape, mybir.dt.from_np(a.dtype), kind="ExternalInput").ap())
    out = nc.dram_tensor("out_0_dram", (B * S, D), mybir.dt.float32, kind="ExternalOutput").ap()
    program(nc, *args, out, phases_run=phases_run)
    r = _run(nc, [maps], core_ids=[0])
    return r.results[0]["out_0_dram"].reshape(B, S, D)
```

```python
import concourse.bass as bass
from concourse import mybir
from contextlib import ExitStack
import numpy as np

B = 2
S = 512
D = 256
P = 128
T = S // P
KD = D // P
INTER0 = 688
M0 = -(-INTER0 // P)
LAST0 = INTER0 - (M0 - 1) * P
LUT = 16
INTER1 = 1024
M1 = INTER1 // P
HEADS = 128
TOPK = 32
ROUNDS = TOPK // 8
SETS = 2
GR = 16
G32 = 32
DI = 512
NH = 64
HP = DI // NH
CONVC = 768
CT = CONVC // P
DCONV = 4
LEVELS = 7
NCUM = LEVELS + 3
EPS = 1e-5
LOWEST = -3.0e38
NPHASE = 12

PHASES = [(kind, b) for kind in ("F0", "A", "F0", "F1", "M", "F1") for b in range(B)]
TILES_OF = {"F0": M0, "F1": M1}


def weave(first, second, every):
    out, rest = [], list(second)
    for i, step in enumerate(first):
        out.append(step)
        if rest and (i + 1) % every == 0:
            out += rest.pop(0)
    return out + sum(rest, [])


def schedule():
    def norm(p):
        return [("stats", p), ("xhat", p), ("front", p)]

    def units(p, m0=0, m1=None):
        return [("unit", p, m) for m in range(m0, TILES_OF[PHASES[p][0]] if m1 is None else m1)]

    def end(p):
        return [("tail", p), ("resid", p)]

    out = norm(0) + [("look", 0)] + norm(1) + [("butterfly",), ("look", 1), ("foldug", 0)]
    for m in range(M0):
        out += units(0, m, m + 1)
        out += [("look", m + 2)] if m + 2 < M0 else [("lookdown", m + 2 - M0)]
        out += [("foldug", m + 1)] + (units(1, m, m + 1) if m < 3 else [])
    out += [("foldug", 7)] + [("folddn", i) for i in range(3)] + [("lookdown", 2)]
    out += end(0) + [("stats", 2), ("xhat", 2), ("folddn", 3)] + units(1, 3, 4) + [("front", 2), ("clear",), ("proj", 0)]
    out += [("keys", 0, 0), ("keys", 0, 1)] + units(1, 4, 5) + [("keys", 0, 2), ("keys", 0, 3)] + units(1, 5)
    out += [("qt", 0), ("hots", 0)] + end(1) + [("stats", 3), ("xhat", 3), ("gather", 0), ("front", 3)]
    out += [("keys", 1, 0), ("keys", 1, 1), ("values", 0), ("keys", 1, 2), ("keys", 1, 3), ("proj", 1), ("hots", 1), ("qt", 1)]
    for n in range(2 * SETS):
        for g in range(GR + 1):
            out += [("att", n, g)]
            if n and 1 <= g <= T:
                out += [("ot", n - 1, g - 1)]
            if g == 6 and n + 1 < 2 * SETS:
                out += [("gather", n + 1)]
            if n + 2 < 2 * SETS and g in (4, 6, 8, 10):
                out += [("keys", n + 2, (g - 4) // 2)]
            if g == 9 and n + 1 < 2 * SETS:
                out += [("values", n + 1)]
            if g == 11 and n + 2 < 2 * SETS:
                out += [("hots", n + 2)]
            if n == 2 and g == 10:
                out += [("oT", 0), ("tail", 2), ("resid", 2), ("stats", 4), ("xhat", 4)]
            if n == 2 and g == 15:
                out += [("front", 4)]
            if n == 3 and g >= 6 and g % 2 == 0:
                out += units(4, (g - 6) // 2, (g - 6) // 2 + 1)
    out += [("ot", 3, t) for t in range(T)] + [("tail", 4), ("resid", 4), ("oT", 1), ("stats", 6), ("xhat", 6)]
    out += [("tail", 3), ("front", 6)] + [("resid", 3), ("stats", 5), ("xhat", 5)] + units(6, 0, 2) + [("front", 5)]
    out += units(5) + units(6, 2, 3) + end(5) + [("stats", 7), ("xhat", 7)]
    out += units(6, 3, 5) + [("front", 7)] + units(6, 5)
    out += units(7, 0, 1) + end(6) + [("stats", 8), ("xhat", 8)] + units(7, 1, 2) + [("front", 8)]

    def scan_front(b):
        return [("conv", b, c) for c in range(CT)] + [("dt", b)] + [("z", b, t) for t in range(T)] \
            + [("G", b)] + [("xt", b, t) for t in range(T)] + [("cum", b, i) for i in range(NCUM // 2)]

    def scan_levels(b):
        steps = []
        for t in range(T):
            steps += [("y0", b, t)] + [("lev", b, t, lv) for lv in range(LEVELS)]
            steps += [("off", b, t)] if t else []
            steps += [("st", b, t)] if t < T - 1 else []
            steps += [("yg", b, t)]
        return steps

    def scan_end(b):
        return [("rr", b)] + [("yT", b, t) for t in range(T)]

    def single(steps):
        return [[step] for step in steps]

    out += weave(scan_front(0), single(units(7, 2, 4)), 6)
    out += weave(scan_levels(0), single(units(7, 4)) + [end(7), [("stats", 9), ("xhat", 9)], [("front", 9)]], 4)
    out += scan_end(0) + [("conv", 1, c) for c in range(3)] + end(8) + [("stats", 10), ("xhat", 10)]
    out += scan_front(1)[3:10] + [("front", 10)] + weave(scan_front(1)[10:], single(units(10, 0, 2)), 5)
    out += weave(scan_levels(1), single(units(10, 2)) + [end(10)], 4)
    out += scan_end(1) + end(9) + norm(11) + units(11) + end(11)
    return out


SCHEDULE = schedule()
NORMS = [s[1] for s in SCHEDULE if s[0] == "stats"]
UNITS = [s[1:] for s in SCHEDULE if s[0] == "unit"]


def constants():
    ident = np.eye(P, dtype=np.float32)
    had = np.array([[1.0]], np.float32)
    while had.shape[0] < P:
        had = np.block([[had, had], [had, -had]]).astype(np.float32)
    t = np.arange(P)
    cum = np.zeros((NCUM, P, P), np.float32)
    pair = np.zeros((LEVELS, P, P), np.float32)
    r, c = np.meshgrid(t, t, indexing="ij")
    for lv in range(LEVELS):
        half = 1 << lv
        mid = (c // (2 * half)) * 2 * half + half
        right = c >= mid
        cum[lv] = np.where(right, (r >= mid) & (r <= c), (r > c) & (r < mid))
        pair[lv] = (r // (2 * half) == c // (2 * half)) & right & (r < mid)
    cum[LEVELS] = r <= c
    cum[LEVELS + 1] = r > c
    cum[LEVELS + 2] = 1.0
    rows = t
    q, g = (rows // 32) % 2, rows % 32
    slot = np.zeros((P, GR, 4), np.float32)
    slot[rows, g // 2, 2 * q + g % 2] = 1.0
    iota32 = np.broadcast_to(np.arange(32, dtype=np.float32), (P, 32))
    return np.concatenate([
        ident, had, -had,
        cum.transpose(1, 0, 2).reshape(P, -1),
        pair.transpose(1, 0, 2).reshape(P, -1),
        slot.reshape(P, -1), iota32,
    ], axis=1).astype(np.float32)


C_ID, C_H, C_NH = 0, P, 2 * P
C_CUM = 3 * P
C_PAIR = C_CUM + NCUM * P
C_SLOT = C_PAIR + LEVELS * P
C_IOTA = C_SLOT + GR * 4
C_ALL = C_IOTA + 32


def psum_uses():
    uses, count, ring = {}, [0] * 8, [0]

    def use(bank, *name):
        count[bank] += 1
        uses[name] = (bank, count[bank])

    def scan(*name):
        use(4 + ring[0] % 4, *name)
        ring[0] += 1

    for kind, *at in SCHEDULE:
        if kind == "front":
            for k in range(KD):
                use(6 + k, "xT", at[0], k)
        elif kind == "foldug":
            use(at[0] % 4, kind, *at)
        elif kind == "folddn":
            use(4 + at[0] % 2, kind, *at)
        elif kind == "unit":
            slot = 6 if at[0] == 4 else 2 * (UNITS.index(tuple(at)) % 2)
            use(slot, "gate", *at)
            use(slot + 1, "up", *at)
        elif kind == "tail":
            for j in range(2):
                use(4 + j, "tail", at[0], j)
        elif kind == "proj":
            for i, n in enumerate(PROJ):
                use(i % 4, n, at[0])
        elif kind == "qt":
            use(4, "qt", at[0])
        elif kind == "gather":
            for i in range(2):
                use(6 + i, "gat", at[0], i)
        elif kind == "att":
            n, g = at
            if g < GR:
                use(4 + g % 2, "arg", n, g)
            if g % 4 == 1:
                use(g // 4, "O", n, g // 4)
        elif kind == "ot":
            use(6 + at[1] % 2, kind, *at)
        elif kind == "oT":
            for k in range(2):
                use(6 + k, "oT", at[0], k)
        elif kind == "G":
            scan("G", at[0])
            scan("BT", at[0])
        elif kind in ("conv", "dt", "z", "xt", "cum", "lev", "off", "st", "yT"):
            scan(kind, *at)
    return uses


COPY_AT = {5: 0, 9: 1, 13: 2, 16: 3}
PROJ = ("k0", "v00", "v01", "k1", "v10", "v11", "q0", "q1")


def program(nc, x, cst, gu_idx, down_idx, lut, w_ug, w_dn, su_ug, su_dp, ws_ug, ws_dp,
            w_qkv, w_qt, w_o, w_in, conv_w, conv_b, dt_bias, a_log, skip_d, norm_w, w_out, out):
    f32, i32, u32 = mybir.dt.float32, mybir.dt.int32, mybir.dt.uint32
    ALU, ACT = mybir.AluOpType, mybir.ActivationFunctionType
    AX = mybir.AxisListType
    USES = psum_uses()
    ctx = ExitStack()
    with ctx:
        def sb(name, shape, dt=f32):
            return ctx.enter_context(nc.sbuf_tensor(name, shape, dt))

        def sem(name):
            return ctx.enter_context(nc.semaphore(name))

        bank = [ctx.enter_context(nc.psum_tensor(f"bank{i}", [P, 512], f32)) for i in range(8)]

        CST = sb("CST", [P, C_ALL])
        IDENT = CST[:, C_ID:C_ID + P]
        HAD, NHAD = CST[:, C_H:C_H + P], CST[:, C_NH:C_NH + P]
        SLOT = CST[:, C_SLOT:C_SLOT + GR * 4]
        IOTA = CST[:, C_IOTA:C_IOTA + 32]
        X = sb("X", [P, B * T, D])
        XH = sb("XH", [P, T, D])
        XT = [sb(f"XT{b}", [P, KD, S]) for b in range(B)]
        STAT = sb("STAT", [P, T, 6])
        MV = sb("MV", [P, T, 2])
        VEPS = sb("VEPS", [P, T])
        RSTD = sb("RSTD", [P, T])
        NHALF = sb("NHALF", [P, T])
        WGU = sb("WGU", [P, 2 * KD * INTER0])
        WDOWN = sb("WDOWN", [P, M0 * D])
        WUG = sb("WUG", [P, KD, 2 * INTER1])
        WDN = sb("WDN", [P, M1, D])
        HT = [sb(f"HT{b}", [P, M1, S]) for b in range(B)]
        SG = [sb(f"SG{i}", [P, S]) for i in range(2)]
        WSUG = sb("WSUG", [P, 2 * M1])
        WSUG16 = sb("WSUG16", [P, 2 * M1])
        SUUG = sb("SUUG", [P, KD])
        SUDP = sb("SUDP", [P, M1])
        WO = sb("WO", [P, 2, D])
        WOUT = sb("WOUT", [P, 4, D])
        NW = sb("NW", [P, 4])
        CW = sb("CW", [P, CT, DCONV])
        CB = sb("CB", [P, CT])
        DTB = sb("DTB", [P, NH])
        NEGA = sb("NEGA", [P, NH])
        SKIP = sb("SKIP", [P, NH])

        USIZE = 23600
        U = sb("U", [P, USIZE])
        cur = [0]

        def part(n):
            cur[0] += n
            assert cur[0] <= USIZE, cur[0]
            return U[:, cur[0] - n:cur[0]]

        def ht(b, at, n):
            return HT[b][:, :, :].rearrange("p a b -> p (a b)")[:, at:at + n]

        NIDX = 2 * KD * INTER0 + M0 * D
        CHUNK = 2 * KD * P
        LUTB = sb("LUTB", [P, LUT])
        LUTX = sb("LUTX", [P, LUT // 2])
        cur[0] = 0
        IDX = part(NIDX)
        MASK = [part(CHUNK) for _ in range(4)]
        SEL = [part(CHUNK) for _ in range(7)]
        WUGRAW = [part(2 * INTER1) for _ in range(KD)]
        WDNRAW = [part(4 * D) for _ in range(2)]
        BUTTER = [part(4 * D) for _ in range(2)]
        WSDP = sb("WSDP", [P, D])

        cur[0] = 0
        WQKV = part(KD * 8 * P).rearrange("p (k n) -> p k n", k=KD)
        WQT = part(KD * P).rearrange("p (k n) -> p k n", k=KD)
        QS = [[part(S) for _ in range(SETS)] for _ in range(B)]
        KEYS = [[part(S) for _ in range(SETS)] for _ in range(B)]
        V = [[[part(S) for _ in range(2)] for _ in range(SETS)] for _ in range(B)]
        QM = [part(S) for _ in range(B)]
        TOP = part(TOPK)
        IDX8 = part(TOPK)
        IA, IB = part(TOPK), part(TOPK)
        IAF, IBF = part(TOPK), part(TOPK)
        EXPO = [part(TOPK) for _ in range(2)]
        IAT, IBT = part(TOPK), part(TOPK)
        VB = ht(0, 0, 2 * S)
        OHC = ht(0, 2 * S, G32 * 32)
        OHA = ht(0, 4 * S, G32 * 16)
        OHB = part(G32 * 4 * 32)
        PR = ht(0, 5 * S, G32 * 2 * 16)
        VS = part(G32 * 2)
        AW = [part(GR * P) for _ in range(2)]
        VM = [part(GR * 32) for _ in range(2)]
        E = [ht(1, (5 + i) * S, S) for i in range(3)]
        OC = ht(1, 0, 4 * S).rearrange("p (j s) -> p j s", j=4)
        OH = part(T * D)
        RD, R1 = part(P // SETS), part(P // SETS)
        OT = part(2 * S)
        OTMP = part(D // SETS)

        cur[0] = 0
        WIN = part(KD * 1344).rearrange("p (k n) -> p k n", k=KD)
        XC = part(CT * S).rearrange("p (c s) -> p c s", c=CT)
        ZS = part(T * DI).rearrange("p (t n) -> p t n", t=T)
        XTOK = part(T * DI).rearrange("p (t n) -> p t n", t=T)
        XDT = [ht(b, 4 * S, T * DI).rearrange("p (t n) -> p t n", t=T) for b in range(B)]
        YT = HT
        BT = part(T * P)
        GM = part(T * LEVELS * P)
        F = part(NCUM * T * NH)
        DTV, DTA, DTU, DTP, DTQ = (part(T * NH) for _ in range(5))
        GCC = part(T)
        GPR = part(T * P)
        W = [part(DI) for _ in range(3)]
        Y = part(DI)
        RF = [part(DI) for _ in range(2)]
        ST = [part(DI) for _ in range(2)]
        SS = part(T)
        SSM = part(T)
        RR = part(T)
        SQ = part(DI)
        COEF = part(NH)

        bank_full = [sem(f"bank_full{i}") for i in range(8)]
        bank_free = [sem(f"bank_free{i}") for i in range(8)]
        x_in = [sem(f"x_in{b}") for b in range(B)]
        cst_in = sem("cst_in")
        tables_in = sem("tables_in")
        lut_in = sem("lut_in")
        gu_first_in = sem("gu_first_in")
        gu_rest_in = sem("gu_rest_in")
        down_idx_in = sem("down_idx_in")
        idx_zero = sem("idx_zero")
        wug_in = sem("wug_in")
        wdn_in = sem("wdn_in")
        small_in = sem("small_in")
        attn_w_in = sem("attn_w_in")
        win_in = sem("win_in")
        out_done = sem("out_done")
        dve_step = sem("dve_step")
        pool_step = sem("pool_step")
        act_step = sem("act_step")
        ghost_w = sem("ghost_w")
        butter = sem("butter")
        fold_scaled = sem("fold_scaled")
        var_ready = sem("var_ready")
        rstd_ready = sem("rstd_ready")
        xhat_ready = sem("xhat_ready")
        xT_ready = sem("xT_ready")
        small_ready = sem("small_ready")
        nega_ready = sem("nega_ready")
        proj_ready = sem("proj_ready")
        oh_zero = sem("oh_zero")
        onehot_ready = sem("onehot_ready")
        top_ready = sem("top_ready")
        aw_ready = sem("aw_ready")
        vm_ready = sem("vm_ready")
        e_ready = sem("e_ready")
        e_used = sem("e_used")
        oh_ready = sem("oh_ready")
        oT_ready = sem("oT_ready")
        conv_ready = sem("conv_ready")
        xc_ready = sem("xc_ready")
        zs_ready = sem("zs_ready")
        dtabs_ready = sem("dtabs_ready")
        dtexp_ready = sem("dtexp_ready")
        da_ready = sem("da_ready")
        bt_ready = sem("bt_ready")
        xtok_ready = sem("xtok_ready")
        xdt_ready = sem("xdt_ready")
        gm_ready = sem("gm_ready")
        w_ready = sem("w_ready")
        rf_ready = sem("rf_ready")
        y_step = sem("y_step")
        state_ready = sem("state_ready")
        yg_ready = sem("yg_ready")
        ss_ready = sem("ss_ready")
        rr_ready = sem("rr_ready")
        yT_ready = sem("yT_ready")
        block = ctx.enter_context(nc.Block())

        def full(eng, *name):
            i, n = USES[name]
            eng.wait_ge(bank_full[i], n)
            return bank[i]

        def emptied(*name):
            return bank_free[USES[name][0]]

        def copied(eng, *name):
            i, n = USES[name]
            eng.wait_ge(bank_free[i], n)

        @block.sync
        def _(sp):
            sp.dma_start(X[:, 0:T, :], x[0:S, :].rearrange("(t p) d -> p t d", p=P)).then_inc(x_in[0], 16)
            sp.dma_start(LUTB[:, :], lut).then_inc(lut_in, 16)
            gu = IDX[:, 0:2 * KD * INTER0].bitcast(i32)
            sp.dma_start(gu[:, 0:CHUNK], gu_idx[:, 0:CHUNK]).then_inc(gu_first_in, 16)
            sp.dma_start(X[:, T:2 * T, :], x[S:2 * S, :].rearrange("(t p) d -> p t d", p=P)).then_inc(x_in[1], 16)
            sp.dma_start(gu[:, CHUNK:2 * KD * INTER0], gu_idx[:, CHUNK:2 * KD * INTER0]).then_inc(gu_rest_in, 16)
            sp.wait_ge(idx_zero, 1)
            dn = IDX[:, 2 * KD * INTER0:NIDX].bitcast(i32)
            sp.dma_start(dn[:, 0:(M0 - 1) * D].rearrange("p (m n) -> p m n", n=D),
                         down_idx[0:(M0 - 1) * P, :].rearrange("(m p) n -> p m n", p=P)).then_inc(down_idx_in, 16)
            sp.dma_start(dn[0:LAST0, (M0 - 1) * D:M0 * D], down_idx[(M0 - 1) * P:INTER0, :]).then_inc(down_idx_in, 16)
            sp.wait_ge(ghost_w, M0 + M0 // 2)
            sp.dma_start(WQKV, w_qkv).then_inc(attn_w_in, 16)
            sp.dma_start(WQT, w_qt).then_inc(attn_w_in, 16)
            if ("tail", 3, 1) in USES:
                copied(sp, "tail", 3, 1)
                sp.dma_start(WIN, w_in).then_inc(win_in, 16)
            last = max(name[1] for name in USES if name[0] == "tail")
            for p in (last - 1, last):
                for j in range(2):
                    copied(sp, "tail", p, j)
            sp.dma_start(out.rearrange("(t p) d -> p t d", p=P), X[:, :, :]).then_inc(out_done, 16)
            sp.wait_ge(out_done, 16)

        WLIST = [(b, t, lv) for b in range(B) for t in range(T) for lv in range(LEVELS + (t < T - 1))]

        def wcount(b, t, lv):
            return WLIST.index((b, t, lv))

        def wname(n):
            b, t, lv = WLIST[n]
            return ("lev", b, t, lv) if lv < LEVELS else ("st", b, t)

        @block.gpsimd
        def _(pool):
            pool.memset(IDX[:, 2 * KD * INTER0 + (M0 - 1) * D:NIDX], 0.0).then_inc(idx_zero, 1)
            steps = [0]

            def link(ins):
                steps[0] += 1
                ins.then_inc(pool_step, 1)
                pool.wait_ge(pool_step, steps[0])

            link(pool.memset(NHALF[:, :], -0.5))

            def butterfly():
                pool.wait_ge(wdn_in, 32)
                hd = [WDNRAW[i].rearrange("p (m n) -> p m n", n=D) for i in range(2)]
                tmp = [BUTTER[i].rearrange("p (m n) -> p m n", n=D) for i in range(2)]
                nc.gpsimd.tensor_tensor(tmp[0], hd[0], hd[1], ALU.add)
                link(nc.gpsimd.tensor_tensor(tmp[1], hd[0], hd[1], ALU.subtract))
                for h in range(2):
                    nc.gpsimd.tensor_tensor(hd[h][:, 0:2, :], tmp[h][:, 0:2, :], tmp[h][:, 2:4, :], ALU.add)
                    link(nc.gpsimd.tensor_tensor(hd[h][:, 2:4, :], tmp[h][:, 0:2, :], tmp[h][:, 2:4, :], ALU.subtract))
                for h in range(2):
                    link(nc.gpsimd.tensor_tensor(tmp[h][:, 0:4:2, :], hd[h][:, 0:4:2, :], hd[h][:, 1:4:2, :], ALU.add))
                    nc.gpsimd.tensor_tensor(tmp[h][:, 1:4:2, :], hd[h][:, 0:4:2, :], hd[h][:, 1:4:2, :],
                                            ALU.subtract).then_inc(butter, 1)
                pool.wait_ge(small_in, 16 * 11)
                nc.gpsimd.tensor_scalar(WSUG16[:, :], WSUG[:, :], 1.0 / 16.0, None, ALU.mult).then_inc(small_ready, 1)
                for k in range(4):
                    last = nc.gpsimd.tensor_scalar(WOUT[:, k, :], WOUT[:, k, :], NW[:, k:k + 1], None, ALU.mult)
                last.then_inc(small_ready, 1)

            def clear():
                pool.wait_ge(ghost_w, M0 + M0 // 2)
                copied(pool, "foldug", 7)
                nc.gpsimd.memset(OHB, 0.0).then_inc(oh_zero, 1)
                for i in range(2):
                    nc.gpsimd.memset(VM[i], 0.0).then_inc(oh_zero, 1)
                pool.wait_ge(oh_zero, 3)
                for i in range(2):
                    vm = VM[i].rearrange("p (g c) -> p g c", g=GR)
                    for sl in range(4):
                        nc.gpsimd.memset(vm[32 * sl:32 * sl + 32, :, 5 * sl:5 * sl + 1], 1.0).then_inc(oh_zero, 1)
                pool.wait_ge(oh_zero, 11)

            def weighted(b, t, lv):
                if (t, lv) == (0, 0):
                    for i in range(NCUM // 2):
                        copied(pool, "cum", b, i)
                if lv == 0:
                    pool.wait_ge(xdt_ready, T * b + t + 1)
                tab = lv if lv < LEVELS else LEVELS + 1
                n = wcount(b, t, lv)
                if n >= 3:
                    full(pool, *wname(n - 3))
                xd = XDT[b][:, t, :].rearrange("p (h c) -> p h c", c=HP)
                ft = F.rearrange("p (i t h) -> p i t h", i=NCUM, t=T)[:, tab, t, :]
                nc.gpsimd.tensor_tensor(W[n % 3].rearrange("p (h c) -> p h c", c=HP), xd,
                                        ft.unsqueeze(2).to_broadcast([P, NH, HP]), ALU.mult).then_inc(w_ready, 1)

            for kind, *at in SCHEDULE:
                if kind == "stats":
                    pool.wait_ge(var_ready, NORMS.index(at[0]) + 1)
                    nc.gpsimd.tensor_tensor(RSTD[:, :], VEPS[:, :], NHALF[:, :], ALU.pow).then_inc(rstd_ready, 1)
                elif kind == "butterfly":
                    butterfly()
                elif kind == "folddn":
                    i = at[0]
                    copied(pool, "folddn", i)
                    nc.gpsimd.tensor_tensor(WDN[:, 2 * i:2 * i + 2, :], WDN[:, 2 * i:2 * i + 2, :],
                                            WSDP[:, :].unsqueeze(1).to_broadcast([P, 2, D]),
                                            ALU.mult).then_inc(fold_scaled, 1)
                elif kind == "clear":
                    clear()
                elif kind == "keys" and at[1] == ROUNDS - 1:
                    n = at[0]
                    pool.wait_ge(top_ready, n + 1)
                    if n == 0:
                        pool.wait_ge(tables_in, 16)
                    if n >= 2:
                        full(pool, "O", n - 2, 3)
                    aw = AW[n % 2].rearrange("p (g j) -> p g j", j=32)
                    nc.gpsimd.tensor_tensor(aw, EXPO[n % 2].unsqueeze(1).to_broadcast([P, GR * 4, 32]),
                                            SLOT.unsqueeze(2).to_broadcast([P, GR * 4, 32]), ALU.mult).then_inc(aw_ready, 1)
                elif kind == "lev":
                    weighted(*at)
                elif kind == "st":
                    weighted(at[0], at[1], LEVELS)
                elif kind == "rr":
                    pool.wait_ge(ss_ready, T * (at[0] + 1))
                    link(nc.gpsimd.tensor_scalar(SSM, SS, 1.0 / DI, EPS, ALU.mult, ALU.add))
                    nc.gpsimd.tensor_tensor(RR, SSM, NHALF[:, :], ALU.pow).then_inc(rr_ready, 1)

        @block.scalar
        def _(act):
            steps = [0]

            def link(ins):
                steps[0] += 1
                ins.then_inc(act_step, 1)
                act.wait_ge(act_step, steps[0])

            act.dma_start(CST[:, 0:C_CUM], cst[:, 0:C_CUM]).then_inc(cst_in, 16)
            for k in range(KD):
                act.dma_start(WUGRAW[k], w_ug[k]).then_inc(wug_in, 16)
            for k in range(2):
                act.dma_start(WDNRAW[k].rearrange("p (m n) -> p m n", n=D), w_dn[k]).then_inc(wdn_in, 16)
            act.dma_start(SUUG[:, :], su_ug).then_inc(small_in, 16)
            act.dma_start(SUDP[:, :], su_dp).then_inc(small_in, 16)
            act.dma_start(WSUG[:, :], ws_ug).then_inc(small_in, 16)
            act.dma_start(WSDP[:, :], ws_dp).then_inc(small_in, 16)
            act.dma_start(WO[:, :, :], w_o).then_inc(small_in, 16)
            act.dma_start(WOUT[:, :, :], w_out).then_inc(small_in, 16)
            act.dma_start(NW[:, :], norm_w).then_inc(small_in, 16)
            act.dma_start(CW[:, :, :], conv_w).then_inc(small_in, 16)
            act.dma_start(CB[:, :], conv_b).then_inc(small_in, 16)
            act.dma_start(DTB[:, :], dt_bias).then_inc(small_in, 16)
            act.dma_start(SKIP[:, :], skip_d).then_inc(small_in, 16)
            act.dma_start(NEGA[:, :], a_log).then_inc(nega_ready, 16)
            act.dma_start(CST[:, C_CUM:C_ALL], cst[:, C_CUM:C_ALL]).then_inc(tables_in, 16)

            def take_xT(p):
                for k in range(KD):
                    src = full(act, "xT", p, k)
                    nc.scalar.activation(XT[PHASES[p][1]][:, k, :], src[:, :], ACT.Copy).then_inc(emptied("xT", p, k), 1)

            def take_projections(b):
                lo, hi = slice(0, 64), slice(64, P)
                for name in PROJ:
                    src = full(act, name, b)
                    s = int(name[1])
                    if name[0] == "k":
                        dst, func, scale = KEYS[b][s], ACT.Copy, -1.0
                    elif name[0] == "v":
                        dst, func, scale = V[b][s][int(name[2])], ACT.Copy, 1.0
                    else:
                        dst, func, scale = QS[b][s], ACT.Relu, -1.0
                    top = dst[lo, :] if name[0] == "q" else dst[lo, ::-1]
                    link(nc.scalar.activation(top, src[lo, :], func))
                    nc.scalar.activation(dst[hi, :], src[hi, :], func, scale=scale).then_inc(emptied(name, b), 1)

            def silu_gate(p, m):
                kind = PHASES[p][0]
                u = UNITS.index((p, m))
                rows = LAST0 if (kind == "F0" and m == M0 - 1) else P
                if u >= 2:
                    copied(act, "up", *UNITS[u - 2])
                src = full(act, "gate", p, m)
                if kind == "F0":
                    ins = nc.scalar.activation(SG[u % 2][0:rows, :], src[0:rows, :], ACT.Silu)
                else:
                    if m == 0:
                        act.wait_ge(small_ready, 1)
                    ins = nc.scalar.activation(SG[u % 2][:, :], src[:, :], ACT.Silu,
                                               scale=WSUG16[:, M1 + m:M1 + m + 1])
                ins.then_inc(emptied("gate", p, m), 1)

            def attend(n, g):
                if g < GR:
                    k = n * GR + g
                    if k >= 3:
                        n3, g3 = divmod(k - 3, GR)
                        if g3 % 4 == 3:
                            full(act, "O", n3, g3 // 4)
                        else:
                            act.wait_ge(e_used, k - 2 - (k - 2) // 4)
                    src = full(act, "arg", n, g)
                    nc.scalar.activation(E[k % 3], src[:, :], ACT.Exp).then_inc(emptied("arg", n, g), 1)
                j = COPY_AT.get(g)
                if j is not None:
                    if n and j == 0:
                        full(act, "ot", n - 1, T - 1)
                    src = full(act, "O", n, j)
                    nc.scalar.activation(OC[:, j, :], src[:, :], ACT.Copy).then_inc(emptied("O", n, j), 1)

            def silu_conv(b, c):
                copied(act, "conv", b, c)
                nc.scalar.activation(XC[:, c, :], XC[:, c, :], ACT.Silu).then_inc(xc_ready, 1)

            for kind, *at in SCHEDULE:
                if kind == "front":
                    take_xT(*at)
                elif kind == "foldug":
                    c, n = at[0] // 4, at[0] % 4
                    if at[0] == 0:
                        act.wait_ge(small_in, 16 * 11)
                    src = full(act, "foldug", *at)
                    nc.scalar.activation(WUG[:, c, n * 512:(n + 1) * 512], src[:, :], ACT.Copy,
                                         scale=SUUG[:, c:c + 1]).then_inc(emptied("foldug", *at), 1)
                elif kind == "folddn":
                    i = at[0]
                    src = full(act, "folddn", i)
                    link(nc.scalar.activation(WDN[:, 2 * i, :], src[:, 0:D], ACT.Copy, scale=SUDP[:, 2 * i:2 * i + 1]))
                    nc.scalar.activation(WDN[:, 2 * i + 1, :], src[:, D:2 * D], ACT.Copy,
                                         scale=SUDP[:, 2 * i + 1:2 * i + 2]).then_inc(emptied("folddn", i), 1)
                elif kind == "clear":
                    act.wait_ge(nega_ready, 16)
                    nc.scalar.activation(NEGA[:, :], NEGA[:, :], ACT.Exp).then_inc(nega_ready, 1)
                elif kind == "unit":
                    silu_gate(*at)
                elif kind == "proj":
                    take_projections(*at)
                elif kind == "att":
                    attend(*at)
                elif kind == "oT":
                    ot = OT.rearrange("p (k n) -> p k n", k=2)
                    for k in range(2):
                        src = full(act, "oT", at[0], k)
                        nc.scalar.activation(ot[:, k, :], src[:, :], ACT.Copy).then_inc(emptied("oT", at[0], k), 1)
                elif kind == "conv":
                    b, c = at
                    src = full(act, "conv", b, c)
                    nc.scalar.activation(XC[:, c, :], src[:, :], ACT.Identity, bias=CB[:, c:c + 1],
                                         scale=CW[:, c, DCONV - 1:DCONV]).then_inc(conv_ready, 1)
                    if c >= 1:
                        silu_conv(b, c - 1)
                elif kind == "dt":
                    b = at[0]
                    silu_conv(b, CT - 1)
                    act.wait_ge(dtabs_ready, b + 1)
                    nc.scalar.activation(DTU, DTA, ACT.Exp, scale=-1.0).then_inc(dtexp_ready, 1)
                elif kind == "z":
                    src = full(act, "z", *at)
                    nc.scalar.activation(ZS[:, at[1], :], src[:, :], ACT.Silu).then_inc(emptied("z", *at), 1)
                elif kind == "G":
                    src = full(act, "BT", *at)
                    nc.scalar.activation(BT, src[:, :], ACT.Copy).then_inc(emptied("BT", *at), 1)
                elif kind == "xt":
                    src = full(act, "xt", *at)
                    nc.scalar.activation(XTOK[:, at[1], :], src[:, :], ACT.Copy).then_inc(emptied("xt", *at), 1)
                elif kind == "cum":
                    b, i = at
                    src = full(act, "cum", b, i)
                    nc.scalar.activation(F[:, i * 2 * T * NH:(i + 1) * 2 * T * NH], src[:, :], ACT.Exp)\
                      .then_inc(emptied("cum", b, i), 1)
                elif kind == "yg":
                    b, t = at
                    act.wait_ge(yg_ready, T * b + t + 1)
                    if b or t:
                        act.wait_ge(ss_ready, T * b + t)
                    nc.scalar.activation(SQ, XTOK[:, t, :], ACT.Square, accum_out=SS[:, t:t + 1]).then_inc(ss_ready, 1)
                elif kind == "yT":
                    b, t = at
                    src = full(act, "yT", b, t)
                    nc.scalar.activation(YT[b][:, t, :], src[:, :], ACT.Copy).then_inc(emptied("yT", b, t), 1)

        @block.vector
        def _(dve):
            steps = [0]

            def link(ins):
                steps[0] += 1
                ins.then_inc(dve_step, 1)
                dve.wait_ge(dve_step, steps[0])

            def lookup(c, dst, at, n):
                if c:
                    dve.wait_ge(ghost_w, c)
                idx = IDX[:, at:at + n].bitcast(i32)
                mask = [m[:, 0:n].bitcast(i32) for m in MASK]
                sel = [dst] + [s[:, 0:n] for s in SEL]
                for i in range(4):
                    ins = nc.vector.tensor_scalar(mask[i], idx, 31 - i, 31, ALU.logical_shift_left, ALU.arith_shift_right)
                link(ins)
                for k in range(8):
                    ins = nc.vector.tensor_scalar(sel[k].bitcast(i32), mask[0], LUTX[:, k:k + 1].bitcast(i32),
                                                  LUTB[:, 2 * k:2 * k + 1].bitcast(i32), ALU.bitwise_and, ALU.bitwise_xor)
                link(ins)
                for k in (0, 2, 4, 6):
                    ins = nc.vector.copy_predicated(sel[k], mask[1], sel[k + 1])
                link(ins)
                for k in (0, 4):
                    ins = nc.vector.copy_predicated(sel[k], mask[2], sel[k + 2])
                link(ins)
                nc.vector.copy_predicated(sel[0], mask[3], sel[4]).then_inc(ghost_w, 1)

            dve.wait_ge(lut_in, 16)
            link(nc.vector.tensor_tensor(LUTX[:, :].bitcast(i32), LUTB[:, 0:LUT:2].bitcast(i32),
                                         LUTB[:, 1:LUT:2].bitcast(i32), ALU.bitwise_xor))

            def stats(p):
                b = PHASES[p][1]
                if p < B:
                    dve.wait_ge(x_in[b], 16)
                for t in range(T):
                    ins = nc.vector.bn_stats(STAT[:, t, :], X[:, b * T + t, :])
                link(ins)
                for t in range(T):
                    ins = nc.vector.bn_aggr(MV[:, t, :], STAT[:, t, :])
                link(ins)
                nc.vector.tensor_scalar(VEPS[:, :], MV[:, :, 1], EPS, None, ALU.add).then_inc(var_ready, 1)

            def xhat(p):
                b = PHASES[p][1]
                i = NORMS.index(p)
                dve.wait_ge(rstd_ready, i + 1)
                if i:
                    full(dve, "xT", NORMS[i - 1], 0)
                    full(dve, "xT", NORMS[i - 1], 1)
                for t in range(T):
                    nc.vector.tensor_scalar(XH[:, t, :], X[:, b * T + t, :], MV[:, t, 0:1], RSTD[:, t:t + 1],
                                            ALU.subtract, ALU.mult).then_inc(xhat_ready, 1)

            def residual(p):
                kind, b = PHASES[p]
                if kind == "M":
                    dve.wait_ge(rr_ready, b + 1)
                for j in range(2):
                    src = full(dve, "tail", p, j)
                    if kind == "M":
                        for i in range(2):
                            t = 2 * j + i
                            ins = nc.vector.scalar_tensor_tensor(X[:, b * T + t, :], src[:, i * D:(i + 1) * D], RR[:, t:t + 1],
                                                                 X[:, b * T + t, :], ALU.mult, ALU.add)
                            if i == 0:
                                link(ins)
                    else:
                        scale = {"F0": 0.5, "A": 1.0, "F1": 0.5 / 32.0}[kind]
                        xs = X[:, b * T + 2 * j:b * T + 2 * j + 2, :].rearrange("p t d -> p (t d)")
                        ins = nc.vector.scalar_tensor_tensor(xs, src[:, :], scale, xs, ALU.mult, ALU.add)
                    if j == 0:
                        ins.then_inc(emptied("tail", p, 0), 1)
                        dve.wait_ge(emptied("tail", p, 0), USES[("tail", p, 0)][1])
                    else:
                        ins.then_inc(emptied("tail", p, 1), 1)
                        dve.wait_ge(emptied("tail", p, 1), USES[("tail", p, 1)][1])

            iota_b = IOTA.unsqueeze(1).to_broadcast([P, G32, 32])
            iota_a = CST[:, C_IOTA:C_IOTA + 16].unsqueeze(1).to_broadcast([P, G32, 16])

            def pick_keys(n, r):
                b, s = n // SETS, n % SETS
                if r == 0:
                    copied(dve, f"k{s}", b)
                keys = KEYS[b][s]
                eight = slice(8 * r, 8 * r + 8)
                link(nc.vector.max(TOP[:, eight], keys))
                link(nc.vector.max_index(IDX8.bitcast(u32)[:, eight], TOP[:, eight], keys))
                if r < ROUNDS - 1:
                    link(nc.vector.match_replace(keys, TOP[:, eight], keys, LOWEST))
                else:
                    nc.vector.tensor_scalar(EXPO[n % 2], TOP, TOP[:, 0:1], None, ALU.subtract).then_inc(top_ready, 1)
                    dve.wait_ge(top_ready, n + 1)

            def one_hots(n):
                b, s = n // SETS, n % SETS
                idx = IDX8.bitcast(u32)
                if n == 0:
                    dve.wait_ge(tables_in, 16)
                link(nc.vector.tensor_scalar(IA.bitcast(u32), idx, 5, None, ALU.logical_shift_right))
                link(nc.vector.tensor_scalar(IB.bitcast(u32), idx, 31, None, ALU.bitwise_and))
                link(nc.vector.tensor_copy(IAF, IA.bitcast(u32)))
                link(nc.vector.tensor_copy(IBF, IB.bitcast(u32)))
                link(nc.vector.transpose(IAT, IAF))
                link(nc.vector.transpose(IBT, IBF))
                ohc = OHC.rearrange("p (g b) -> p g b", b=32)
                oha = OHA.rearrange("p (g a) -> p g a", a=16)
                link(nc.vector.tensor_tensor(ohc, IBT.unsqueeze(2).to_broadcast([P, G32, 32]), iota_b, ALU.is_equal))
                link(nc.vector.tensor_tensor(oha, IAT.unsqueeze(2).to_broadcast([P, G32, 16]), iota_a, ALU.is_equal))
                if n == 0:
                    dve.wait_ge(oh_zero, 11)
                ohb = OHB.rearrange("p (g k j) -> p g k j", g=G32, k=4)
                if n:
                    full(dve, "gat", n - 1, 1)
                for k in range(4):
                    rows = slice(32 * k, 32 * k + 32)
                    link(nc.vector.transpose(ohb[rows, :, k, :], ohc[rows, :, :]))
                vb = VB.rearrange("p (c a g) -> p c a g", c=2, a=16)
                for c in range(2):
                    copied(dve, f"v{s}{c}", b)
                    ins = nc.vector.transpose(vb[:, c, :, :], V[b][s][c].rearrange("p (a b) -> p a b", b=32))
                    if c == 0:
                        link(ins)
                ins.then_inc(onehot_ready, 1)

            def pick_values(n):
                oha = OHA.rearrange("p (g a) -> p g a", a=16)
                pr = PR.rearrange("p (g c a) -> p g c a", c=2, a=16)
                vs = VS.rearrange("p (g c) -> p g c", c=2)
                for i in range(2):
                    src = full(dve, "gat", n, i)[:, :].rearrange("p (g c a) -> p g c a", c=2, a=16)
                    for c in range(2):
                        ins = nc.vector.tensor_tensor(pr[:, 16 * i:16 * i + 16, c, :], src[:, :, c, :],
                                                      oha[:, 16 * i:16 * i + 16, :], ALU.mult)
                        if c == 0:
                            link(ins)
                    ins.then_inc(emptied("gat", n, i), 1)
                copied(dve, "gat", n, 0)
                copied(dve, "gat", n, 1)
                link(nc.vector.tensor_reduce(VS, PR.rearrange("p (g a) -> p g a", a=16), AX.X, ALU.add))
                if n >= 2:
                    full(dve, "O", n - 2, 3)
                vm = VM[n % 2].rearrange("p (g c) -> p g c", g=GR)
                for q in range(2):
                    for e in range(2):
                        for sign in range(2):
                            to = 32 * (2 * q + e)
                            fr = 32 * (2 * sign + q)
                            col = 5 * (2 * q + e) + 1 + 2 * sign
                            ins = nc.vector.tensor_copy(vm[to:to + 32, :, col:col + 2],
                                                        vs[fr:fr + 32, e:G32:2, :])
                            if (q, e, sign) != (1, 1, 1):
                                link(ins)
                ins.then_inc(vm_ready, 1)
                dve.wait_ge(vm_ready, n + 1)

            def combine(n, t):
                b, s = n // SETS, n % SETS
                src = full(dve, "ot", n, t)
                sums = src[:, :].rearrange("p (g k) -> p g k", k=32)[:, :, 0:20].rearrange("p g (m c) -> p g m c", c=5)
                heads_s = slice(s * P // SETS, (s + 1) * P // SETS)
                qm = QM[b][:, t * P:(t + 1) * P][:, heads_s]
                oh = OH.rearrange("p (t m c) -> p t m c", t=T, c=2)[:, t, heads_s, :].rearrange("p (g m) c -> p g m c", m=4)
                if b == 1:
                    full(dve, "oT", 0, 1)
                four = lambda ap: ap.rearrange("p (g m) -> p g m", m=4)
                link(nc.vector.reciprocal(four(RD), sums[:, :, :, 0]))
                link(nc.vector.tensor_tensor(R1, RD, qm, ALU.mult))
                link(nc.vector.tensor_tensor(RD, RD, R1, ALU.subtract))
                tm = OTMP.rearrange("p (g m c) -> p g m c", m=4, c=2)
                to = [P, GR, 4, 2]
                link(nc.vector.tensor_tensor(oh, sums[:, :, :, 1:3], four(R1).unsqueeze(3).to_broadcast(to), ALU.mult))
                nc.vector.tensor_tensor(tm, sums[:, :, :, 3:5], four(RD).unsqueeze(3).to_broadcast(to), ALU.mult)\
                    .then_inc(emptied("ot", n, t), 1)
                copied(dve, "ot", n, t)
                nc.vector.tensor_tensor(oh, oh, tm, ALU.add).then_inc(oh_ready, 1)
                dve.wait_ge(oh_ready, T * n + t + 1)

            def ffn_unit(p, m):
                kind, b = PHASES[p]
                u = UNITS.index((p, m))
                rows = LAST0 if (kind == "F0" and m == M0 - 1) else P
                copied(dve, "gate", p, m)
                src = full(dve, "up", p, m)
                if kind == "F0":
                    ins = nc.vector.tensor_tensor(HT[b][0:rows, m, :], src[0:rows, :], SG[u % 2][0:rows, :], ALU.mult)
                else:
                    if m == 0:
                        dve.wait_ge(small_ready, 1)
                    ins = nc.vector.scalar_tensor_tensor(HT[b][:, m, :], src[:, :], WSUG16[:, m:m + 1],
                                                         SG[u % 2][:, :], ALU.mult, ALU.mult)
                ins.then_inc(emptied("up", p, m), 1)

            def heads(ap):
                return ap.rearrange("p (h c) -> p h c", c=HP)

            f4 = F.rearrange("p (i t h) -> p i t h", i=NCUM, t=T)

            def spread(tab, t):
                return f4[:, tab, t, :].unsqueeze(2).to_broadcast([P, NH, HP])

            def convolve(b):
                for c in range(CT):
                    dve.wait_ge(conv_ready, CT * b + c + 1)
                    src = full(dve, "conv", b, c)
                    for back in range(1, DCONV):
                        ins = nc.vector.scalar_tensor_tensor(
                            XC[:, c, back:S], src[:, 0:S - back], CW[:, c, DCONV - 1 - back:DCONV - back],
                            XC[:, c, back:S], ALU.mult, ALU.add)
                        if back < DCONV - 1:
                            link(ins)
                    ins.then_inc(emptied("conv", b, c), 1)

            def time_steps(b):
                src = full(dve, "dt", b)
                v3 = DTV.rearrange("p (t h) -> p t h", t=T)
                nc.vector.tensor_tensor(v3, src[:, 0:T * NH].rearrange("p (t h) -> p t h", t=T),
                                        DTB[:, :].unsqueeze(1).to_broadcast([P, T, NH]), ALU.add)\
                    .then_inc(emptied("dt", b), 1)
                copied(dve, "dt", b)
                nc.vector.tensor_scalar(DTA.bitcast(i32), DTV.bitcast(i32), 0x7FFFFFFF, None, ALU.bitwise_and).then_inc(dtabs_ready, 1)
                dve.wait_ge(dtexp_ready, b + 1)
                link(nc.vector.tensor_scalar(DTA, DTU, 2.0, None, ALU.add))
                link(nc.vector.reciprocal(DTP, DTA))
                link(nc.vector.tensor_tensor(DTU, DTU, DTP, ALU.mult))
                link(nc.vector.tensor_tensor(DTQ, DTU, DTU, ALU.mult))
                link(nc.vector.tensor_scalar(DTP, DTQ, 1.0 / 17.0, None, ALU.mult))
                for k in range(7, 0, -1):
                    link(nc.vector.scalar_tensor_tensor(DTP, DTP, 1.0 / (2 * k + 1), DTQ, ALU.add, ALU.mult))
                link(nc.vector.scalar_tensor_tensor(DTP, DTP, 1.0, DTU, ALU.add, ALU.mult))
                link(nc.vector.tensor_scalar(DTV, DTV, 0.0, None, ALU.max))
                link(nc.vector.scalar_tensor_tensor(DTV, DTP, 2.0, DTV, ALU.mult, ALU.add))
                nc.vector.scalar_tensor_tensor(DTA.rearrange("p (t h) -> p t h", t=T), v3, -1.0,
                                               NEGA[:, :].unsqueeze(1).to_broadcast([P, T, NH]),
                                               ALU.mult, ALU.mult).then_inc(da_ready, 1)

            def mask_products(b):
                src = full(dve, "G", b)
                gm = GM.rearrange("p (t l c) -> p t l c", t=T, l=LEVELS)
                pair = CST[:, C_PAIR:C_PAIR + LEVELS * P].rearrange("p (l c) -> p l c", l=LEVELS)
                link(nc.vector.tensor_tensor(GPR.rearrange("p (t c) -> p t c", t=T), src[:, :].rearrange("p (t c) -> p t c", t=T),
                                             IDENT.unsqueeze(1).to_broadcast([P, T, P]), ALU.mult))
                link(nc.vector.tensor_reduce(GCC, GPR.rearrange("p (t c) -> p t c", t=T), AX.X, ALU.add))
                for t in range(T):
                    ins = nc.vector.tensor_tensor(gm[:, t], src[:, t * P:(t + 1) * P].unsqueeze(1).to_broadcast([P, LEVELS, P]),
                                                  pair, ALU.mult)
                    if t < T - 1:
                        link(ins)
                ins.then_inc(emptied("G", b), 1)

            v3 = DTV.rearrange("p (t h) -> p t h", t=T)

            def own_term(b, t):
                if t == 0:
                    for i in range(NCUM // 2):
                        copied(dve, "cum", b, i)
                link(nc.vector.scalar_tensor_tensor(COEF, v3[:, t, :], GCC[:, t:t + 1], SKIP[:, :], ALU.mult, ALU.add))
                link(nc.vector.tensor_tensor(heads(Y), heads(XTOK[:, t, :]), COEF.unsqueeze(2).to_broadcast([P, NH, HP]), ALU.mult))

            def add_span(name, b, t, lv, tab):
                src = full(dve, *name)
                rf = RF[lv % 2]
                nc.vector.tensor_tensor(heads(rf), heads(src[:, :]), spread(tab, t), ALU.mult).then_inc(emptied(*name), 1)
                copied(dve, *name)
                link(nc.vector.tensor_tensor(Y, Y, rf, ALU.add))

            def state(b, t):
                src = full(dve, "st", b, t)
                if t == 0:
                    nc.vector.tensor_copy(ST[0], src[:, :]).then_inc(emptied("st", b, t), 1)
                else:
                    link(nc.vector.tensor_tensor(heads(RF[0]), heads(ST[(t - 1) % 2]), spread(LEVELS + 2, t), ALU.mult))
                    nc.vector.tensor_tensor(ST[t % 2], RF[0], src[:, :], ALU.add).then_inc(emptied("st", b, t), 1)
                copied(dve, "st", b, t)

            for kind, *at in SCHEDULE:
                if kind == "stats":
                    stats(*at)
                elif kind == "xhat":
                    xhat(*at)
                elif kind == "look":
                    m = at[0]
                    if m < 2:
                        dve.wait_ge((gu_first_in, gu_rest_in)[m], 16)
                    n = 2 * KD * (LAST0 if m == M0 - 1 else P)
                    lookup(m, WGU[:, m * CHUNK:m * CHUNK + n], m * CHUNK, n)
                elif kind == "lookdown":
                    i = at[0]
                    if i == 0:
                        dve.wait_ge(down_idx_in, 32)
                    lookup(M0 + i, WDOWN[:, i * CHUNK:(i + 1) * CHUNK], 2 * KD * INTER0 + i * CHUNK, CHUNK)
                elif kind == "unit":
                    ffn_unit(*at)
                elif kind == "resid":
                    residual(*at)
                elif kind == "qt":
                    src = full(dve, "qt", *at)
                    nc.vector.tensor_scalar(QM[at[0]], src[:, :], 0.0, None, ALU.is_gt).then_inc(emptied("qt", *at), 1)
                elif kind == "keys":
                    pick_keys(*at)
                elif kind == "hots":
                    one_hots(*at)
                elif kind == "values":
                    pick_values(*at)
                elif kind == "ot":
                    combine(*at)
                elif kind == "conv":
                    b, c = at
                    dve.wait_ge(conv_ready, CT * b + c + 1)
                    src = full(dve, "conv", b, c)
                    for back in range(1, DCONV):
                        ins = nc.vector.scalar_tensor_tensor(
                            XC[:, c, back:S], src[:, 0:S - back], CW[:, c, DCONV - 1 - back:DCONV - back],
                            XC[:, c, back:S], ALU.mult, ALU.add)
                        if back < DCONV - 1:
                            link(ins)
                    ins.then_inc(emptied("conv", b, c), 1)
                elif kind == "dt":
                    time_steps(*at)
                elif kind == "G":
                    mask_products(*at)
                elif kind == "xt":
                    b, t = at
                    copied(dve, "xt", b, t)
                    nc.vector.tensor_tensor(heads(XDT[b][:, t, :]), heads(XTOK[:, t, :]),
                                            v3[:, t, :].unsqueeze(2).to_broadcast([P, NH, HP]), ALU.mult).then_inc(xdt_ready, 1)
                elif kind == "y0":
                    own_term(*at)
                elif kind == "lev":
                    b, t, lv = at
                    add_span(("lev", b, t, lv), b, t, lv, lv)
                elif kind == "off":
                    b, t = at
                    add_span(("off", b, t), b, t, LEVELS, LEVELS)
                elif kind == "st":
                    state(*at)
                elif kind == "yg":
                    b, t = at
                    if t == 0:
                        copied(dve, "z", b, T - 1)
                    nc.vector.tensor_tensor(XTOK[:, t, :], Y, ZS[:, t, :], ALU.mult).then_inc(yg_ready, 1)
                    dve.wait_ge(yg_ready, T * b + t + 1)

        @block.tensor
        def _(pe):
            def begin(*name):
                i, n = USES[name]
                if n > 1:
                    pe.wait_ge(bank_free[i], n - 1)
                return bank[i]

            def done(ins, *name):
                ins.then_inc(bank_full[USES[name][0]], 1)

            def front(p):
                pe.wait_ge(xhat_ready, T * (NORMS.index(p) + 1))
                for k in range(KD):
                    dst = begin("xT", p, k)
                    for t in range(T):
                        ins = nc.tensor.transpose(dst[:, t * P:(t + 1) * P], XH[:, t, k * P:(k + 1) * P], IDENT)
                    done(ins, "xT", p, k)

            def projections(b):
                if b == 0:
                    pe.wait_ge(attn_w_in, 32)
                at = {"q0": 0, "q1": 1, "k0": 2, "k1": 3, "v00": 4, "v01": 5, "v10": 6, "v11": 7}
                for n in PROJ:
                    dst = begin(n, b)
                    for k in range(KD):
                        ins = nc.tensor.matmul(dst[:, :], WQKV[:, k, at[n] * P:(at[n] + 1) * P], XT[b][:, k, :],
                                               start=(k == 0), stop=(k == KD - 1))
                    done(ins, n, b)

            def queries(b):
                dst = begin("qt", b)
                for t in range(T):
                    for k in range(KD):
                        ins = nc.tensor.matmul(dst[:, t * P:(t + 1) * P], XT[b][:, k, t * P:(t + 1) * P], WQT[:, k, :],
                                               start=(k == 0), stop=(k == KD - 1))
                done(ins, "qt", b)

            def ffn_unit(p, m):
                kind, b = PHASES[p]
                rows = LAST0 if (kind == "F0" and m == M0 - 1) else P
                if m == 0:
                    for k in range(KD):
                        copied(pe, "xT", p, k)
                if p < B:
                    pe.wait_ge(ghost_w, m + 1)
                for i, name in enumerate(("gate", "up")):
                    dst = begin(name, p, m)
                    for k in range(KD):
                        if kind == "F0":
                            at = m * CHUNK + (i * KD + k) * rows
                            w = WGU[:, at:at + rows]
                        else:
                            at = m * P + (INTER1 if name == "gate" else 0)
                            w = WUG[:, k, at:at + P]
                        ins = nc.tensor.matmul(dst[0:rows, :], w, XT[b][:, k, :], start=(k == 0), stop=(k == KD - 1))
                    done(ins, name, p, m)

            def gather(n):
                pe.wait_ge(onehot_ready, n + 1)
                vb = VB.rearrange("p (c a g) -> p c a g", c=2, a=16)
                for i in range(2):
                    dst = begin("gat", n, i)
                    for g in range(16):
                        gg = 16 * i + g
                        ins = nc.tensor.matmul(dst[:, g * 32:(g + 1) * 32], OHB[:, gg * P:(gg + 1) * P],
                                               vb[:, :, :, gg], start=True, stop=True)
                    done(ins, "gat", n, i)

            def attend(n, step):
                b, s = n // SETS, n % SETS
                if step == 0:
                    pe.wait_ge(aw_ready, n + 1)
                    pe.wait_ge(vm_ready, n + 1)
                    copied(pe, f"q{s}", b)
                if step < GR:
                    dst = begin("arg", n, step)
                    done(nc.tensor.matmul(dst[:, :], AW[n % 2][:, step * P:(step + 1) * P], QS[b][s],
                                          start=True, stop=True), "arg", n, step)
                if step:
                    g = step - 1
                    copied(pe, "arg", n, g)
                    dst = begin("O", n, g // 4) if g % 4 == 0 else bank[USES[("O", n, g // 4)][0]]
                    at = 32 * (g % 4)
                    ins = nc.tensor.matmul(dst[at:at + 32, :], VM[n % 2][:, g * 32:(g + 1) * 32], E[(n * GR + g) % 3],
                                           start=True, stop=True)
                    if g % 4 == 3:
                        done(ins, "O", n, g // 4)
                    else:
                        ins.then_inc(e_used, 1)

            def turn_sums(n, t):
                if t == 0:
                    copied(pe, "O", n, 3)
                dst = begin("ot", n, t)
                for j in range(4):
                    ins = nc.tensor.transpose(dst[:, j * P:(j + 1) * P], OC[:, j, t * P:(t + 1) * P], IDENT)
                done(ins, "ot", n, t)

            def tail(p):
                kind, b = PHASES[p]
                if kind == "F0":
                    if p == 0:
                        pe.wait_ge(ghost_w, M0 + M0 // 2)
                    for m in range(M0):
                        copied(pe, "up", p, m)
                    rows = [LAST0 if m == M0 - 1 else P for m in range(M0)]
                    terms = [(lambda t, m=m: HT[b][0:rows[m], m, t * P:(t + 1) * P], WDOWN[0:rows[m], m * D:(m + 1) * D]) for m in range(M0)]
                if kind == "F1":
                    pe.wait_ge(fold_scaled, 4)
                    for m in range(M1):
                        copied(pe, "up", p, m)
                    terms = [(lambda t, m=m: HT[b][:, m, t * P:(t + 1) * P], WDN[:, m, :]) for m in range(M1)]
                if kind == "A":
                    copied(pe, "oT", b, 0)
                    copied(pe, "oT", b, 1)
                    terms = [(lambda t, k=k: OT[:, k * S + t * P:k * S + (t + 1) * P], WO[:, k, :]) for k in range(2)]
                if kind == "M":
                    pe.wait_ge(small_ready, 2)
                    for t in range(T):
                        copied(pe, "yT", b, t)
                    terms = [(lambda t, c=c: YT[b][:, t, c * P:(c + 1) * P], WOUT[:, c, :]) for c in range(4)]
                for j in range(2):
                    dst = begin("tail", p, j)
                    for i in range(2):
                        for m, (lhs, rhs) in enumerate(terms):
                            ins = nc.tensor.matmul(dst[:, i * D:(i + 1) * D], lhs(2 * j + i), rhs,
                                                   start=(m == 0), stop=(m == len(terms) - 1))
                    done(ins, "tail", p, j)

            pe.wait_ge(cst_in, 16)
            for kind, *at in SCHEDULE:
                if kind == "front":
                    front(*at)
                elif kind == "foldug":
                    i = at[0]
                    c, n = i // 4, i % 4
                    if i == 0:
                        pe.wait_ge(wug_in, 32)
                    dst = begin("foldug", i)
                    for k in range(KD):
                        ins = nc.tensor.matmul(dst[:, :], NHAD if (c and k) else HAD, WUGRAW[k][:, n * 512:(n + 1) * 512],
                                               start=(k == 0), stop=(k == KD - 1))
                    done(ins, "foldug", i)
                elif kind == "folddn":
                    i = at[0]
                    if i == 0:
                        pe.wait_ge(butter, 2)
                    dst = begin("folddn", i)
                    done(nc.tensor.matmul(dst[:, :], HAD, BUTTER[i // 2][:, (i % 2) * 2 * D:(i % 2 + 1) * 2 * D],
                                          start=True, stop=True), "folddn", i)
                elif kind == "unit":
                    ffn_unit(*at)
                elif kind == "tail":
                    tail(*at)
                elif kind == "proj":
                    for k in range(KD):
                        copied(pe, "xT", B + at[0], k)
                    projections(*at)
                elif kind == "qt":
                    queries(*at)
                elif kind == "gather":
                    gather(*at)
                elif kind == "att":
                    attend(*at)
                elif kind == "ot":
                    turn_sums(*at)
                elif kind == "oT":
                    b = at[0]
                    pe.wait_ge(oh_ready, T * SETS * (b + 1))
                    for k in range(2):
                        dst = begin("oT", b, k)
                        for t in range(T):
                            ins = nc.tensor.transpose(dst[:, t * P:(t + 1) * P], OH[:, t * D + k * P:t * D + (k + 1) * P], IDENT)
                        done(ins, "oT", b, k)
                elif kind == "conv":
                    b, c = at
                    if c == 0:
                        for k in range(KD):
                            copied(pe, "xT", 4 * B + b, k)
                        pe.wait_ge(win_in, 16)
                    dst = begin("conv", b, c)
                    for k in range(KD):
                        ins = nc.tensor.matmul(dst[:, :], WIN[:, k, DI + c * P:DI + (c + 1) * P], XT[b][:, k, :],
                                               start=(k == 0), stop=(k == KD - 1))
                    done(ins, "conv", b, c)
                elif kind == "dt":
                    b = at[0]
                    dst = begin("dt", b)
                    for t in range(T):
                        for k in range(KD):
                            ins = nc.tensor.matmul(dst[:, t * NH:(t + 1) * NH], XT[b][:, k, t * P:(t + 1) * P],
                                                   WIN[:, k, DI + CONVC:DI + CONVC + NH], start=(k == 0), stop=(k == KD - 1))
                    done(ins, "dt", b)
                elif kind == "z":
                    b, t = at
                    dst = begin("z", b, t)
                    for k in range(KD):
                        ins = nc.tensor.matmul(dst[:, :], XT[b][:, k, t * P:(t + 1) * P], WIN[:, k, 0:DI],
                                               start=(k == 0), stop=(k == KD - 1))
                    done(ins, "z", b, t)
                elif kind == "G":
                    b = at[0]
                    pe.wait_ge(xc_ready, CT * (b + 1))
                    dst = begin("G", b)
                    for t in range(T):
                        ts = slice(t * P, (t + 1) * P)
                        ins = nc.tensor.matmul(dst[:, ts], XC[:, 4, ts], XC[:, 5, ts], start=True, stop=True)
                    done(ins, "G", b)
                    dst = begin("BT", b)
                    for t in range(T):
                        ts = slice(t * P, (t + 1) * P)
                        ins = nc.tensor.transpose(dst[:, ts], XC[:, 4, ts], IDENT)
                    done(ins, "BT", b)
                elif kind == "xt":
                    b, t = at
                    dst = begin("xt", b, t)
                    for c in range(4):
                        ins = nc.tensor.transpose(dst[:, c * P:(c + 1) * P], XC[:, c, t * P:(t + 1) * P], IDENT)
                    done(ins, "xt", b, t)
                elif kind == "cum":
                    b, i = at
                    if i == 0:
                        pe.wait_ge(da_ready, b + 1)
                        pe.wait_ge(tables_in, 16)
                    dst = begin("cum", b, i)
                    for j in range(2):
                        col = C_CUM + (2 * i + j) * P
                        ins = nc.tensor.matmul(dst[:, j * T * NH:(j + 1) * T * NH], CST[:, col:col + P], DTA, start=True, stop=True)
                    done(ins, "cum", b, i)
                elif kind == "lev":
                    b, t, lv = at
                    if (t, lv) == (0, 0):
                        copied(pe, "G", b)
                        copied(pe, "BT", b)
                    n = wcount(b, t, lv)
                    dst = begin("lev", b, t, lv)
                    pe.wait_ge(w_ready, n + 1)
                    col = (t * LEVELS + lv) * P
                    done(nc.tensor.matmul(dst[:, :], GM[:, col:col + P], W[n % 3], start=True, stop=True), "lev", b, t, lv)
                elif kind == "off":
                    b, t = at
                    dst = begin("off", b, t)
                    copied(pe, "st", b, t - 1)
                    done(nc.tensor.matmul(dst[:, :], XC[:, 5, t * P:(t + 1) * P], ST[(t - 1) % 2],
                                          start=True, stop=True), "off", b, t)
                elif kind == "st":
                    b, t = at
                    n = wcount(b, t, LEVELS)
                    dst = begin("st", b, t)
                    pe.wait_ge(w_ready, n + 1)
                    done(nc.tensor.matmul(dst[:, :], BT[:, t * P:(t + 1) * P], W[n % 3], start=True, stop=True), "st", b, t)
                elif kind == "yT":
                    b, t = at
                    pe.wait_ge(yg_ready, T * b + t + 1)
                    dst = begin("yT", b, t)
                    for c in range(4):
                        ins = nc.tensor.transpose(dst[:, c * P:(c + 1) * P], XTOK[:, t, c * P:(c + 1) * P], IDENT)
                    done(ins, "yT", b, t)


def kernel(**inputs):
    import concourse.bacc as _bacc
    from concourse.bass_utils import run_bass_kernel_spmd as _run

    inp = {k: np.asarray(v) for k, v in inputs.items()}

    def rows(w, k):
        return np.ascontiguousarray(w.reshape(k, P, -1).transpose(1, 0, 2))

    def spread(v):
        return np.ascontiguousarray(np.broadcast_to(v, (P, v.shape[0])))

    def dup(w, s):
        return np.concatenate([w[64 * s:64 * s + 64]] * 2, axis=0).T

    wq, wk, wv = inp["L0_attn_Wq"], inp["L0_attn_Wk"], inp["L0_attn_Wv"]
    wvh = wv.reshape(HEADS, 2, D)
    w_qkv = np.concatenate([dup(wq, 0), dup(wq, 1), dup(wk, 0), dup(wk, 1)]
                           + [dup(wvh[:, c], s) for s in range(SETS) for c in range(2)], axis=1)
    order = np.array([64 * s + 32 * q + 2 * g + e for s in range(SETS) for g in range(GR) for q in range(2) for e in range(2)])
    w_o = inp["L0_attn_Wo"].T.reshape(HEADS, 2, D)[order].reshape(D, D)
    gu_idx = np.concatenate([rows(inp[name][m * P:(m + 1) * P].T, KD).reshape(P, -1)
                             for m in range(M0) for name in ("L0_ffn_gate_idx", "L0_ffn_up_idx")], axis=1)
    w_up, w_gate = inp["L1_ffn_W_up"], inp["L1_ffn_W_gate"]
    arrays = {
        "x": inp["L0_attn_x"].reshape(B * S, D),
        "cst": constants(),
        "gu_idx": gu_idx,
        "down_idx": inp["L0_ffn_down_idx"].T,
        "lut": spread(inp["L0_ffn_lut"]),
        "w_ug": np.concatenate([w_up, w_gate], axis=0).T.reshape(KD, P, 2 * INTER1),
        "w_dn": inp["L1_ffn_W_down"].T.reshape(2, 4, P, D).transpose(0, 2, 1, 3),
        "su_ug": inp["L1_ffn_SU_ug"].reshape(KD, P).T,
        "su_dp": inp["L1_ffn_SU_dp"].reshape(M1, P).T,
        "ws_ug": inp["L1_ffn_Wscale_ug"].reshape(2 * M1, P).T,
        "ws_dp": spread(inp["L1_ffn_Wscale_dp"]),
        "w_qkv": rows(w_qkv, KD),
        "w_qt": rows(wq[order].T, KD),
        "w_o": rows(w_o, 2),
        "w_in": rows(inp["L1_attn_in_proj_w"].T, KD),
        "conv_w": rows(inp["L1_attn_conv_w"], CT),
        "conv_b": inp["L1_attn_conv_b"].reshape(CT, P).T,
        "dt_bias": spread(inp["L1_attn_dt_bias"]),
        "a_log": spread(inp["L1_attn_A_log"]),
        "skip_d": spread(inp["L1_attn_D"]),
        "norm_w": inp["L1_attn_norm_weight"].reshape(4, P).T,
        "w_out": rows(inp["L1_attn_out_proj_w"].T, 4),
    }
    nc = _bacc.Bacc("TRN2", target_bir_lowering=False, num_devices=1)
    maps, args = {}, []
    for name, a in arrays.items():
        a = np.ascontiguousarray(a)
        maps[f"in_{name}"] = a
        args.append(nc.dram_tensor(f"in_{name}", a.shape, mybir.dt.from_np(a.dtype), kind="ExternalInput").ap())
    out = nc.dram_tensor("out_0_dram", (B * S, D), mybir.dt.float32, kind="ExternalOutput").ap()
    program(nc, *args, out)
    r = _run(nc, [maps], core_ids=[0])
    return r.results[0]["out_0_dram"].reshape(B, S, D)
```

```python
import concourse.bass as bass
from concourse import mybir
from contextlib import ExitStack
import numpy as np

B = 2
S = 512
D = 256
P = 128
T = S // P
KD = D // P
INTER0 = 688
M0 = -(-INTER0 // P)
LAST0 = INTER0 - (M0 - 1) * P
LUT = 16
INTER1 = 1024
M1 = INTER1 // P
HEADS = 128
TOPK = 32
ROUNDS = TOPK // 8
SETS = 2
GR = 16
G32 = 32
DI = 512
NH = 64
HP = DI // NH
CONVC = 768
CT = CONVC // P
DCONV = 4
LEVELS = 7
NCUM = LEVELS + 3
EPS = 1e-5
LOWEST = -3.0e38
DOWN_DVE = 2
LAG = 2

PHASES = [(kind, b) for kind in ("F0", "A", "F0", "F1", "M", "F1") for b in range(B)]
TILES_OF = {"F0": M0, "F1": M1}


def weave(first, second, every):
    out, rest = [], list(second)
    for i, step in enumerate(first):
        out.append(step)
        if rest and (i + 1) % every == 0:
            out += rest.pop(0)
    return out + sum(rest, [])


def schedule():
    def norm(p):
        return [("stats", p), ("xhat", p), ("front", p)]

    def units(p, m0=0, m1=None):
        return [("unit", p, m) for m in range(m0, TILES_OF[PHASES[p][0]] if m1 is None else m1)]

    def end(p):
        return [("tail", p), ("resid", p)]

    pool_lookups = [("lookpool", i, q) for i in range(DOWN_DVE, M0 // 2) for q in range(4)]
    out = norm(0) + [("look", 0)] + norm(1) + pool_lookups + [("butterfly",), ("look", 1), ("foldug", 0)]
    for m in range(M0):
        out += units(0, m, m + 1)
        out += [("look", m + 2)] if m + 2 < M0 else [("lookdown", m + 2 - M0)]
        out += [("foldug", m + 1)] + (units(1, m, m + 1) if m < 4 else [])
    out += [("foldug", 7)]
    out += end(0) + [("stats", 2), ("xhat", 2), ("folddn", 0)] + units(1, 4, 5) + [("front", 2)]
    out += [("folddn", i) for i in range(1, 4)] + [("clear",), ("proj", 0)]
    out += [("keys", 0, 0), ("turn", 0), ("keys", 0, 1), ("split", 0), ("keys", 0, 2), ("keys", 0, 3)] + units(1, 5)
    out += [("qt", 0), ("hots", 0)] + end(1) + [("stats", 3), ("xhat", 3), ("gather", 0), ("front", 3)]
    out += [("keys", 1, 0), ("keys", 1, 1), ("values", 0), ("turn", 1), ("keys", 1, 2), ("keys", 1, 3), ("proj", 1), ("split", 1), ("hots", 1), ("qt", 1)]
    for n in range(2 * SETS):
        for g in range(GR + LAG):
            out += [("att", n, g)]
            if n and 1 <= g <= T:
                out += [("ot", n - 1, g - 1)]
            if g == 6 and n + 1 < 2 * SETS:
                out += [("gather", n + 1)]
            if n + 2 < 2 * SETS and g in (2, 4, 6, 8):
                out += [("keys", n + 2, (g - 2) // 2)]
            if g == 9 and n + 1 < 2 * SETS:
                out += [("values", n + 1)]
            if g == 10 and n + 2 < 2 * SETS:
                out += [("turn", n + 2)]
            if g == 12 and n + 2 < 2 * SETS:
                out += [("split", n + 2), ("hots", n + 2)]
            if n == 2 and g == 10:
                out += [("oT", 0), ("tail", 2), ("resid", 2), ("stats", 4), ("xhat", 4)]
            if n == 3 and g < M0:
                out += [("gsplit", g)]
            if n == 2 and g == 15:
                out += [("front", 4)]
            if n == 3 and g >= 5 and g % 2 == 1 and (g - 5) // 2 < M0:
                out += units(4, (g - 5) // 2, (g - 5) // 2 + 1)
    out += [("ot", 3, t) for t in range(T)] + [("oT", 1), ("tail", 3), ("resid", 3), ("tail", 4), ("stats", 5), ("xhat", 5)]
    out += [("resid", 4), ("front", 5), ("stats", 6), ("xhat", 6)] + units(5, 0, 2) + [("front", 6)] + units(5, 2)
    out += [("wsplit", m) for m in range(5)] + [("tail", 5), ("resid", 5), ("stats", 7)] + units(6, 0, 1) + [("xhat", 7)]
    for m in range(1, M1):
        out += ([("wsplit", m + 4)] if m + 4 < M1 else []) + units(6, m, m + 1)
        out += [("front", 7)] if m == 4 else []
    out += units(7, 0, 1) + end(6) + [("stats", 8), ("xhat", 8)] + units(7, 1, 3) + [("front", 8)]

    def scan_front(b, fill):
        return [("dt", b)] + [("conv", b, c) for c in range(3)] + fill[0] + [("ratio", b)] \
            + [("conv", b, c) for c in range(3, CT)] + [("z", b, t) for t in range(T)] + fill[1] \
            + [("G", b)] + [("xt", b, t) for t in range(T)] + [("cum", b, i) for i in range(NCUM // 2)] + fill[2]

    def scan_levels(b):
        steps = []
        for t in range(T):
            steps += [("y0", b, t)] + [("lev", b, t, lv) for lv in range(LEVELS)]
            steps += [("off", b, t)] if t else []
            steps += [("st", b, t)] if t < T - 1 else []
            steps += [("yg", b, t)]
        return steps

    def scan_end(b):
        return [("rr", b)] + [("yT", b, t) for t in range(T)]

    def single(steps):
        return [[step] for step in steps]

    out += scan_front(0, [[], units(7, 3, 4), units(7, 4, 5)])
    out += weave(scan_levels(0), single(units(7, 5)) + [end(7), [("stats", 9), ("xhat", 9)], [("front", 9)]], 8)
    out += scan_end(0)
    out += scan_front(1, [end(8) + [("stats", 10), ("xhat", 10)], [("front", 10)] + units(10, 0, 1), units(10, 1, 2)])
    out += weave(scan_levels(1), single(units(10, 2)), 6)
    out += scan_end(1) + end(9) + [("stats", 11), ("xhat", 11)] + end(10) + [("front", 11)] + units(11) + end(11)
    return out


def in_parts(p):
    return p >= 4 and PHASES[p][0] in TILES_OF


SCHEDULE = schedule()
NORMS = [s[1] for s in SCHEDULE if s[0] == "stats"]
UNITS = [s[1:] for s in SCHEDULE if s[0] == "unit"]


def constants():
    ident = np.eye(P, dtype=np.float32)
    had = np.array([[1.0]], np.float32)
    while had.shape[0] < P:
        had = np.block([[had, had], [had, -had]]).astype(np.float32)
    t = np.arange(P)
    cum = np.zeros((NCUM, P, P), np.float32)
    pair = np.zeros((LEVELS, P, P), np.float32)
    r, c = np.meshgrid(t, t, indexing="ij")
    for lv in range(LEVELS):
        half = 1 << lv
        mid = (c // (2 * half)) * 2 * half + half
        right = c >= mid
        cum[lv] = np.where(right, (r >= mid) & (r <= c), (r > c) & (r < mid))
        pair[lv] = (r // (2 * half) == c // (2 * half)) & right & (r < mid)
    cum[LEVELS] = r <= c
    cum[LEVELS + 1] = r > c
    cum[LEVELS + 2] = 1.0
    rows = t
    q, g = (rows // 32) % 2, rows % 32
    slot = np.zeros((P, GR, 4), np.float32)
    slot[rows, g // 2, 2 * q + g % 2] = 1.0
    iota32 = np.broadcast_to(np.arange(32, dtype=np.float32), (P, 32))
    return np.concatenate([
        ident, had, -had,
        cum.transpose(1, 0, 2).reshape(P, -1),
        pair.transpose(1, 0, 2).reshape(P, -1),
        slot.reshape(P, -1), iota32,
    ], axis=1).astype(np.float32)


C_ID, C_H, C_NH = 0, P, 2 * P
C_CUM = 3 * P
C_PAIR = C_CUM + NCUM * P
C_SLOT = C_PAIR + LEVELS * P
C_IOTA = C_SLOT + GR * 4
C_ALL = C_IOTA + 32


def psum_uses():
    uses, count, ring = {}, [0] * 8, [0]

    def use(bank, *name):
        count[bank] += 1
        uses[name] = (bank, count[bank])

    def scan(*name):
        use(4 + ring[0] % 4, *name)
        ring[0] += 1

    for kind, *at in SCHEDULE:
        if kind == "front":
            for k in range(KD):
                use(6 + k, "xT", at[0], k)
        elif kind == "foldug":
            use(at[0] % 4, kind, *at)
        elif kind == "folddn":
            use(4 + at[0] % 2, kind, *at)
        elif kind == "unit":
            slot = 6 if at[0] == 4 else 2 * (UNITS.index(tuple(at)) % 2)
            use(slot, "gate", *at)
            use(slot + 1, "up", *at)
        elif kind == "tail":
            for j in range(2):
                use(4 + j, "tail", at[0], j)
        elif kind == "proj":
            for i, n in enumerate(PROJ):
                use(i % 4, n, at[0])
        elif kind == "qt":
            use(4, "qt", at[0])
        elif kind == "gather":
            for i in range(2):
                use(6 + i, "gat", at[0], i)
        elif kind == "att":
            n, g = at
            if g < GR:
                use(4 + g % 2, "arg", n, g)
            if g % 4 == 2 and g < GR:
                use(g // 4, "O", n, g // 4)
        elif kind == "ot":
            use(6 + at[1] % 2, kind, *at)
        elif kind == "oT":
            for k in range(2):
                use(6 + k, "oT", at[0], k)
        elif kind == "G":
            scan("G", at[0])
            scan("BT", at[0])
        elif kind in ("conv", "dt", "z", "xt", "cum", "lev", "off", "st", "yT"):
            scan(kind, *at)
    return uses


COPY_AT = {6: 0, 10: 1, 14: 2, 17: 3}
PROJ = ("k0", "v00", "v01", "k1", "v10", "v11", "q0", "q1")


def program(nc, x, cst, gu_idx, down_idx, lut, w_ug, w_dn, su_ug, su_dp, ws_ug, ws_dp,
            w_qkv, w_qt, w_o, w_in, conv_w, conv_b, dt_bias, a_log, skip_d, norm_w, w_out, out):
    f32, f32r, bf16 = mybir.dt.float32, mybir.dt.float32r, mybir.dt.bfloat16
    i32, u32 = mybir.dt.int32, mybir.dt.uint32
    ALU, ACT = mybir.AluOpType, mybir.ActivationFunctionType
    AX = mybir.AxisListType
    USES = psum_uses()
    ctx = ExitStack()
    with ctx:
        def sb(name, shape, dt=f32):
            return ctx.enter_context(nc.sbuf_tensor(name, shape, dt))

        def overlaid(*tensors):
            handles = []
            for name, shape, dt in tensors[:-1]:
                with nc.sbuf_tensor(name, shape, dt) as handle:
                    handles.append(handle)
            return handles + [sb(*tensors[-1])]

        def sem(name):
            return ctx.enter_context(nc.semaphore(name))

        bank = [ctx.enter_context(nc.psum_tensor(f"bank{i}", [P, 512], f32)) for i in range(8)]

        CST = sb("CST", [P, C_ALL])
        IDENT = CST[:, C_ID:C_ID + P]
        HAD, NHAD = CST[:, C_H:C_H + P], CST[:, C_NH:C_NH + P]
        SLOT = CST[:, C_SLOT:C_SLOT + GR * 4]
        IOTA = CST[:, C_IOTA:C_IOTA + 32]
        X = sb("X", [P, B * T, D])
        XH = sb("XH", [P, T, D])
        XT, XTH = zip(*[overlaid((f"XT{b}", [P, KD, S], f32), (f"XTH{b}", [P, KD, S], f32r)) for b in range(B)])
        STAT = sb("STAT", [P, T, 6])
        MV = sb("MV", [P, T, 2])
        VEPS = sb("VEPS", [P, T])
        RSTD = sb("RSTD", [P, T])
        NHALF = sb("NHALF", [P, T])
        WUGL, WGUH, WGHOST = overlaid(("WUGL", [P, M1, KD, 2, P], f32r), ("WGUH", [P, 2 * KD * INTER0], f32r),
                                      ("WGHOST", [P, 2 * KD * INTER0 + M0 * D], f32))
        WGU = WGHOST[:, 0:2 * KD * INTER0]
        WDOWN = WGHOST[:, 2 * KD * INTER0:]
        WUG, WUGH = overlaid(("WUG", [P, KD, 2 * INTER1], f32), ("WUGH", [P, KD, 2 * INTER1], f32r))
        WDN = sb("WDN", [P, M1, D])
        HT = [sb(f"HT{b}", [P, M1, S]) for b in range(B)]
        SG = [sb(f"SG{i}", [P, S]) for i in range(2)]
        WSUG = sb("WSUG", [P, 2 * M1])
        WSUG16 = sb("WSUG16", [P, 2 * M1])
        SUUG = sb("SUUG", [P, KD])
        SUDP = sb("SUDP", [P, M1])
        WO = sb("WO", [P, 2, D])
        WOUT = sb("WOUT", [P, 4, D])
        NW = sb("NW", [P, 4])
        CW = sb("CW", [P, CT, DCONV])
        CB = sb("CB", [P, CT])
        DTB = sb("DTB", [P, NH])
        NEGA = sb("NEGA", [P, NH])
        SKIP = sb("SKIP", [P, NH])

        USIZE = 23800
        XTLB, LOWS, U = overlaid(("XTL", [P, B, KD, S], f32r), ("LOWS", [P, B * KD * S + 2 * KD * INTER0], f32r), ("U", [P, USIZE], f32))
        XTL = [XTLB[:, b] for b in range(B)]
        WGUL = LOWS[:, B * KD * S:]
        cur = [0]

        def part(n):
            cur[0] += n
            assert cur[0] <= USIZE, cur[0]
            return U[:, cur[0] - n:cur[0]]

        def ht(b, at, n):
            return HT[b][:, :, :].rearrange("p a b -> p (a b)")[:, at:at + n]

        NIDX = 2 * KD * INTER0 + M0 * D
        CHUNK = 2 * KD * P
        LUTB = sb("LUTB", [P, LUT])
        LUTX = sb("LUTX", [P, LUT // 2])
        cur[0] = 0
        IDX = part(NIDX)
        MASK = [part(CHUNK) for _ in range(4)]
        SEL = [part(CHUNK) for _ in range(7)]
        TERM = [part(CHUNK) for _ in range(2)]
        WUGRAW = [part(2 * INTER1) for _ in range(KD)]
        WDNRAW = [part(4 * D) for _ in range(2)]
        BUTTER = [part(4 * D) for _ in range(2)]
        WSDP = part(D)

        cur[0] = 0
        WQKV = part(KD * 8 * P).rearrange("p (k n) -> p k n", k=KD)
        WQT = part(KD * P).rearrange("p (k n) -> p k n", k=KD)
        V = [[[part(S) for _ in range(2)] for _ in range(SETS)] for _ in range(B)]
        cur_v = B * KD * S + 2 * KD * INTER0
        HIGHG = [U[:, cur_v + i * CHUNK:cur_v + (i + 1) * CHUNK] for i in range(2)]
        assert cur_v + 2 * CHUNK <= cur[0]
        QS = [[part(S) for _ in range(SETS)] for _ in range(B)]
        KEYS = [[part(S) for _ in range(SETS)] for _ in range(B)]
        QM = [part(S) for _ in range(B)]
        TOP = part(TOPK)
        IDX8 = part(TOPK)
        IA, IB = part(TOPK), part(TOPK)
        IAF, IBF = part(TOPK), part(TOPK)
        EXPO = [part(TOPK) for _ in range(2)]
        IAT, IBT = part(TOPK), part(TOPK)
        VB = ht(0, 0, 2 * S)
        OHC = ht(0, 2 * S, G32 * 32 // 2).bitcast(bf16)
        OHA = ht(0, 4 * S, G32 * 16)
        OHB = part(G32 * 4 * 32 // 2).bitcast(bf16)
        V3 = [part(S).bitcast(bf16) for _ in range(3)]
        PR = ht(0, 5 * S, G32 * 2 * 16)
        VS = part(G32 * 2)
        AW = [part(GR * P) for _ in range(2)]
        VM = [part(GR * 32) for _ in range(2)]
        E = [ht(1, (5 + i) * S, S) for i in range(3)]
        OC = ht(1, 0, 4 * S).rearrange("p (j s) -> p j s", j=4)
        OH = part(T * D)
        RD, R1 = part(P // SETS), part(P // SETS)
        OT = part(2 * S)
        OTMP = part(D // SETS)

        cur[0] = B * KD * S
        WIN = part(KD * 1344).rearrange("p (k n) -> p k n", k=KD)
        XC = part(CT * S).rearrange("p (c s) -> p c s", c=CT)
        ZS = part(T * DI).rearrange("p (t n) -> p t n", t=T)
        XTOK = part(T * DI).rearrange("p (t n) -> p t n", t=T)
        XDT = [ht(b, 4 * S, T * DI).rearrange("p (t n) -> p t n", t=T) for b in range(B)]
        YT = HT
        BT = part(T * P)
        GM = part(T * LEVELS * P)
        F = part(NCUM * T * NH)
        DTV, DTA = part(T * NH), part(T * NH)
        GCC = part(T)
        W = [part(DI) for _ in range(3)]
        Y = part(DI)
        RF = [part(DI) for _ in range(2)]
        DTU, DTR = RF[0][:, 0:T * NH], RF[0][:, T * NH:2 * T * NH]
        DTP, DTQ = RF[1][:, 0:T * NH], RF[1][:, T * NH:2 * T * NH]
        ST = [part(DI) for _ in range(2)]
        SS = part(T)
        SSM = part(T)
        RR = part(T)
        SQ = part(DI)
        GPR = SQ
        COEF = part(NH)
        HIGH = [XC[:, 2 * i:2 * i + 1, :].rearrange("p o (k h n) -> p (o k) h n", k=KD, h=2) for i in range(2)]

        bank_full = [sem(f"bank_full{i}") for i in range(8)]
        bank_free = [sem(f"bank_free{i}") for i in range(8)]
        x_in = [sem(f"x_in{b}") for b in range(B)]
        cst_in = sem("cst_in")
        tables_in = sem("tables_in")
        lut_in = sem("lut_in")
        gu_first_in = sem("gu_first_in")
        gu_rest_in = sem("gu_rest_in")
        down_idx_in = sem("down_idx_in")
        idx_zero = sem("idx_zero")
        wug_in = sem("wug_in")
        wdn_in = sem("wdn_in")
        small_in = sem("small_in")
        attn_w_in = sem("attn_w_in")
        win_in = sem("win_in")
        out_done = sem("out_done")
        dve_step = sem("dve_step")
        pool_step = sem("pool_step")
        act_step = sem("act_step")
        ghost_w = sem("ghost_w")
        ghost_w_pool = sem("ghost_w_pool")
        butter = sem("butter")
        fold_scaled = sem("fold_scaled")
        var_ready = sem("var_ready")
        rstd_ready = sem("rstd_ready")
        xhat_ready = sem("xhat_ready")
        xT_high = sem("xT_high")
        w_high = sem("w_high")
        w_low = sem("w_low")
        w_split = sem("w_split")
        g_high = sem("g_high")
        g_low = sem("g_low")
        g_split = sem("g_split")
        small_ready = sem("small_ready")
        nega_ready = sem("nega_ready")
        oh_zero = sem("oh_zero")
        onehot_ready = sem("onehot_ready")
        vb_ready = sem("vb_ready")
        v_rest_ready = sem("v_rest_ready")
        v3_ready = sem("v3_ready")
        top_ready = sem("top_ready")
        aw_ready = sem("aw_ready")
        vm_ready = sem("vm_ready")
        e_used = sem("e_used")
        oh_ready = sem("oh_ready")
        conv_ready = sem("conv_ready")
        xc_ready = sem("xc_ready")
        dtabs_ready = sem("dtabs_ready")
        dtexp_ready = sem("dtexp_ready")
        ratio_ready = sem("ratio_ready")
        da_ready = sem("da_ready")
        xdt_ready = sem("xdt_ready")
        w_ready = sem("w_ready")
        yg_ready = sem("yg_ready")
        ss_ready = sem("ss_ready")
        rr_ready = sem("rr_ready")
        block = ctx.enter_context(nc.Block())

        def full(eng, *name):
            i, n = USES[name]
            eng.wait_ge(bank_full[i], n)
            return bank[i]

        def emptied(*name):
            return bank_free[USES[name][0]]

        def copied(eng, *name):
            i, n = USES[name]
            eng.wait_ge(bank_free[i], n)

        SPLIT = [s[1] for s in SCHEDULE if s[0] == "front" and in_parts(s[1])]

        def ghost_tile(m):
            return slice(m * CHUNK, m * CHUNK + 2 * KD * (LAST0 if m == M0 - 1 else P))

        def weights_of(w, m):
            return w[:, :, :].rearrange("p k (h n) -> p k h n", h=2)[:, :, :, m * P:(m + 1) * P]

        def looked_up(eng):
            eng.wait_ge(ghost_w, M0 + DOWN_DVE)
            eng.wait_ge(ghost_w_pool, M0 // 2 - DOWN_DVE)

        @block.sync
        def _(sp):
            sp.dma_start(X[:, 0:T, :], x[0:S, :].rearrange("(t p) d -> p t d", p=P)).then_inc(x_in[0], 16)
            sp.dma_start(LUTB[:, :], lut).then_inc(lut_in, 16)
            gu = IDX[:, 0:2 * KD * INTER0].bitcast(i32)
            sp.dma_start(gu[:, 0:CHUNK], gu_idx[:, 0:CHUNK]).then_inc(gu_first_in, 16)
            sp.dma_start(X[:, T:2 * T, :], x[S:2 * S, :].rearrange("(t p) d -> p t d", p=P)).then_inc(x_in[1], 16)
            sp.dma_start(gu[:, CHUNK:2 * KD * INTER0], gu_idx[:, CHUNK:2 * KD * INTER0]).then_inc(gu_rest_in, 16)
            sp.wait_ge(idx_zero, 1)
            dn = IDX[:, 2 * KD * INTER0:NIDX].bitcast(i32)
            sp.dma_start(dn[:, 0:(M0 - 1) * D].rearrange("p (m n) -> p m n", n=D),
                         down_idx[0:(M0 - 1) * P, :].rearrange("(m p) n -> p m n", p=P)).then_inc(down_idx_in, 16)
            sp.dma_start(dn[0:LAST0, (M0 - 1) * D:M0 * D], down_idx[(M0 - 1) * P:INTER0, :]).then_inc(down_idx_in, 16)
            looked_up(sp)
            sp.dma_start(WQKV, w_qkv).then_inc(attn_w_in, 16)
            sp.dma_start(WQT, w_qt).then_inc(attn_w_in, 16)
            if ("up", 5, M0 - 1) in USES:
                copied(sp, "up", 5, M0 - 1)
                sp.dma_start(WIN, w_in).then_inc(win_in, 16)
            last = max(name[1] for name in USES if name[0] == "tail")
            for p in (last - 1, last):
                for j in range(2):
                    copied(sp, "tail", p, j)
            sp.dma_start(out.rearrange("(t p) d -> p t d", p=P), X[:, :, :]).then_inc(out_done, 16)
            sp.wait_ge(out_done, 16)

        WLIST = [(b, t, lv) for b in range(B) for t in range(T) for lv in range(LEVELS + (t < T - 1))]

        def wcount(b, t, lv):
            return WLIST.index((b, t, lv))

        def wname(n):
            b, t, lv = WLIST[n]
            return ("lev", b, t, lv) if lv < LEVELS else ("st", b, t)

        @block.gpsimd
        def _(pool):
            pool.memset(IDX[:, 2 * KD * INTER0 + (M0 - 1) * D:NIDX], 0.0).then_inc(idx_zero, 1)
            steps = [0]

            def link(ins):
                steps[0] += 1
                ins.then_inc(pool_step, 1)
                pool.wait_ge(pool_step, steps[0])

            link(pool.memset(NHALF[:, :], -0.5))

            def lookup(i, q):
                if (i, q) == (DOWN_DVE, 0):
                    pool.wait_ge(down_idx_in, 32)
                    pool.wait_ge(lut_in, 16)
                at = 2 * KD * INTER0 + i * CHUNK
                w = WDOWN[:, i * CHUNK:(i + 1) * CHUNK]
                for k in range(4 * q, 4 * q + 4):
                    term = TERM[k % 2] if k else w
                    link(nc.gpsimd.tensor_scalar(term, IDX[:, at:at + CHUNK].bitcast(i32), float(k), LUTB[:, k:k + 1],
                                                 ALU.is_equal, ALU.mult))
                    if k == LUT - 1:
                        nc.gpsimd.tensor_tensor(w, w, term, ALU.add).then_inc(ghost_w_pool, 1)
                    elif k:
                        link(nc.gpsimd.tensor_tensor(w, w, term, ALU.add))

            def butterfly():
                pool.wait_ge(wdn_in, 32)
                hd = [WDNRAW[i].rearrange("p (m n) -> p m n", n=D) for i in range(2)]
                tmp = [BUTTER[i].rearrange("p (m n) -> p m n", n=D) for i in range(2)]
                nc.gpsimd.tensor_tensor(tmp[0], hd[0], hd[1], ALU.add)
                link(nc.gpsimd.tensor_tensor(tmp[1], hd[0], hd[1], ALU.subtract))
                for h in range(2):
                    nc.gpsimd.tensor_tensor(hd[h][:, 0:2, :], tmp[h][:, 0:2, :], tmp[h][:, 2:4, :], ALU.add)
                    link(nc.gpsimd.tensor_tensor(hd[h][:, 2:4, :], tmp[h][:, 0:2, :], tmp[h][:, 2:4, :], ALU.subtract))
                for h in range(2):
                    link(nc.gpsimd.tensor_tensor(tmp[h][:, 0:4:2, :], hd[h][:, 0:4:2, :], hd[h][:, 1:4:2, :], ALU.add))
                    nc.gpsimd.tensor_tensor(tmp[h][:, 1:4:2, :], hd[h][:, 0:4:2, :], hd[h][:, 1:4:2, :],
                                            ALU.subtract).then_inc(butter, 1)
                pool.wait_ge(small_in, 16 * 11)
                nc.gpsimd.tensor_scalar(WSUG16[:, :], WSUG[:, :], 1.0 / 16.0, None, ALU.mult).then_inc(small_ready, 1)
                for k in range(4):
                    last = nc.gpsimd.tensor_scalar(WOUT[:, k, :], WOUT[:, k, :], NW[:, k:k + 1], None, ALU.mult)
                last.then_inc(small_ready, 1)

            def clear():
                looked_up(pool)
                copied(pool, "foldug", 7)
                nc.gpsimd.memset(OHB, 0.0).then_inc(oh_zero, 1)
                for i in range(2):
                    nc.gpsimd.memset(VM[i], 0.0).then_inc(oh_zero, 1)
                pool.wait_ge(oh_zero, 3)
                for i in range(2):
                    vm = VM[i].rearrange("p (g c) -> p g c", g=GR)
                    for sl in range(4):
                        nc.gpsimd.memset(vm[32 * sl:32 * sl + 32, :, 5 * sl:5 * sl + 1], 1.0).then_inc(oh_zero, 1)
                pool.wait_ge(oh_zero, 11)

            def split_values(n, k):
                pool.wait_ge(vb_ready, 2 * n + k)
                if k == 1:
                    nc.gpsimd.tensor_tensor(VB, VB, V3[0], ALU.subtract).then_inc(v_rest_ready, 1)
                else:
                    nc.gpsimd.tensor_tensor(V3[2], VB, V3[1], ALU.subtract).then_inc(v3_ready, 1)

            def time_steps(b):
                pool.wait_ge(ratio_ready, b + 1)
                link(nc.gpsimd.tensor_tensor(DTQ, DTR, DTR, ALU.mult))
                link(nc.gpsimd.tensor_scalar(DTP, DTQ, 1.0 / 17.0, 1.0 / 15.0, ALU.mult, ALU.add))
                for k in range(6, -1, -1):
                    link(nc.gpsimd.tensor_tensor(DTP, DTP, DTQ, ALU.mult))
                    link(nc.gpsimd.tensor_scalar(DTP, DTP, 1.0 / (2 * k + 1), None, ALU.add))
                link(nc.gpsimd.tensor_tensor(DTP, DTP, DTR, ALU.mult))
                link(nc.gpsimd.tensor_scalar(DTP, DTP, 2.0, None, ALU.mult))
                link(nc.gpsimd.tensor_scalar(DTV, DTV, 0.0, None, ALU.max))
                link(nc.gpsimd.tensor_tensor(DTV, DTV, DTP, ALU.add))
                v3 = DTV.rearrange("p (t h) -> p t h", t=T)
                link(nc.gpsimd.tensor_tensor(DTA.rearrange("p (t h) -> p t h", t=T), v3,
                                             NEGA[:, :].unsqueeze(1).to_broadcast([P, T, NH]), ALU.mult))
                nc.gpsimd.tensor_scalar(DTA, DTA, -1.0, None, ALU.mult).then_inc(da_ready, 1)

            def weighted(b, t, lv):
                if (t, lv) == (0, 0):
                    for i in range(NCUM // 2):
                        copied(pool, "cum", b, i)
                if lv == 0:
                    pool.wait_ge(xdt_ready, T * b + t + 1)
                tab = lv if lv < LEVELS else LEVELS + 1
                n = wcount(b, t, lv)
                if n >= 3:
                    full(pool, *wname(n - 3))
                xd = XDT[b][:, t, :].rearrange("p (h c) -> p h c", c=HP)
                ft = F.rearrange("p (i t h) -> p i t h", i=NCUM, t=T)[:, tab, t, :]
                nc.gpsimd.tensor_tensor(W[n % 3].rearrange("p (h c) -> p h c", c=HP), xd,
                                        ft.unsqueeze(2).to_broadcast([P, NH, HP]), ALU.mult).then_inc(w_ready, 1)

            for kind, *at in SCHEDULE:
                if kind == "stats":
                    pool.wait_ge(var_ready, NORMS.index(at[0]) + 1)
                    nc.gpsimd.tensor_tensor(RSTD[:, :], VEPS[:, :], NHALF[:, :], ALU.pow).then_inc(rstd_ready, 1)
                elif kind == "lookpool":
                    lookup(*at)
                elif kind == "butterfly":
                    butterfly()
                elif kind == "folddn":
                    i = at[0]
                    copied(pool, "folddn", i)
                    nc.gpsimd.tensor_tensor(WDN[:, 2 * i:2 * i + 2, :], WDN[:, 2 * i:2 * i + 2, :],
                                            WSDP.unsqueeze(1).to_broadcast([P, 2, D]),
                                            ALU.mult).then_inc(fold_scaled, 1)
                elif kind == "clear":
                    clear()
                elif kind == "turn":
                    split_values(at[0], 1)
                elif kind == "split":
                    split_values(at[0], 2)
                elif kind == "hots":
                    n = at[0]
                    pool.wait_ge(top_ready, n + 1)
                    if n == 0:
                        pool.wait_ge(tables_in, 16)
                    if n >= 2:
                        full(pool, "O", n - 2, 3)
                    aw = AW[n % 2].rearrange("p (g j) -> p g j", j=32)
                    nc.gpsimd.tensor_tensor(aw, EXPO[n % 2].unsqueeze(1).to_broadcast([P, GR * 4, 32]),
                                            SLOT.unsqueeze(2).to_broadcast([P, GR * 4, 32]), ALU.mult).then_inc(aw_ready, 1)
                elif kind == "ratio":
                    time_steps(*at)
                elif kind == "lev":
                    weighted(*at)
                elif kind == "st":
                    weighted(at[0], at[1], LEVELS)
                elif kind == "rr":
                    pool.wait_ge(ss_ready, T * (at[0] + 1))
                    link(nc.gpsimd.tensor_scalar(SSM, SS, 1.0 / DI, EPS, ALU.mult, ALU.add))
                    nc.gpsimd.tensor_tensor(RR, SSM, NHALF[:, :], ALU.pow).then_inc(rr_ready, 1)

        @block.scalar
        def _(act):
            steps = [0]

            def link(ins):
                steps[0] += 1
                ins.then_inc(act_step, 1)
                act.wait_ge(act_step, steps[0])

            act.dma_start(CST[:, 0:C_CUM], cst[:, 0:C_CUM]).then_inc(cst_in, 16)
            for k in range(KD):
                act.dma_start(WUGRAW[k], w_ug[k]).then_inc(wug_in, 16)
            for k in range(2):
                act.dma_start(WDNRAW[k].rearrange("p (m n) -> p m n", n=D), w_dn[k]).then_inc(wdn_in, 16)
            act.dma_start(SUUG[:, :], su_ug).then_inc(small_in, 16)
            act.dma_start(SUDP[:, :], su_dp).then_inc(small_in, 16)
            act.dma_start(WSUG[:, :], ws_ug).then_inc(small_in, 16)
            act.dma_start(WSDP, ws_dp).then_inc(small_in, 16)
            act.dma_start(WO[:, :, :], w_o).then_inc(small_in, 16)
            act.dma_start(WOUT[:, :, :], w_out).then_inc(small_in, 16)
            act.dma_start(NW[:, :], norm_w).then_inc(small_in, 16)
            act.dma_start(CW[:, :, :], conv_w).then_inc(small_in, 16)
            act.dma_start(CB[:, :], conv_b).then_inc(small_in, 16)
            act.dma_start(DTB[:, :], dt_bias).then_inc(small_in, 16)
            act.dma_start(SKIP[:, :], skip_d).then_inc(small_in, 16)
            act.dma_start(NEGA[:, :], a_log).then_inc(nega_ready, 16)
            act.dma_start(CST[:, C_CUM:C_ALL], cst[:, C_CUM:C_ALL]).then_inc(tables_in, 16)

            def take_xT(p):
                kind, b = PHASES[p]
                for k in range(KD):
                    src = full(act, "xT", p, k)
                    if in_parts(p):
                        nc.scalar.activation(XTH[b][:, k, :], src[:, :], ACT.Copy).then_inc(xT_high, 1)
                    else:
                        nc.scalar.activation(XT[b][:, k, :], src[:, :], ACT.Copy).then_inc(emptied("xT", p, k), 1)

            def high_ghost(m):
                if m == 0:
                    act.wait_ge(vb_ready, 2 * (B * SETS - 1) + 1)
                at = ghost_tile(m)
                high = HIGHG[m % 2][:, 0:at.stop - at.start].bitcast(f32r)
                nc.scalar.activation(high, WGU[:, at], ACT.Copy).then_inc(g_high, 1)
                act.wait_ge(g_low, m + 1)
                nc.scalar.activation(WGUH[:, at], high, ACT.Copy).then_inc(g_split, 1)

            def high_weights(m):
                if m == 0:
                    full(act, "up", 5, M0 - 1)
                nc.scalar.activation(HIGH[m % 2].bitcast(f32r), weights_of(WUG, m), ACT.Copy).then_inc(w_high, 1)
                act.wait_ge(w_low, m + 1)
                nc.scalar.activation(weights_of(WUGH, m), HIGH[m % 2].bitcast(f32r), ACT.Copy).then_inc(w_split, 1)

            def take_projections(b):
                lo, hi = slice(0, 64), slice(64, P)
                for name in PROJ:
                    src = full(act, name, b)
                    s = int(name[1])
                    if name[0] == "k":
                        dst, func, scale = KEYS[b][s], ACT.Copy, -1.0
                    elif name[0] == "v":
                        dst, func, scale = V[b][s][int(name[2])], ACT.Copy, 1.0
                    else:
                        dst, func, scale = QS[b][s], ACT.Relu, -1.0
                    top = dst[lo, :] if name[0] == "q" else dst[lo, ::-1]
                    link(nc.scalar.activation(top, src[lo, :], func))
                    nc.scalar.activation(dst[hi, :], src[hi, :], func, scale=scale).then_inc(emptied(name, b), 1)

            def silu_gate(p, m):
                kind = PHASES[p][0]
                u = UNITS.index((p, m))
                rows = LAST0 if (kind == "F0" and m == M0 - 1) else P
                if u >= 2:
                    copied(act, "up", *UNITS[u - 2])
                src = full(act, "gate", p, m)
                if kind == "F0":
                    ins = nc.scalar.activation(SG[u % 2][0:rows, :], src[0:rows, :], ACT.Silu)
                else:
                    if m == 0:
                        act.wait_ge(small_ready, 1)
                    ins = nc.scalar.activation(SG[u % 2][:, :], src[:, :], ACT.Silu,
                                               scale=WSUG16[:, M1 + m:M1 + m + 1])
                ins.then_inc(emptied("gate", p, m), 1)

            def attend(n, g):
                if g < GR:
                    k = n * GR + g
                    if k >= 3:
                        n3, g3 = divmod(k - 3, GR)
                        if g3 % 4 == 3:
                            full(act, "O", n3, g3 // 4)
                        else:
                            act.wait_ge(e_used, k - 2 - (k - 2) // 4)
                    src = full(act, "arg", n, g)
                    nc.scalar.activation(E[k % 3], src[:, :], ACT.Exp).then_inc(emptied("arg", n, g), 1)
                j = COPY_AT.get(g)
                if j is not None:
                    if n and j == 0:
                        full(act, "ot", n - 1, T - 1)
                    src = full(act, "O", n, j)
                    nc.scalar.activation(OC[:, j, :], src[:, :], ACT.Copy).then_inc(emptied("O", n, j), 1)

            def silu_conv(b, c):
                copied(act, "conv", b, c)
                nc.scalar.activation(XC[:, c, :], XC[:, c, :], ACT.Silu).then_inc(xc_ready, 1)

            for kind, *at in SCHEDULE:
                if kind == "front":
                    take_xT(*at)
                elif kind == "foldug":
                    c, n = at[0] // 4, at[0] % 4
                    if at[0] == 0:
                        act.wait_ge(small_in, 16 * 11)
                    src = full(act, "foldug", *at)
                    nc.scalar.activation(WUG[:, c, n * 512:(n + 1) * 512], src[:, :], ACT.Copy,
                                         scale=SUUG[:, c:c + 1]).then_inc(emptied("foldug", *at), 1)
                elif kind == "folddn":
                    i = at[0]
                    src = full(act, "folddn", i)
                    link(nc.scalar.activation(WDN[:, 2 * i, :], src[:, 0:D], ACT.Copy, scale=SUDP[:, 2 * i:2 * i + 1]))
                    nc.scalar.activation(WDN[:, 2 * i + 1, :], src[:, D:2 * D], ACT.Copy,
                                         scale=SUDP[:, 2 * i + 1:2 * i + 2]).then_inc(emptied("folddn", i), 1)
                elif kind == "clear":
                    act.wait_ge(nega_ready, 16)
                    nc.scalar.activation(NEGA[:, :], NEGA[:, :], ACT.Exp).then_inc(nega_ready, 1)
                elif kind == "gsplit":
                    high_ghost(*at)
                elif kind == "wsplit":
                    high_weights(*at)
                elif kind == "unit":
                    silu_gate(*at)
                elif kind == "proj":
                    take_projections(*at)
                elif kind == "att":
                    attend(*at)
                elif kind == "oT":
                    ot = OT.rearrange("p (k n) -> p k n", k=2)
                    for k in range(2):
                        src = full(act, "oT", at[0], k)
                        nc.scalar.activation(ot[:, k, :], src[:, :], ACT.Copy).then_inc(emptied("oT", at[0], k), 1)
                elif kind == "conv":
                    b, c = at
                    src = full(act, "conv", b, c)
                    nc.scalar.activation(XC[:, c, :], src[:, :], ACT.Identity, bias=CB[:, c:c + 1],
                                         scale=CW[:, c, DCONV - 1:DCONV]).then_inc(conv_ready, 1)
                    if c >= 1:
                        silu_conv(b, c - 1)
                elif kind == "dt":
                    b = at[0]
                    act.wait_ge(dtabs_ready, b + 1)
                    nc.scalar.activation(DTU, DTA, ACT.Exp, scale=-1.0).then_inc(dtexp_ready, 1)
                elif kind == "z":
                    if at[1] == 0:
                        silu_conv(at[0], CT - 1)
                    src = full(act, "z", *at)
                    nc.scalar.activation(ZS[:, at[1], :], src[:, :], ACT.Silu).then_inc(emptied("z", *at), 1)
                elif kind == "G":
                    src = full(act, "BT", *at)
                    nc.scalar.activation(BT, src[:, :], ACT.Copy).then_inc(emptied("BT", *at), 1)
                elif kind == "xt":
                    src = full(act, "xt", *at)
                    nc.scalar.activation(XTOK[:, at[1], :], src[:, :], ACT.Copy).then_inc(emptied("xt", *at), 1)
                elif kind == "cum":
                    b, i = at
                    src = full(act, "cum", b, i)
                    nc.scalar.activation(F[:, i * 2 * T * NH:(i + 1) * 2 * T * NH], src[:, :], ACT.Exp)\
                      .then_inc(emptied("cum", b, i), 1)
                elif kind == "yg":
                    b, t = at
                    act.wait_ge(yg_ready, T * b + t + 1)
                    if b or t:
                        act.wait_ge(ss_ready, T * b + t)
                    nc.scalar.activation(SQ, XTOK[:, t, :], ACT.Square, accum_out=SS[:, t:t + 1]).then_inc(ss_ready, 1)
                elif kind == "yT":
                    b, t = at
                    src = full(act, "yT", b, t)
                    nc.scalar.activation(YT[b][:, t, :], src[:, :], ACT.Copy).then_inc(emptied("yT", b, t), 1)

        @block.vector
        def _(dve):
            steps = [0]

            def link(ins):
                steps[0] += 1
                ins.then_inc(dve_step, 1)
                dve.wait_ge(dve_step, steps[0])

            def lookup(c, dst, at, n):
                if c:
                    dve.wait_ge(ghost_w, c)
                idx = IDX[:, at:at + n].bitcast(i32)
                mask = [m[:, 0:n].bitcast(i32) for m in MASK]
                sel = [dst] + [s[:, 0:n] for s in SEL]
                for i in range(4):
                    ins = nc.vector.tensor_scalar(mask[i], idx, 31 - i, 31, ALU.logical_shift_left, ALU.arith_shift_right)
                link(ins)
                for k in range(8):
                    ins = nc.vector.tensor_scalar(sel[k].bitcast(i32), mask[0], LUTX[:, k:k + 1].bitcast(i32),
                                                  LUTB[:, 2 * k:2 * k + 1].bitcast(i32), ALU.bitwise_and, ALU.bitwise_xor)
                link(ins)
                for k in (0, 2, 4, 6):
                    ins = nc.vector.copy_predicated(sel[k], mask[1], sel[k + 1])
                link(ins)
                for k in (0, 4):
                    ins = nc.vector.copy_predicated(sel[k], mask[2], sel[k + 2])
                link(ins)
                nc.vector.copy_predicated(sel[0], mask[3], sel[4]).then_inc(ghost_w, 1)

            dve.wait_ge(lut_in, 16)
            link(nc.vector.tensor_tensor(LUTX[:, :].bitcast(i32), LUTB[:, 0:LUT:2].bitcast(i32),
                                         LUTB[:, 1:LUT:2].bitcast(i32), ALU.bitwise_xor))

            def stats(p):
                b = PHASES[p][1]
                if p < B:
                    dve.wait_ge(x_in[b], 16)
                for t in range(T):
                    ins = nc.vector.bn_stats(STAT[:, t, :], X[:, b * T + t, :])
                link(ins)
                for t in range(T):
                    ins = nc.vector.bn_aggr(MV[:, t, :], STAT[:, t, :])
                link(ins)
                nc.vector.tensor_scalar(VEPS[:, :], MV[:, :, 1], EPS, None, ALU.add).then_inc(var_ready, 1)

            def xhat(p):
                b = PHASES[p][1]
                i = NORMS.index(p)
                dve.wait_ge(rstd_ready, i + 1)
                if i:
                    full(dve, "xT", NORMS[i - 1], 0)
                    full(dve, "xT", NORMS[i - 1], 1)
                for t in range(T):
                    nc.vector.tensor_scalar(XH[:, t, :], X[:, b * T + t, :], MV[:, t, 0:1], RSTD[:, t:t + 1],
                                            ALU.subtract, ALU.mult).then_inc(xhat_ready, 1)

            def low_xT(p):
                b = PHASES[p][1]
                for k in range(KD):
                    src = full(dve, "xT", p, k)
                    dve.wait_ge(xT_high, KD * SPLIT.index(p) + k + 1)
                    nc.vector.tensor_tensor(XTL[b][:, k, :], src[:, :], XTH[b][:, k, :].bitcast(f32),
                                            ALU.subtract).then_inc(emptied("xT", p, k), 1)

            def low_ghost(m):
                at = ghost_tile(m)
                dve.wait_ge(g_high, m + 1)
                nc.vector.tensor_tensor(WGUL[:, at], WGU[:, at], HIGHG[m % 2][:, 0:at.stop - at.start],
                                        ALU.subtract).then_inc(g_low, 1)

            def low_weights(m):
                if (m + 1) * 2 * KD * P <= 2 * KD * INTER0:
                    full(dve, "up", 5, M0 - 1)
                else:
                    full(dve, "tail", 5, 1)
                dve.wait_ge(w_high, m + 1)
                nc.vector.tensor_tensor(WUGL[:, m], weights_of(WUG, m), HIGH[m % 2], ALU.subtract).then_inc(w_low, 1)

            def residual(p):
                kind, b = PHASES[p]
                if kind == "M":
                    dve.wait_ge(rr_ready, b + 1)
                for j in range(2):
                    src = full(dve, "tail", p, j)
                    if kind == "M":
                        for i in range(2):
                            t = 2 * j + i
                            ins = nc.vector.scalar_tensor_tensor(X[:, b * T + t, :], src[:, i * D:(i + 1) * D], RR[:, t:t + 1],
                                                                 X[:, b * T + t, :], ALU.mult, ALU.add)
                            if i == 0:
                                link(ins)
                    else:
                        scale = {"F0": 0.5, "A": 1.0, "F1": 0.5 / 32.0}[kind]
                        xs = X[:, b * T + 2 * j:b * T + 2 * j + 2, :].rearrange("p t d -> p (t d)")
                        ins = nc.vector.scalar_tensor_tensor(xs, src[:, :], scale, xs, ALU.mult, ALU.add)
                    if j == 0:
                        ins.then_inc(emptied("tail", p, 0), 1)
                        dve.wait_ge(emptied("tail", p, 0), USES[("tail", p, 0)][1])
                    else:
                        ins.then_inc(emptied("tail", p, 1), 1)
                        dve.wait_ge(emptied("tail", p, 1), USES[("tail", p, 1)][1])

            iota_b = IOTA.unsqueeze(1).to_broadcast([P, G32, 32])
            iota_a = CST[:, C_IOTA:C_IOTA + 16].unsqueeze(1).to_broadcast([P, G32, 16])

            def pick_keys(n, r):
                b, s = n // SETS, n % SETS
                if r == 0:
                    copied(dve, f"k{s}", b)
                keys = KEYS[b][s]
                eight = slice(8 * r, 8 * r + 8)
                link(nc.vector.max(TOP[:, eight], keys))
                nc.vector.max_index(IDX8.bitcast(u32)[:, eight], TOP[:, eight], keys)
                if r < ROUNDS - 1:
                    link(nc.vector.match_replace(keys, TOP[:, eight], keys, LOWEST))
                else:
                    nc.vector.tensor_scalar(EXPO[n % 2], TOP, TOP[:, 0:1], None, ALU.subtract).then_inc(top_ready, 1)
                    dve.wait_ge(top_ready, n + 1)

            def one_hots(n):
                b, s = n // SETS, n % SETS
                idx = IDX8.bitcast(u32)
                if n == 0:
                    dve.wait_ge(tables_in, 16)
                nc.vector.tensor_scalar(IA.bitcast(u32), idx, 5, None, ALU.logical_shift_right)
                link(nc.vector.tensor_scalar(IB.bitcast(u32), idx, 31, None, ALU.bitwise_and))
                nc.vector.tensor_copy(IAF, IA.bitcast(u32))
                link(nc.vector.tensor_copy(IBF, IB.bitcast(u32)))
                nc.vector.transpose(IAT, IAF)
                link(nc.vector.transpose(IBT, IBF))
                ohc = OHC.rearrange("p (g b) -> p g b", b=32)
                oha = OHA.rearrange("p (g a) -> p g a", a=16)
                nc.vector.tensor_tensor(ohc, IBT.unsqueeze(2).to_broadcast([P, G32, 32]), iota_b, ALU.is_equal)
                link(nc.vector.tensor_tensor(oha, IAT.unsqueeze(2).to_broadcast([P, G32, 16]), iota_a, ALU.is_equal))
                if n == 0:
                    dve.wait_ge(oh_zero, 11)
                ohb = OHB.rearrange("p (g k j) -> p g k j", g=G32, k=4)
                if n:
                    full(dve, "gat", n - 1, 1)
                for k in range(4):
                    rows = slice(32 * k, 32 * k + 32)
                    ins = nc.vector.transpose(ohb[rows, :, k, :], ohc[rows, :, :])
                ins.then_inc(onehot_ready, 1)

            def turn_values(n):
                b, s = n // SETS, n % SETS
                if n:
                    dve.wait_ge(v3_ready, n)
                vb = VB.rearrange("p (c a g) -> p c a g", c=2, a=16)
                for c in range(2):
                    copied(dve, f"v{s}{c}", b)
                    ins = nc.vector.transpose(vb[:, c, :, :], V[b][s][c].rearrange("p (a b) -> p a b", b=32))
                link(ins)
                if n:
                    full(dve, "gat", n - 1, 1)
                nc.vector.tensor_copy(V3[0], VB).then_inc(vb_ready, 1)

            def second_part(n):
                dve.wait_ge(v_rest_ready, n + 1)
                nc.vector.tensor_copy(V3[1], VB).then_inc(vb_ready, 1)

            def pick_values(n):
                oha = OHA.rearrange("p (g a) -> p g a", a=16)
                pr = PR.rearrange("p (g c a) -> p g c a", c=2, a=16)
                vs = VS.rearrange("p (g c) -> p g c", c=2)
                for i in range(2):
                    src = full(dve, "gat", n, i)[:, :].rearrange("p (g c a) -> p g c a", c=2, a=16)
                    for c in range(2):
                        ins = nc.vector.tensor_tensor(pr[:, 16 * i:16 * i + 16, c, :], src[:, :, c, :],
                                                      oha[:, 16 * i:16 * i + 16, :], ALU.mult)
                    ins.then_inc(emptied("gat", n, i), 1)
                copied(dve, "gat", n, 0)
                copied(dve, "gat", n, 1)
                link(nc.vector.tensor_reduce(VS, PR.rearrange("p (g a) -> p g a", a=16), AX.X, ALU.add))
                if n >= 2:
                    full(dve, "O", n - 2, 3)
                vm = VM[n % 2].rearrange("p (g c) -> p g c", g=GR)
                for q in range(2):
                    for e in range(2):
                        for sign in range(2):
                            to = 32 * (2 * q + e)
                            fr = 32 * (2 * sign + q)
                            col = 5 * (2 * q + e) + 1 + 2 * sign
                            ins = nc.vector.tensor_copy(vm[to:to + 32, :, col:col + 2],
                                                        vs[fr:fr + 32, e:G32:2, :])
                ins.then_inc(vm_ready, 1)
                dve.wait_ge(vm_ready, n + 1)

            def combine(n, t):
                b, s = n // SETS, n % SETS
                src = full(dve, "ot", n, t)
                sums = src[:, :].rearrange("p (g k) -> p g k", k=32)[:, :, 0:20].rearrange("p g (m c) -> p g m c", c=5)
                heads_s = slice(s * P // SETS, (s + 1) * P // SETS)
                qm = QM[b][:, t * P:(t + 1) * P][:, heads_s]
                oh = OH.rearrange("p (t m c) -> p t m c", t=T, c=2)[:, t, heads_s, :].rearrange("p (g m) c -> p g m c", m=4)
                if b == 1:
                    full(dve, "oT", 0, 1)
                four = lambda ap: ap.rearrange("p (g m) -> p g m", m=4)
                link(nc.vector.reciprocal(four(RD), sums[:, :, :, 0]))
                link(nc.vector.tensor_tensor(R1, RD, qm, ALU.mult))
                nc.vector.tensor_tensor(RD, RD, R1, ALU.subtract)
                tm = OTMP.rearrange("p (g m c) -> p g m c", m=4, c=2)
                to = [P, GR, 4, 2]
                link(nc.vector.tensor_tensor(oh, sums[:, :, :, 1:3], four(R1).unsqueeze(3).to_broadcast(to), ALU.mult))
                nc.vector.tensor_tensor(tm, sums[:, :, :, 3:5], four(RD).unsqueeze(3).to_broadcast(to), ALU.mult)\
                    .then_inc(emptied("ot", n, t), 1)
                copied(dve, "ot", n, t)
                nc.vector.tensor_tensor(oh, oh, tm, ALU.add).then_inc(oh_ready, 1)
                dve.wait_ge(oh_ready, T * n + t + 1)

            def ffn_unit(p, m):
                kind, b = PHASES[p]
                u = UNITS.index((p, m))
                rows = LAST0 if (kind == "F0" and m == M0 - 1) else P
                copied(dve, "gate", p, m)
                src = full(dve, "up", p, m)
                if kind == "F0":
                    ins = nc.vector.tensor_tensor(HT[b][0:rows, m, :], src[0:rows, :], SG[u % 2][0:rows, :], ALU.mult)
                else:
                    if m == 0:
                        dve.wait_ge(small_ready, 1)
                    ins = nc.vector.scalar_tensor_tensor(HT[b][:, m, :], src[:, :], WSUG16[:, m:m + 1],
                                                         SG[u % 2][:, :], ALU.mult, ALU.mult)
                ins.then_inc(emptied("up", p, m), 1)

            def heads(ap):
                return ap.rearrange("p (h c) -> p h c", c=HP)

            f4 = F.rearrange("p (i t h) -> p i t h", i=NCUM, t=T)

            def spread(tab, t):
                return f4[:, tab, t, :].unsqueeze(2).to_broadcast([P, NH, HP])

            def time_steps(b):
                src = full(dve, "dt", b)
                v3 = DTV.rearrange("p (t h) -> p t h", t=T)
                nc.vector.tensor_tensor(v3, src[:, 0:T * NH].rearrange("p (t h) -> p t h", t=T),
                                        DTB[:, :].unsqueeze(1).to_broadcast([P, T, NH]), ALU.add)\
                    .then_inc(emptied("dt", b), 1)
                copied(dve, "dt", b)
                nc.vector.tensor_scalar(DTA.bitcast(i32), DTV.bitcast(i32), 0x7FFFFFFF, None, ALU.bitwise_and).then_inc(dtabs_ready, 1)

            def mask_products(b):
                src = full(dve, "G", b)
                gm = GM.rearrange("p (t l c) -> p t l c", t=T, l=LEVELS)
                pair = CST[:, C_PAIR:C_PAIR + LEVELS * P].rearrange("p (l c) -> p l c", l=LEVELS)
                link(nc.vector.tensor_tensor(GPR.rearrange("p (t c) -> p t c", t=T), src[:, :].rearrange("p (t c) -> p t c", t=T),
                                             IDENT.unsqueeze(1).to_broadcast([P, T, P]), ALU.mult))
                link(nc.vector.tensor_reduce(GCC, GPR.rearrange("p (t c) -> p t c", t=T), AX.X, ALU.add))
                for t in range(T):
                    ins = nc.vector.tensor_tensor(gm[:, t], src[:, t * P:(t + 1) * P].unsqueeze(1).to_broadcast([P, LEVELS, P]),
                                                  pair, ALU.mult)
                ins.then_inc(emptied("G", b), 1)

            v3 = DTV.rearrange("p (t h) -> p t h", t=T)

            def own_term(b, t):
                if t == 0:
                    for i in range(NCUM // 2):
                        copied(dve, "cum", b, i)
                link(nc.vector.scalar_tensor_tensor(COEF, v3[:, t, :], GCC[:, t:t + 1], SKIP[:, :], ALU.mult, ALU.add))
                link(nc.vector.tensor_tensor(heads(Y), heads(XTOK[:, t, :]), COEF.unsqueeze(2).to_broadcast([P, NH, HP]), ALU.mult))

            rf_of = []

            def span(name, t, i, tab):
                src = full(dve, *name)
                nc.vector.tensor_tensor(heads(RF[i % 2]), heads(src[:, :]), spread(tab, t), ALU.mult).then_inc(emptied(*name), 1)
                if i:
                    add_span()
                rf_of.append((name, RF[i % 2]))

            def add_span():
                name, rf = rf_of.pop()
                copied(dve, *name)
                link(nc.vector.tensor_tensor(Y, Y, rf, ALU.add))

            def state(b, t):
                src = full(dve, "st", b, t)
                if t == 0:
                    nc.vector.tensor_copy(ST[0], src[:, :]).then_inc(emptied("st", b, t), 1)
                else:
                    link(nc.vector.tensor_tensor(heads(ST[t % 2]), heads(ST[(t - 1) % 2]), spread(LEVELS + 2, t), ALU.mult))
                    nc.vector.tensor_tensor(ST[t % 2], ST[t % 2], src[:, :], ALU.add).then_inc(emptied("st", b, t), 1)
                copied(dve, "st", b, t)

            for kind, *at in SCHEDULE:
                if kind == "stats":
                    stats(*at)
                elif kind == "xhat":
                    xhat(*at)
                elif kind == "front" and in_parts(at[0]):
                    low_xT(*at)
                elif kind == "gsplit":
                    low_ghost(*at)
                elif kind == "wsplit":
                    low_weights(*at)
                elif kind == "look":
                    m = at[0]
                    if m < 2:
                        dve.wait_ge((gu_first_in, gu_rest_in)[m], 16)
                    n = 2 * KD * (LAST0 if m == M0 - 1 else P)
                    lookup(m, WGU[:, m * CHUNK:m * CHUNK + n], m * CHUNK, n)
                elif kind == "lookdown":
                    i = at[0]
                    if i == 0:
                        dve.wait_ge(down_idx_in, 32)
                    lookup(M0 + i, WDOWN[:, i * CHUNK:(i + 1) * CHUNK], 2 * KD * INTER0 + i * CHUNK, CHUNK)
                elif kind == "unit":
                    ffn_unit(*at)
                elif kind == "resid":
                    residual(*at)
                elif kind == "qt":
                    src = full(dve, "qt", *at)
                    nc.vector.tensor_scalar(QM[at[0]], src[:, :], 0.0, None, ALU.is_gt).then_inc(emptied("qt", *at), 1)
                elif kind == "keys":
                    pick_keys(*at)
                elif kind == "turn":
                    turn_values(*at)
                elif kind == "split":
                    second_part(*at)
                elif kind == "hots":
                    one_hots(*at)
                elif kind == "values":
                    pick_values(*at)
                elif kind == "ot":
                    combine(*at)
                elif kind == "conv":
                    b, c = at
                    dve.wait_ge(conv_ready, CT * b + c + 1)
                    src = full(dve, "conv", b, c)
                    for back in range(1, DCONV):
                        ins = nc.vector.scalar_tensor_tensor(
                            XC[:, c, back:S], src[:, 0:S - back], CW[:, c, DCONV - 1 - back:DCONV - back],
                            XC[:, c, back:S], ALU.mult, ALU.add)
                        if back < DCONV - 1:
                            link(ins)
                    ins.then_inc(emptied("conv", b, c), 1)
                elif kind == "dt":
                    time_steps(*at)
                elif kind == "ratio":
                    dve.wait_ge(dtexp_ready, at[0] + 1)
                    link(nc.vector.tensor_scalar(DTQ, DTU, 2.0, None, ALU.add))
                    link(nc.vector.reciprocal(DTP, DTQ))
                    nc.vector.tensor_tensor(DTR, DTU, DTP, ALU.mult).then_inc(ratio_ready, 1)
                elif kind == "G":
                    mask_products(*at)
                elif kind == "xt":
                    b, t = at
                    if t == 0:
                        dve.wait_ge(da_ready, b + 1)
                    copied(dve, "xt", b, t)
                    nc.vector.tensor_tensor(heads(XDT[b][:, t, :]), heads(XTOK[:, t, :]),
                                            v3[:, t, :].unsqueeze(2).to_broadcast([P, NH, HP]), ALU.mult).then_inc(xdt_ready, 1)
                elif kind == "y0":
                    own_term(*at)
                elif kind == "lev":
                    b, t, lv = at
                    span(("lev", b, t, lv), t, lv, lv)
                elif kind == "off":
                    b, t = at
                    span(("off", b, t), t, LEVELS, LEVELS)
                elif kind == "st":
                    state(*at)
                elif kind == "yg":
                    b, t = at
                    add_span()
                    if t == 0:
                        copied(dve, "z", b, T - 1)
                    nc.vector.tensor_tensor(XTOK[:, t, :], Y, ZS[:, t, :], ALU.mult).then_inc(yg_ready, 1)
                    dve.wait_ge(yg_ready, T * b + t + 1)

        @block.tensor
        def _(pe):
            def begin(*name):
                i, n = USES[name]
                if n > 1:
                    pe.wait_ge(bank_free[i], n - 1)
                return bank[i]

            def done(ins, *name):
                ins.then_inc(bank_full[USES[name][0]], 1)

            def front(p):
                pe.wait_ge(xhat_ready, T * (NORMS.index(p) + 1))
                for k in range(KD):
                    dst = begin("xT", p, k)
                    for t in range(T):
                        ins = nc.tensor.transpose(dst[:, t * P:(t + 1) * P], XH[:, t, k * P:(k + 1) * P], IDENT)
                    done(ins, "xT", p, k)

            def projections(b):
                if b == 0:
                    pe.wait_ge(attn_w_in, 32)
                at = {"q0": 0, "q1": 1, "k0": 2, "k1": 3, "v00": 4, "v01": 5, "v10": 6, "v11": 7}
                for n in PROJ:
                    dst = begin(n, b)
                    for k in range(KD):
                        ins = nc.tensor.matmul(dst[:, :], WQKV[:, k, at[n] * P:(at[n] + 1) * P], XT[b][:, k, :],
                                               start=(k == 0), stop=(k == KD - 1))
                    done(ins, n, b)

            def queries(b):
                dst = begin("qt", b)
                for t in range(T):
                    for k in range(KD):
                        ins = nc.tensor.matmul(dst[:, t * P:(t + 1) * P], XT[b][:, k, t * P:(t + 1) * P], WQT[:, k, :],
                                               start=(k == 0), stop=(k == KD - 1))
                done(ins, "qt", b)

            def ffn_unit(p, m):
                kind, b = PHASES[p]
                rows = LAST0 if (kind == "F0" and m == M0 - 1) else P
                if m == 0:
                    for k in range(KD):
                        copied(pe, "xT", p, k)
                if p < B:
                    pe.wait_ge(ghost_w, m + 1)
                if p == 4:
                    pe.wait_ge(g_split, m + 1)
                if p == 6:
                    pe.wait_ge(w_split, m + 1)
                for i, name in enumerate(("gate", "up")):
                    dst = begin(name, p, m)
                    terms = []
                    for k in range(KD):
                        x_high, x_low = XTH[b][:, k, :], XTL[b][:, k, :]
                        if kind == "F0":
                            at = m * CHUNK + (i * KD + k) * rows
                            at = slice(at, at + rows)
                            if p < B:
                                terms += [(WGU[:, at], XT[b][:, k, :])]
                                continue
                            high, low = WGUH[:, at], WGUL[:, at]
                        else:
                            half = 1 - i
                            at = m * P + half * INTER1
                            high, low = WUGH[:, k, at:at + P], WUGL[:, m, k, half, :]
                        terms += [(high, x_high), (high, x_low), (low, x_high)]
                    for t, (w, xt) in enumerate(terms):
                        ins = nc.tensor.matmul(dst[0:rows, :], w, xt, start=(t == 0), stop=(t == len(terms) - 1))
                    done(ins, name, p, m)

            def gather(n):
                pe.wait_ge(onehot_ready, n + 1)
                pe.wait_ge(v3_ready, n + 1)
                v3 = [v.rearrange("p (c a g) -> p c a g", c=2, a=16) for v in V3]
                for i in range(2):
                    dst = begin("gat", n, i)
                    for g in range(16):
                        gg = 16 * i + g
                        for k in range(3):
                            ins = nc.tensor.matmul(dst[:, g * 32:(g + 1) * 32], OHB[:, gg * P:(gg + 1) * P],
                                                   v3[k][:, :, :, gg], start=(k == 0), stop=(k == 2))
                    done(ins, "gat", n, i)

            def attend(n, step):
                b, s = n // SETS, n % SETS
                if step == 0:
                    pe.wait_ge(aw_ready, n + 1)
                    pe.wait_ge(vm_ready, n + 1)
                    copied(pe, f"q{s}", b)
                if step < GR:
                    dst = begin("arg", n, step)
                    done(nc.tensor.matmul(dst[:, :], AW[n % 2][:, step * P:(step + 1) * P], QS[b][s],
                                          start=True, stop=True), "arg", n, step)
                if step >= LAG:
                    g = step - LAG
                    copied(pe, "arg", n, g)
                    dst = begin("O", n, g // 4) if g % 4 == 0 else bank[USES[("O", n, g // 4)][0]]
                    at = 32 * (g % 4)
                    ins = nc.tensor.matmul(dst[at:at + 32, :], VM[n % 2][:, g * 32:(g + 1) * 32], E[(n * GR + g) % 3],
                                           start=True, stop=True)
                    if g % 4 == 3:
                        done(ins, "O", n, g // 4)
                    else:
                        ins.then_inc(e_used, 1)

            def turn_sums(n, t):
                if t == 0:
                    copied(pe, "O", n, 3)
                dst = begin("ot", n, t)
                for j in range(4):
                    ins = nc.tensor.transpose(dst[:, j * P:(j + 1) * P], OC[:, j, t * P:(t + 1) * P], IDENT)
                done(ins, "ot", n, t)

            def tail(p):
                kind, b = PHASES[p]
                if kind == "F0":
                    if p == 0:
                        looked_up(pe)
                    for m in range(M0):
                        copied(pe, "up", p, m)
                    rows = [LAST0 if m == M0 - 1 else P for m in range(M0)]
                    terms = [(lambda t, m=m: HT[b][0:rows[m], m, t * P:(t + 1) * P], WDOWN[0:rows[m], m * D:(m + 1) * D]) for m in range(M0)]
                if kind == "F1":
                    pe.wait_ge(fold_scaled, 4)
                    for m in range(M1):
                        copied(pe, "up", p, m)
                    terms = [(lambda t, m=m: HT[b][:, m, t * P:(t + 1) * P], WDN[:, m, :]) for m in range(M1)]
                if kind == "A":
                    copied(pe, "oT", b, 0)
                    copied(pe, "oT", b, 1)
                    terms = [(lambda t, k=k: OT[:, k * S + t * P:k * S + (t + 1) * P], WO[:, k, :]) for k in range(2)]
                if kind == "M":
                    pe.wait_ge(small_ready, 2)
                    for t in range(T):
                        copied(pe, "yT", b, t)
                    terms = [(lambda t, c=c: YT[b][:, t, c * P:(c + 1) * P], WOUT[:, c, :]) for c in range(4)]
                for j in range(2):
                    dst = begin("tail", p, j)
                    for i in range(2):
                        for m, (lhs, rhs) in enumerate(terms):
                            ins = nc.tensor.matmul(dst[:, i * D:(i + 1) * D], lhs(2 * j + i), rhs,
                                                   start=(m == 0), stop=(m == len(terms) - 1))
                    done(ins, "tail", p, j)

            pe.wait_ge(cst_in, 16)
            for kind, *at in SCHEDULE:
                if kind == "front":
                    front(*at)
                elif kind == "foldug":
                    i = at[0]
                    c, n = i // 4, i % 4
                    if i == 0:
                        pe.wait_ge(wug_in, 32)
                    dst = begin("foldug", i)
                    for k in range(KD):
                        ins = nc.tensor.matmul(dst[:, :], NHAD if (c and k) else HAD, WUGRAW[k][:, n * 512:(n + 1) * 512],
                                               start=(k == 0), stop=(k == KD - 1))
                    done(ins, "foldug", i)
                elif kind == "folddn":
                    i = at[0]
                    if i == 0:
                        pe.wait_ge(butter, 2)
                    dst = begin("folddn", i)
                    done(nc.tensor.matmul(dst[:, :], HAD, BUTTER[i // 2][:, (i % 2) * 2 * D:(i % 2 + 1) * 2 * D],
                                          start=True, stop=True), "folddn", i)
                elif kind == "unit":
                    ffn_unit(*at)
                elif kind == "tail":
                    tail(*at)
                elif kind == "proj":
                    for k in range(KD):
                        copied(pe, "xT", B + at[0], k)
                    projections(*at)
                elif kind == "qt":
                    queries(*at)
                elif kind == "gather":
                    gather(*at)
                elif kind == "att":
                    attend(*at)
                elif kind == "ot":
                    turn_sums(*at)
                elif kind == "oT":
                    b = at[0]
                    pe.wait_ge(oh_ready, T * SETS * (b + 1))
                    for k in range(2):
                        dst = begin("oT", b, k)
                        for t in range(T):
                            ins = nc.tensor.transpose(dst[:, t * P:(t + 1) * P], OH[:, t * D + k * P:t * D + (k + 1) * P], IDENT)
                        done(ins, "oT", b, k)
                elif kind == "conv":
                    b, c = at
                    dst = begin("conv", b, c)
                    for k in range(KD):
                        ins = nc.tensor.matmul(dst[:, :], WIN[:, k, DI + c * P:DI + (c + 1) * P], XT[b][:, k, :],
                                               start=(k == 0), stop=(k == KD - 1))
                    done(ins, "conv", b, c)
                elif kind == "dt":
                    b = at[0]
                    for k in range(KD):
                        copied(pe, "xT", 4 * B + b, k)
                    pe.wait_ge(win_in, 16)
                    dst = begin("dt", b)
                    for t in range(T):
                        for k in range(KD):
                            ins = nc.tensor.matmul(dst[:, t * NH:(t + 1) * NH], XT[b][:, k, t * P:(t + 1) * P],
                                                   WIN[:, k, DI + CONVC:DI + CONVC + NH], start=(k == 0), stop=(k == KD - 1))
                    done(ins, "dt", b)
                elif kind == "z":
                    b, t = at
                    dst = begin("z", b, t)
                    for k in range(KD):
                        ins = nc.tensor.matmul(dst[:, :], XT[b][:, k, t * P:(t + 1) * P], WIN[:, k, 0:DI],
                                               start=(k == 0), stop=(k == KD - 1))
                    done(ins, "z", b, t)
                elif kind == "G":
                    b = at[0]
                    pe.wait_ge(xc_ready, CT * (b + 1))
                    dst = begin("G", b)
                    for t in range(T):
                        ts = slice(t * P, (t + 1) * P)
                        ins = nc.tensor.matmul(dst[:, ts], XC[:, 4, ts], XC[:, 5, ts], start=True, stop=True)
                    done(ins, "G", b)
                    dst = begin("BT", b)
                    for t in range(T):
                        ts = slice(t * P, (t + 1) * P)
                        ins = nc.tensor.transpose(dst[:, ts], XC[:, 4, ts], IDENT)
                    done(ins, "BT", b)
                elif kind == "xt":
                    b, t = at
                    dst = begin("xt", b, t)
                    for c in range(4):
                        ins = nc.tensor.transpose(dst[:, c * P:(c + 1) * P], XC[:, c, t * P:(t + 1) * P], IDENT)
                    done(ins, "xt", b, t)
                elif kind == "cum":
                    b, i = at
                    if i == 0:
                        pe.wait_ge(da_ready, b + 1)
                        pe.wait_ge(tables_in, 16)
                    dst = begin("cum", b, i)
                    for j in range(2):
                        col = C_CUM + (2 * i + j) * P
                        ins = nc.tensor.matmul(dst[:, j * T * NH:(j + 1) * T * NH], CST[:, col:col + P], DTA, start=True, stop=True)
                    done(ins, "cum", b, i)
                elif kind == "lev":
                    b, t, lv = at
                    if (t, lv) == (0, 0):
                        copied(pe, "G", b)
                        copied(pe, "BT", b)
                    n = wcount(b, t, lv)
                    dst = begin("lev", b, t, lv)
                    pe.wait_ge(w_ready, n + 1)
                    col = (t * LEVELS + lv) * P
                    done(nc.tensor.matmul(dst[:, :], GM[:, col:col + P], W[n % 3], start=True, stop=True), "lev", b, t, lv)
                elif kind == "off":
                    b, t = at
                    dst = begin("off", b, t)
                    copied(pe, "st", b, t - 1)
                    done(nc.tensor.matmul(dst[:, :], XC[:, 5, t * P:(t + 1) * P], ST[(t - 1) % 2],
                                          start=True, stop=True), "off", b, t)
                elif kind == "st":
                    b, t = at
                    n = wcount(b, t, LEVELS)
                    dst = begin("st", b, t)
                    pe.wait_ge(w_ready, n + 1)
                    done(nc.tensor.matmul(dst[:, :], BT[:, t * P:(t + 1) * P], W[n % 3], start=True, stop=True), "st", b, t)
                elif kind == "yT":
                    b, t = at
                    pe.wait_ge(yg_ready, T * b + t + 1)
                    dst = begin("yT", b, t)
                    for c in range(4):
                        ins = nc.tensor.transpose(dst[:, c * P:(c + 1) * P], XTOK[:, t, c * P:(c + 1) * P], IDENT)
                    done(ins, "yT", b, t)


def kernel(**inputs):
    import concourse.bacc as _bacc
    from concourse.bass_utils import run_bass_kernel_spmd as _run

    inp = {k: np.asarray(v) for k, v in inputs.items()}

    def rows(w, k):
        return np.ascontiguousarray(w.reshape(k, P, -1).transpose(1, 0, 2))

    def spread(v):
        return np.ascontiguousarray(np.broadcast_to(v, (P, v.shape[0])))

    def dup(w, s):
        return np.concatenate([w[64 * s:64 * s + 64]] * 2, axis=0).T

    wq, wk, wv = inp["L0_attn_Wq"], inp["L0_attn_Wk"], inp["L0_attn_Wv"]
    wvh = wv.reshape(HEADS, 2, D)
    w_qkv = np.concatenate([dup(wq, 0), dup(wq, 1), dup(wk, 0), dup(wk, 1)]
                           + [dup(wvh[:, c], s) for s in range(SETS) for c in range(2)], axis=1)
    order = np.array([64 * s + 32 * q + 2 * g + e for s in range(SETS) for g in range(GR) for q in range(2) for e in range(2)])
    w_o = inp["L0_attn_Wo"].T.reshape(HEADS, 2, D)[order].reshape(D, D)
    gu_idx = np.concatenate([rows(inp[name][m * P:(m + 1) * P].T, KD).reshape(P, -1)
                             for m in range(M0) for name in ("L0_ffn_gate_idx", "L0_ffn_up_idx")], axis=1)
    w_up, w_gate = inp["L1_ffn_W_up"], inp["L1_ffn_W_gate"]
    arrays = {
        "x": inp["L0_attn_x"].reshape(B * S, D),
        "cst": constants(),
        "gu_idx": gu_idx,
        "down_idx": inp["L0_ffn_down_idx"].T,
        "lut": spread(inp["L0_ffn_lut"]),
        "w_ug": np.concatenate([w_up, w_gate], axis=0).T.reshape(KD, P, 2 * INTER1),
        "w_dn": inp["L1_ffn_W_down"].T.reshape(2, 4, P, D).transpose(0, 2, 1, 3),
        "su_ug": inp["L1_ffn_SU_ug"].reshape(KD, P).T,
        "su_dp": inp["L1_ffn_SU_dp"].reshape(M1, P).T,
        "ws_ug": inp["L1_ffn_Wscale_ug"].reshape(2 * M1, P).T,
        "ws_dp": spread(inp["L1_ffn_Wscale_dp"]),
        "w_qkv": rows(w_qkv, KD),
        "w_qt": rows(wq[order].T, KD),
        "w_o": rows(w_o, 2),
        "w_in": rows(inp["L1_attn_in_proj_w"].T, KD),
        "conv_w": rows(inp["L1_attn_conv_w"], CT),
        "conv_b": inp["L1_attn_conv_b"].reshape(CT, P).T,
        "dt_bias": spread(inp["L1_attn_dt_bias"]),
        "a_log": spread(inp["L1_attn_A_log"]),
        "skip_d": spread(inp["L1_attn_D"]),
        "norm_w": inp["L1_attn_norm_weight"].reshape(4, P).T,
        "w_out": rows(inp["L1_attn_out_proj_w"].T, 4),
    }
    nc = _bacc.Bacc("TRN2", target_bir_lowering=False, num_devices=1)
    maps, args = {}, []
    for name, a in arrays.items():
        a = np.ascontiguousarray(a)
        maps[f"in_{name}"] = a
        args.append(nc.dram_tensor(f"in_{name}", a.shape, mybir.dt.from_np(a.dtype), kind="ExternalInput").ap())
    out = nc.dram_tensor("out_0_dram", (B * S, D), mybir.dt.float32, kind="ExternalOutput").ap()
    program(nc, *args, out)
    r = _run(nc, [maps], core_ids=[0])
    return r.results[0]["out_0_dram"].reshape(B, S, D)
```
